# Optimizing a Trainium2 kernel written in Bass

```python
import numpy as np
import jax
import jax.numpy as jnp

def _softmax(x, axis=-1):
    return jax.nn.softmax(x, axis=axis)

def _gelu(x):
    return jax.nn.gelu(x, approximate=True)

def _silu(x):
    return jax.nn.silu(x)

def _sigmoid(x):
    return jax.nn.sigmoid(x)

def _layernorm(x, axis=-1, eps=1e-05):
    m = jnp.mean(x, axis=axis, keepdims=True)
    v = jnp.var(x, axis=axis, keepdims=True)
    return (x - m) / jnp.sqrt(v + eps)

def _scatter_add(tgt, idx, src, axis=0):
    return tgt.at[idx].add(src)

def _segment_sum(src, seg, n):
    return jax.ops.segment_sum(src, seg, n)
kernel_name = 'mk_seq_preln_d1_jaxref_r4_95ad8f'

def setup_inputs(seed: int=0):
    np.random.seed(seed)
    _w = jnp.asarray

    def _L0_attn_setup():
        import jax, jax.numpy as jnp
        import numpy as np
        B, T, D = (4, 512, 512)
        H = 8
        DK = D // H
        DV = D // H
        KCONV = 4
        L2_EPS = 1e-06
        RMS_EPS = 1e-05

        def short_conv_silu(x, w):
            t = x.shape[1]
            xp = jnp.pad(x, ((0, 0), (KCONV - 1, 0), (0, 0)))
            y = sum((xp[:, i:i + t, :] * w[:, i] for i in range(KCONV)))
            return jax.nn.silu(y)

        def l2norm(x):
            return x * jax.lax.rsqrt(jnp.sum(x * x, axis=-1, keepdims=True) + L2_EPS)

        def delta_rule(q, k, v, beta):
            q = q * q.shape[-1] ** (-0.5)
            qt = jnp.swapaxes(q, 0, 1)
            kt = jnp.swapaxes(k, 0, 1)
            vt = jnp.swapaxes(v, 0, 1)
            bt = jnp.swapaxes(beta, 0, 1)

            def step(S, inp):
                q_, k_, v_, b_ = inp
                u = b_[..., None] * (v_ - jnp.einsum('bhk,bhkv->bhv', k_, S))
                S = S + jnp.einsum('bhk,bhv->bhkv', k_, u)
                o = jnp.einsum('bhk,bhkv->bhv', q_, S)
                return (S, o)
            S0 = jnp.zeros((q.shape[0], q.shape[2], q.shape[3], v.shape[3]), q.dtype)
            _, o = jax.lax.scan(step, S0, (qt, kt, vt, bt))
            return jnp.swapaxes(o, 0, 1)
        key = jax.random.key(seed)
        ks = jax.random.split(key, 10)
        w = 0.02
        return {'hidden_states': jax.random.normal(ks[0], (B, T, D), jnp.float32), 'Wq': jax.random.normal(ks[1], (D, D), jnp.float32) * w, 'Wk': jax.random.normal(ks[2], (D, D), jnp.float32) * w, 'Wv': jax.random.normal(ks[3], (D, D), jnp.float32) * w, 'Wb': jax.random.normal(ks[4], (D, H), jnp.float32) * w, 'conv_q': jax.random.normal(ks[5], (D, KCONV), jnp.float32) * 0.3, 'conv_k': jax.random.normal(ks[6], (D, KCONV), jnp.float32) * 0.3, 'conv_v': jax.random.normal(ks[7], (D, KCONV), jnp.float32) * 0.3, 'norm_w': jnp.ones((DV,), jnp.float32), 'Wo': jax.random.normal(ks[8], (D, D), jnp.float32) * w}
    _L0_attn_in = _L0_attn_setup()

    def _L0_ffn_setup():
        import jax, jax.numpy as jnp
        import numpy as np
        H = 512
        I = 352
        E = 16
        G = 4
        TOPK_GROUP = 2
        K = 4
        SI = 2 * I
        SCALE = 1.0
        NORM = True
        B, S = (4, 128)

        def _swiglu(h):
            g, u = jnp.split(h, 2, axis=-1)
            return jax.nn.silu(g) * u

        def _combine_weights(xt, gate_w):
            T = xt.shape[0]
            scores = jax.nn.softmax(xt @ gate_w.T, axis=-1)
            group_scores = scores.reshape(T, G, E // G).max(axis=-1)
            _, gidx = jax.lax.top_k(group_scores, TOPK_GROUP)
            gmask = jnp.zeros((T, G), bool).at[jnp.arange(T)[:, None], gidx].set(True)
            emask = jnp.repeat(gmask, E // G, axis=1)
            masked = jnp.where(emask, scores, 0.0)
            w, eidx = jax.lax.top_k(masked, K)
            if NORM:
                w = w / (w.sum(-1, keepdims=True) + 1e-20)
            w = w * SCALE
            return jnp.zeros((T, E), xt.dtype).at[jnp.arange(T)[:, None], eidx].add(w)
        key = jax.random.key(seed)
        ks = jax.random.split(key, 6)
        sc = lambda fan_in: 1.0 / np.sqrt(fan_in)
        return {'x': jax.random.normal(ks[0], (B, S, H), jnp.float32), 'gate_w': jax.random.normal(ks[1], (E, H), jnp.float32) * sc(H), 'expert_up_w': jax.random.normal(ks[2], (E, 2 * I, H), jnp.float32) * sc(H), 'expert_down_w': jax.random.normal(ks[3], (E, H, I), jnp.float32) * sc(I), 'shared_up_w': jax.random.normal(ks[4], (2 * SI, H), jnp.float32) * sc(H), 'shared_down_w': jax.random.normal(ks[5], (H, SI), jnp.float32) * sc(SI)}
    _L0_ffn_in = _L0_ffn_setup()
    _d = {'L0_attn_hidden_states': _L0_attn_in['hidden_states'], 'L0_attn_Wq': _L0_attn_in['Wq'], 'L0_attn_Wk': _L0_attn_in['Wk'], 'L0_attn_Wv': _L0_attn_in['Wv'], 'L0_attn_Wb': _L0_attn_in['Wb'], 'L0_attn_conv_q': _L0_attn_in['conv_q'], 'L0_attn_conv_k': _L0_attn_in['conv_k'], 'L0_attn_conv_v': _L0_attn_in['conv_v'], 'L0_attn_norm_w': _L0_attn_in['norm_w'], 'L0_attn_Wo': _L0_attn_in['Wo'], 'L0_ffn_gate_w': _L0_ffn_in['gate_w'], 'L0_ffn_expert_up_w': _L0_ffn_in['expert_up_w'], 'L0_ffn_expert_down_w': _L0_ffn_in['expert_down_w'], 'L0_ffn_shared_up_w': _L0_ffn_in['shared_up_w'], 'L0_ffn_shared_down_w': _L0_ffn_in['shared_down_w']}
    _x0 = _d['L0_attn_hidden_states']
    _d['L0_attn_hidden_states'] = jax.random.normal(jax.random.fold_in(jax.random.key(seed), 1), (1, 2048, 512), dtype=_x0.dtype)
    del _x0
    return _d

def reference(L0_attn_hidden_states, L0_attn_Wq, L0_attn_Wk, L0_attn_Wv, L0_attn_Wb, L0_attn_conv_q, L0_attn_conv_k, L0_attn_conv_v, L0_attn_norm_w, L0_attn_Wo, L0_ffn_gate_w, L0_ffn_expert_up_w, L0_ffn_expert_down_w, L0_ffn_shared_up_w, L0_ffn_shared_down_w):

    def _L0_attn_ref(hidden_states, Wq, Wk, Wv, Wb, conv_q, conv_k, conv_v, norm_w, Wo):
        import jax, jax.numpy as jnp
        import numpy as np
        B, T, D = (4, 512, 512)
        H = 8
        DK = D // H
        DV = D // H
        KCONV = 4
        L2_EPS = 1e-06
        RMS_EPS = 1e-05

        def short_conv_silu(x, w):
            t = x.shape[1]
            xp = jnp.pad(x, ((0, 0), (KCONV - 1, 0), (0, 0)))
            y = sum((xp[:, i:i + t, :] * w[:, i] for i in range(KCONV)))
            return jax.nn.silu(y)

        def l2norm(x):
            return x * jax.lax.rsqrt(jnp.sum(x * x, axis=-1, keepdims=True) + L2_EPS)

        def delta_rule(q, k, v, beta):
            q = q * q.shape[-1] ** (-0.5)
            qt = jnp.swapaxes(q, 0, 1)
            kt = jnp.swapaxes(k, 0, 1)
            vt = jnp.swapaxes(v, 0, 1)
            bt = jnp.swapaxes(beta, 0, 1)

            def step(S, inp):
                q_, k_, v_, b_ = inp
                u = b_[..., None] * (v_ - jnp.einsum('bhk,bhkv->bhv', k_, S))
                S = S + jnp.einsum('bhk,bhv->bhkv', k_, u)
                o = jnp.einsum('bhk,bhkv->bhv', q_, S)
                return (S, o)
            S0 = jnp.zeros((q.shape[0], q.shape[2], q.shape[3], v.shape[3]), q.dtype)
            _, o = jax.lax.scan(step, S0, (qt, kt, vt, bt))
            return jnp.swapaxes(o, 0, 1)
        x = hidden_states
        q = short_conv_silu(x @ Wq, conv_q)
        k = short_conv_silu(x @ Wk, conv_k)
        v = short_conv_silu(x @ Wv, conv_v)
        b, t = (x.shape[0], x.shape[1])
        q = q.reshape(b, t, H, DK)
        k = k.reshape(b, t, H, DK)
        v = v.reshape(b, t, H, DV)
        q = l2norm(q)
        k = l2norm(k)
        beta = jax.nn.sigmoid(x @ Wb)
        o = delta_rule(q, k, v, beta)
        o = o * jax.lax.rsqrt(jnp.mean(o * o, axis=-1, keepdims=True) + RMS_EPS) * norm_w
        o = o.reshape(b, t, H * DV)
        return o @ Wo

    def _L0_ffn_ref(x, gate_w, expert_up_w, expert_down_w, shared_up_w, shared_down_w):
        import jax, jax.numpy as jnp
        import numpy as np
        H = 512
        I = 352
        E = 16
        G = 4
        TOPK_GROUP = 2
        K = 4
        SI = 2 * I
        SCALE = 1.0
        NORM = True
        B, S = (4, 128)

        def _swiglu(h):
            g, u = jnp.split(h, 2, axis=-1)
            return jax.nn.silu(g) * u

        def _combine_weights(xt, gate_w):
            T = xt.shape[0]
            scores = jax.nn.softmax(xt @ gate_w.T, axis=-1)
            group_scores = scores.reshape(T, G, E // G).max(axis=-1)
            _, gidx = jax.lax.top_k(group_scores, TOPK_GROUP)
            gmask = jnp.zeros((T, G), bool).at[jnp.arange(T)[:, None], gidx].set(True)
            emask = jnp.repeat(gmask, E // G, axis=1)
            masked = jnp.where(emask, scores, 0.0)
            w, eidx = jax.lax.top_k(masked, K)
            if NORM:
                w = w / (w.sum(-1, keepdims=True) + 1e-20)
            w = w * SCALE
            return jnp.zeros((T, E), xt.dtype).at[jnp.arange(T)[:, None], eidx].add(w)
        Bq, Sq, _ = x.shape
        xt = x.reshape(-1, H)
        cw = _combine_weights(xt, gate_w)
        out = jnp.zeros_like(xt)
        for e in range(E):
            a = _swiglu(xt @ expert_up_w[e].T)
            out = out + cw[:, e:e + 1] * (a @ expert_down_w[e].T)
        out = out + _swiglu(xt @ shared_up_w.T) @ shared_down_w.T
        return out.reshape(Bq, Sq, H)
    x = L0_attn_hidden_states
    x = x + _L0_attn_ref(_layernorm(x, axis=-1), L0_attn_Wq, L0_attn_Wk, L0_attn_Wv, L0_attn_Wb, L0_attn_conv_q, L0_attn_conv_k, L0_attn_conv_v, L0_attn_norm_w, L0_attn_Wo)
    x = x + _L0_ffn_ref(_layernorm(x, axis=-1), L0_ffn_gate_w, L0_ffn_expert_up_w, L0_ffn_expert_down_w, L0_ffn_shared_up_w, L0_ffn_shared_down_w)
    return x

_drawn_inputs = setup_inputs


def setup_inputs(seed=0):
    import zlib

    import numpy as np

    out = dict(_drawn_inputs(seed))
    spreads = {'L0_attn_norm_w': (1.0, 0.2)}
    factors = {}
    for name, (base, spread) in spreads.items():
        noise = np.random.default_rng([zlib.crc32(name.encode()), seed]).standard_normal(out[name].shape)
        drawn = base * np.exp(spread * noise) if base else spread * noise
        out[name] = jnp.asarray(drawn.astype(out[name].dtype))
    for name, factor in factors.items():
        out[name] = (out[name] * factor).astype(out[name].dtype)
    return out
```

```python
from contextlib import ExitStack

import concourse.bass as bass
from concourse import mybir

F32 = mybir.dt.float32
I32 = mybir.dt.int32
ALU = mybir.AluOpType
ACT = mybir.ActivationFunctionType
AX = mybir.AxisListType

P = 128
T, D = 2048, 512
H, DH = 8, 64
NT = T // P
DC = D // P
HH = H // 2
TAPS = 4
HALO = TAPS - 1
LEVELS = 6
E = 16
LN_EPS, L2_EPS, RMS_EPS = 1e-5, 1e-6, 1e-5


T_STARTS = 4
T_UPDATES = 4 * (LEVELS - 1) + 2


def t_updates(k, hf):
    return 4 * (k - 1) + (2 * hf + 2 if k < LEVELS else hf + 1)


class Tile:

    def __init__(self, v, par):
        self.v, self.par = v, par


def wait_tile(eng, sem, tile, per_tile=1, k=None):
    k = per_tile if k is None else k
    eng.wait_ge(sem, tile.v * per_tile + k)


def wait_before(eng, sem, tile, per_tile=1, back=1):
    if isinstance(tile.v, int) and tile.v < back:
        return
    eng.wait_ge(sem, (tile.v - (back - 1)) * per_tile)


class Chain:

    def __init__(self, eng, sem, per_tile):
        self.eng, self.sem, self.n, self.k = eng, sem, per_tile, 0

    def begin(self, tile):
        assert self.k in (0, self.n), (self.k, self.n)
        self.tile, self.k = tile, 0
        self.started = not (isinstance(tile.v, int) and tile.v == 0)

    def done(self, ins):
        ins.then_inc(self.sem, 1)
        self.k += 1
        return self.k

    def wait(self, k=None):
        k = self.k if k is None else k
        if k or self.started:
            self.eng.wait_ge(self.sem, self.tile.v * self.n + k)


def run_tiles(eng, step):
    a, b = (lambda v: Tile(v, 0)), (lambda v: Tile(v, 1))
    step(None, a(0), None)
    step(a(0), b(1), None)
    step(b(1), a(2), a(0))
    with eng.Fori(2, NT - 2, 2) as i:
        step(a(i), b(i + 1), b(i - 1))
        step(b(i + 1), a(i + 2), a(i))
    step(a(NT - 2), b(NT - 1), b(NT - 3))
    step(b(NT - 1), None, a(NT - 2))
    step(None, None, b(NT - 1))


def attention(nc, es, x_d, wq_d, wk_d, wv_d, wb_d, cq_d, ck_d, cv_d, nw_d, wo_d, gw_d, xall, x2nT, lg):

    def sb(name, shape, dt=F32):
        return es.enter_context(nc.sbuf_tensor(name, shape, dt))

    def sem(name):
        return es.enter_context(nc.semaphore(name))

    ident = sb("ident", [P, P])
    causal = sb("causal", [P, P])
    xor_i, xor_j = sb("xor_i", [P, P], I32), sb("xor_j", [P, P], I32)
    dist = sb("dist", [P, P])
    dist_lo, dist_up = sb("dist_lo", [P, P]), sb("dist_up", [P, P])
    ge_a, ge_b = sb("ge_a", [P, P]), sb("ge_b", [P, P])
    m_lo = sb("m_lo", [P, LEVELS, P], I32)
    m_up = sb("m_up", [P, LEVELS, P], I32)
    nhalf = sb("nhalf", [P, 16])
    w3 = sb("w3", [P, 3, DC, D])
    wb = sb("wb", [P, DC, H])
    cw = sb("cw", [P, 3 * DC, TAPS])
    nw = sb("nw", [P, 1])
    wo = sb("wo", [P, DC, D])
    gw = sb("gw", [P, DC, E])
    xn = sb("xn", [P, D])
    xnT = sb("xnT", [P, DC, P])
    st1, mv1, r1 = sb("st1", [P, 6]), sb("mv1", [P, 2]), sb("r1", [P, 1])
    ve1 = sb("ve1", [P, 1])
    raw = sb("raw", [P, 3 * DC, HALO + P])
    acc = sb("acc", [P, 3 * DC, P])
    sil = sb("sil", [P, 3 * DC, P])
    th, beta, nbeta = sb("th", [P, H]), sb("beta", [P, H]), sb("nbeta", [P, H])
    tok = sb("tok", [P, 2, D])
    sq = sb("sq", [P, 2, D])
    ss, rqk = sb("ss", [P, 2 * H]), sb("rqk", [P, 2 * H])
    qn = sb("qn", [P, D])
    kn = [sb(f"kn{i}", [P, D]) for i in range(2)]
    nkb = sb("nkb", [P, D])
    vb = [sb(f"vb{i}", [P, D]) for i in range(2)]
    QT, KT, KBT = ([sb(f"{n}{i}", [P, DC, P]) for i in range(2)] for n in ("QT", "KT", "KBT"))
    AT, Ti, TiT, Ys, PT = ([sb(f"{n}{i}", [P, HH, P]) for i in range(2)] for n in ("AT", "Ti", "TiT", "Ys", "PT"))
    S = sb("S", [P, HH * DH])
    R, U = sb("R", [P, 2, HH, DH]), sb("U", [P, 2, HH, DH])
    osb, osq, on = sb("osb", [P, D]), sb("osq", [P, D]), sb("on", [P, D])
    so, ro = sb("so", [P, H]), sb("ro", [P, H])
    oT = sb("oT", [P, DC, P])
    st2, mv2, r2, ve2 = sb("st2", [P, 6]), sb("mv2", [P, 2]), sb("r2", [P, 1]), sb("ve2", [P, 1])
    x2n = sb("x2n", [P, D])
    x2g = sb("x2g", [P, DC, P])

    def bank(name):
        return es.enter_context(nc.psum_tensor(name, [P, D], F32))

    pY, pZ, pZT = ([bank(f"{n}{i}") for i in range(2)] for n in ("pY", "pZ", "pZT"))
    pF = [bank(f"pF{i}") for i in range(2)]

    (s_xload, s_wload, s_wo, s_iota, s_const, s_masks, s_wos, s_S0,
     s_stats, s_r1, s_xn, s_xTp, s_xnT, s_proj, s_raw, s_conv, s_sil, s_bp, s_th, s_beta, s_nbeta,
     s_tokp, s_tok, s_sq, s_vb, s_ss, s_rqk, s_knorm, s_back, s_qkT,
     s_D1, s_AT, s_T0, s_PT, s_Y, s_Ys, s_Z, s_T, s_Rp, s_R, s_Up, s_U, s_Op, s_O, s_Sp, s_S,
     s_so, s_ro, s_on, s_oTp, s_oT, s_yp, s_x2, s_r2, s_x2n, s_x2Tp, s_x2nT, s_lgp, s_lg,
     c_dF, c_dD, c_dB, c_aF, c_init) = (sem(n) for n in (
        "x_loaded", "w_loaded", "wo_loaded", "iota_done", "const_done", "masks_done", "wo_scaled", "S_zeroed",
        "ln1_stats", "ln1_rstd", "xn_ready", "xnT_psum", "xnT_ready", "proj_psum", "raw_ready", "conv_done",
        "silu_done", "beta_psum", "tanh_done", "beta_ready", "nbeta_ready",
        "tok_psum", "tok_ready", "tok_squared", "vb_ready", "qk_sums", "qk_rnorm", "qk_normed", "back_psum", "qkT_ready",
        "gram_psum", "AT_ready", "T_started", "PT_ready", "Y_psum", "Y_ready", "Z_psum", "T_updated",
        "R_psum", "R_ready", "U_psum", "U_ready", "O_psum", "O_ready", "S_psum", "S_ready",
        "o_sums", "o_rnorm", "on_ready", "oT_psum", "oT_ready", "y_psum", "x2_ready", "ln2_rstd", "x2n_ready",
        "x2nT_psum", "x2nT_ready", "logit_psum", "logits_ready",
        "dve_front", "dve_delta", "dve_back", "act_front", "init_chain"))

    def heads(ap):
        return ap.rearrange("p (h d) -> p h d", d=DH)

    def mats(ap):
        return ap.rearrange("p (h n) -> p h n", n=P)

    def over_heads(ap):
        return ap.unsqueeze(2).to_broadcast([P, H, DH])

    def by_half(buf, hf):
        return buf[:, :].rearrange("p (n f d) -> p f n d", f=2, d=DH)[:, hf]

    def settle(eng):
        eng.nop(nofuse=True)
        eng.wait_ge(s_const, 5)

    def over_mats(ap):
        return ap.unsqueeze(1).to_broadcast([P, HH, P])

    with nc.Block() as block:

        @block.sync
        def _(sp):
            xv = x_d.rearrange("b (t p) d -> p (b t) d", p=P)
            for g in range(4):
                sp.dma_start(xall[:, 4 * g:4 * g + 4, :], xv[:, 4 * g:4 * g + 4, :]).then_inc(s_xload, 16)
                if g == 0:
                    for i, w in enumerate((wq_d, wk_d, wv_d)):
                        sp.dma_start(w3[:, i], w.rearrange("(c p) n -> p c n", p=P)).then_inc(s_wload, 16)
                    sp.dma_start(wb[:, :, :], wb_d.rearrange("(c p) n -> p c n", p=P)).then_inc(s_wload, 16)
                    for i, w in enumerate((cq_d, ck_d, cv_d)):
                        sp.dma_start(cw[:, DC * i:DC * i + DC, :], w.rearrange("(c p) n -> p c n", p=P))\
                          .then_inc(s_wload, 16)
            for i in range(2):
                sp.dma_start(nw[DH * i:DH * i + DH, :], nw_d.rearrange("(p o) -> p o", o=1)).then_inc(s_wo, 16)
            sp.dma_start(wo[:, :, :], wo_d.rearrange("(c p) n -> p c n", p=P)).then_inc(s_wo, 16)
            sp.dma_start(gw[:, :, :], gw_d.rearrange("(c p) n -> p c n", p=P)).then_inc(s_wo, 16)

        @block.gpsimd
        def _(pool):
            pool.memset(ident[:, :], 0.0).then_inc(s_const, 1)
            pool.memset(causal[:, :], 1.0).then_inc(s_const, 1)
            pool.memset(nhalf[:, :], -0.5).then_inc(s_const, 1)
            pool.iota(xor_i[:, :], pattern=[[0, P]], base=0, channel_multiplier=1).then_inc(s_iota, 1)
            pool.iota(xor_j[:, :], pattern=[[1, P]], base=0, channel_multiplier=0).then_inc(s_iota, 1)
            pool.wait_ge(s_const, 3)
            pool.affine_select(out=ident[:, :], in_=ident[:, :], compare_op=ALU.not_equal, fill=1.0,
                               base=0, pattern=[[-1, P]], channel_multiplier=1).then_inc(s_const, 1)
            pool.affine_select(out=causal[:, :], in_=causal[:, :], compare_op=ALU.is_ge, fill=0.0,
                               base=0, pattern=[[1, P]], channel_multiplier=-1).then_inc(s_const, 1)
            pool.wait_ge(s_masks, 2)
            pool.affine_select(out=dist_lo[:, :], in_=dist[:, :], compare_op=ALU.is_gt, fill=0.0,
                               base=0, pattern=[[-1, P]], channel_multiplier=1).then_inc(s_const, 1)
            pool.affine_select(out=dist_up[:, :], in_=dist[:, :], compare_op=ALU.is_gt, fill=0.0,
                               base=0, pattern=[[1, P]], channel_multiplier=-1).then_inc(s_const, 1)

            def rstd1(t):
                wait_tile(pool, s_stats, t)
                wait_before(pool, s_xn, t)
                pool.tensor_tensor(r1[:, :], ve1[:, :], nhalf[:, 0:1], ALU.pow).then_inc(s_r1, 1)

            def qk_norms(t):
                wait_tile(pool, s_ss, t, 2)
                wait_before(pool, s_knorm, t, 3)
                pool.tensor_tensor(rqk[:, :], ss[:, :], nhalf[:, :], ALU.pow).then_inc(s_rqk, 1)
                wait_tile(pool, s_rqk, t)
                wait_tile(pool, s_beta, t)
                wait_before(pool, s_back, t, 3)
                wait_before(pool, s_Sp, t, back=2)
                pool.tensor_tensor(heads(qn[:, :]), heads(tok[:, 0, :]), over_heads(rqk[:, 0:H]), ALU.mult)\
                    .then_inc(s_knorm, 1)
                pool.tensor_tensor(heads(kn[t.par][:, :]), heads(tok[:, 1, :]), over_heads(rqk[:, H:2 * H]), ALU.mult)\
                    .then_inc(s_knorm, 1)
                wait_tile(pool, s_knorm, t, 3, 2)
                pool.tensor_tensor(heads(nkb[:, :]), heads(kn[t.par][:, :]), over_heads(nbeta[:, :]), ALU.mult)\
                    .then_inc(s_knorm, 1)

            def o_rnorm(t):
                wait_tile(pool, s_so, t)
                wait_before(pool, s_on, t)
                pool.tensor_tensor(ro[:, :], so[:, :], nhalf[:, 0:H], ALU.pow).then_inc(s_ro, 1)

            def rstd2(t):
                wait_tile(pool, s_x2, t, 2)
                wait_before(pool, s_x2n, t)
                pool.tensor_tensor(r2[:, :], ve2[:, :], nhalf[:, 0:1], ALU.pow).then_inc(s_r2, 1)

            def step(t, nxt, prev):
                if nxt:
                    rstd1(nxt)
                if prev:
                    o_rnorm(prev)
                    rstd2(prev)
                if nxt:
                    qk_norms(nxt)

            run_tiles(pool, step)

        @block.scalar
        def _(act):
            cf = Chain(act, c_aF, 3)

            def xT_copy(t):
                wait_tile(act, s_xTp, t)
                wait_before(act, s_bp, t)
                act.activation(xnT[:, :, :], mats(pF[0][:, :]), ACT.Copy).then_inc(s_xnT, 1)

            def raw_copy(t, i):
                if i == 0:
                    cf.begin(t)
                sec = slice(DC * i, DC * i + DC)
                if isinstance(t.v, int) and t.v == 0:
                    act.wait_ge(s_S0, 2)
                    cf.done(act.activation(raw[:, sec, 0:HALO], raw[:, sec, P:P + HALO], ACT.Copy))
                else:
                    wait_before(act, s_conv, t, 3 * 4)
                    cf.done(act.activation(raw[:, sec, 0:HALO], raw[:, sec, P:P + HALO], ACT.Copy))
                cf.wait()
                wait_tile(act, s_proj, t, 3, i + 1)
                act.activation(raw[:, sec, HALO:], mats(pF[(i + 1) % 2][:, :]), ACT.Copy).then_inc(s_raw, 1)

            def silu(t, i):
                sec = slice(DC * i, DC * i + DC)
                wait_tile(act, s_conv, t, 3 * 4, 4 * i + 4)
                wait_before(act, s_tokp, t, 3)
                act.activation(sil[:, sec, :], acc[:, sec, :], ACT.Silu).then_inc(s_sil, 1)

            def tanh(t):
                wait_tile(act, s_bp, t)
                wait_before(act, s_beta, t)
                act.activation(th[:, :], pF[0][:, 0:H], ACT.Tanh, scale=0.5).then_inc(s_th, 1)

            def tok_copy(t, i):
                wait_tile(act, s_tokp, t, 3, i + 1)
                wait_before(act, s_knorm, t, 3)
                act.activation(tok[:, i, :], pF[(1, 0)[i]][:, :], ACT.Copy).then_inc(s_tok, 1)
                wait_before(act, s_ss, t, 2)
                act.activation(sq[:, i, :], pF[(1, 0)[i]][:, :], ACT.Square).then_inc(s_sq, 1)

            def back_copy(t, i):
                dst = (QT, KT, KBT)[i][t.par]
                wait_tile(act, s_back, t, 3, i + 1)
                wait_before(act, s_Op, t, back=2)
                act.activation(dst[:, :, :], mats(pF[i % 2][:, :]), ACT.Copy,
                               scale=DH ** -0.5 if i == 0 else 1.0).then_inc(s_qkT, 1)

            def at_copy(t, hf):
                wait_tile(act, s_D1, t, 2, hf + 1)
                wait_before(act, s_Z, t, 12)
                wait_before(act, s_T0, t, T_STARTS)
                act.activation(AT[hf][:, :, :], mats(pZ[hf][:, :]), ACT.Copy).then_inc(s_AT, 1)

            def y_copy(t, k, hf):
                wait_tile(act, s_Y, t, 2 * LEVELS, 2 * k - 1 + hf)
                if k > 1:
                    wait_tile(act, s_Z, t, 2 * LEVELS, 2 * k - 3 + hf)
                else:
                    wait_before(act, s_Z, t, 2 * LEVELS)
                if k < LEVELS:
                    act.activation(Ys[hf][:, :, :], mats(pY[hf][:, :]), ACT.Copy).then_inc(s_Ys, 1)
                else:
                    act.activation(Ys[hf][DH:P, :, 0:DH], mats(pY[hf][DH:P, :])[:, :, 0:DH], ACT.Copy)\
                       .then_inc(s_Ys, 1)

            def u_copy(t):
                wait_tile(act, s_Up, t)
                wait_before(act, s_Sp, t)
                act.activation(U[:, :, :, :], pZT[0][:, :].rearrange("p (f n d) -> p f n d", f=2, d=DH), ACT.Copy)\
                   .then_inc(s_U, 1)

            def o_copy(t):
                wait_tile(act, s_Op, t)
                wait_before(act, s_on, t)
                for hf in range(2):
                    o = heads(pZ[hf][:, 0:HH * DH])
                    act.activation(by_half(osb, hf), o, ACT.Copy).then_inc(s_O, 1)
                    act.activation(by_half(osq, hf), o, ACT.Square).then_inc(s_O, 1)

            def oT_copy(t):
                wait_tile(act, s_oTp, t)
                wait_before(act, s_yp, t)
                act.activation(oT[:, :, :], mats(pF[1][:, :]), ACT.Copy).then_inc(s_oT, 1)

            def x2T_copy(t):
                wait_tile(act, s_x2Tp, t)
                wait_before(act, s_lgp, t)
                act.activation(x2g[:, :, :], mats(pF[0][:, :]), ACT.Copy).then_inc(s_x2nT, 1)
                act.activation(x2nT[:, :, bass.ts(t.v, P)], mats(pF[0][:, :]), ACT.Copy).then_inc(s_x2nT, 1)

            def step(t, nxt, prev):
                if t:
                    at_copy(t, 0)
                    at_copy(t, 1)
                for k in range(1, LEVELS + 1):
                    if t:
                        y_copy(t, k, 0)
                        y_copy(t, k, 1)
                    if nxt:
                        if k == 1:
                            xT_copy(nxt)
                            raw_copy(nxt, 0)
                        elif k == 2:
                            raw_copy(nxt, 1)
                            raw_copy(nxt, 2)
                        elif k == 3:
                            tanh(nxt)
                            silu(nxt, 0)
                        elif k == 4:
                            silu(nxt, 1)
                            tok_copy(nxt, 0)
                        elif k == 5:
                            silu(nxt, 2)
                            tok_copy(nxt, 1)
                    if prev:
                        if k == 3:
                            oT_copy(prev)
                        elif k == 6:
                            x2T_copy(prev)
                if t:
                    u_copy(t)
                    o_copy(t)
                if nxt:
                    for i in range(3):
                        back_copy(nxt, i)

            run_tiles(act, step)

        @block.tensor
        def _(pe):
            def xT(t):
                wait_tile(pe, s_xn, t)
                wait_before(pe, s_qkT, t, 3)
                for c in range(DC):
                    mm = pe.transpose(pF[0][:, c * P:(c + 1) * P], xn[:, c * P:(c + 1) * P], ident[:, :])
                mm.then_inc(s_xTp, 1)

            def project(t, i):
                if i == 0:
                    wait_tile(pe, s_xnT, t)
                if i == 2:
                    wait_tile(pe, s_raw, t, 3, 1)
                if i == 1:
                    wait_tile(pe, s_xnT, t)
                for c in range(DC):
                    for k in range(DC):
                        mm = pe.matmul(pF[(i + 1) % 2][:, c * P:(c + 1) * P], w3[:, i, k, c * P:(c + 1) * P],
                                       xnT[:, k, :], start=(k == 0), stop=(k == DC - 1))
                mm.then_inc(s_proj, 1)

            def betas(t):
                wait_tile(pe, s_raw, t, 3, 2)
                for k in range(DC):
                    mm = pe.matmul(pF[0][:, 0:H], xnT[:, k, :], wb[:, k, :], start=(k == 0), stop=(k == DC - 1))
                mm.then_inc(s_bp, 1)

            def to_tokens(t, i):
                wait_tile(pe, s_sil, t, 3, i + 1)
                if i == 0:
                    wait_tile(pe, s_raw, t, 3, 3)
                elif i == 1:
                    wait_tile(pe, s_th, t)
                else:
                    wait_tile(pe, s_sq, t, 2, 1)
                for c in range(DC):
                    mm = pe.transpose(pF[(1, 0, 1)[i]][:, c * P:(c + 1) * P], sil[:, DC * i + c, :], ident[:, :])
                mm.then_inc(s_tokp, 1)

            def to_channels(t, i):
                src = (qn, kn[t.par], nkb)[i]
                wait_tile(pe, s_knorm, t, 3, i + 1)
                if i == 0:
                    wait_tile(pe, s_sq, t, 2, 2)
                elif i == 1:
                    wait_tile(pe, s_vb, t)
                else:
                    wait_tile(pe, s_qkT, t, 3, 1)
                for c in range(DC):
                    mm = pe.transpose(pF[i % 2][:, c * P:(c + 1) * P], src[:, c * P:(c + 1) * P], ident[:, :])
                mm.then_inc(s_back, 1)

            def gram(t, hf):
                if hf == 0:
                    wait_tile(pe, s_qkT, t, 3)
                    wait_before(pe, s_O, t, 4)
                    wait_before(pe, s_S, t)
                q, k, kb = QT[t.par], KT[t.par], KBT[t.par]
                for n in range(HH):
                    rows, cols = slice(DH * hf, DH * hf + DH), slice(n * P, (n + 1) * P)
                    pe.matmul(pZ[hf][:, cols], k[rows, n, :], kb[rows, n, :], start=True, stop=True)
                    pe.matmul(pY[hf][:, cols], kb[rows, n, :], k[rows, n, :], start=True, stop=True)
                    mm = pe.matmul(pZT[hf][:, cols], k[rows, n, :], q[rows, n, :], start=True, stop=True)
                mm.then_inc(s_D1, 1)

            def level_y(t, k, hf):
                if k == 1:
                    wait_tile(pe, s_AT, t, 2, hf + 1)
                    wait_tile(pe, s_T0, t, T_STARTS, 2 * hf + 2)
                else:
                    wait_tile(pe, s_Ys, t, 2 * LEVELS, 2 * k - 3 + hf)
                    wait_tile(pe, s_T, t, T_UPDATES, t_updates(k - 1, hf))
                if k == LEVELS:
                    settle(pe)
                for n in range(HH):
                    if k < LEVELS:
                        mm = pe.matmul(pY[hf][:, n * P:(n + 1) * P], AT[hf][:, n, :], Ti[hf][:, n, :],
                                       start=True, stop=True)
                    else:
                        mm = pe.matmul(pY[hf][DH:P, n * P:n * P + DH], AT[hf][0:DH, n, DH:P], Ti[hf][0:DH, n, 0:DH],
                                       start=True, stop=True)
                mm.then_inc(s_Y, 1)

            def level_z(t, k, hf):
                wait_tile(pe, s_Ys, t, 2 * LEVELS, 2 * k - 1 + hf)
                if k == 1:
                    wait_tile(pe, s_PT, t, 2, hf + 1)
                if k == LEVELS:
                    settle(pe)
                for n in range(HH):
                    cols = slice(n * P, (n + 1) * P)
                    if k < LEVELS:
                        pe.matmul(pZ[hf][:, cols], TiT[hf][:, n, :], Ys[hf][:, n, :], start=True, stop=True)
                        mm = pe.matmul(pZT[hf][:, cols], Ys[hf][:, n, :], TiT[hf][:, n, :], start=True, stop=True)
                    else:
                        mm = pe.matmul(pZT[hf][0:DH, n * P + DH:(n + 1) * P], Ys[hf][DH:P, n, 0:DH],
                                       TiT[hf][DH:P, n, DH:P], start=True, stop=True)
                mm.then_inc(s_Z, 1)

            def state_out(t):
                wait_tile(pe, s_Ys, t, 2 * LEVELS)
                if isinstance(t.v, int) and t.v == 0:
                    pe.wait_ge(s_S0, 1)
                else:
                    wait_before(pe, s_S, t)
                for hf in range(2):
                    rows = slice(DH * hf, DH * hf + DH)
                    for n in range(HH):
                        mm = pe.matmul(pY[hf][:, n * DH:(n + 1) * DH], KBT[t.par][rows, n, :],
                                       S[rows, n * DH:(n + 1) * DH], start=True, stop=True)
                    mm.then_inc(s_Rp, 1)

            def solve(t):
                wait_tile(pe, s_T, t, T_UPDATES)
                for hf in range(2):
                    wait_tile(pe, s_R, t, 2, hf + 1)
                    for n in range(HH):
                        mm = pe.matmul(pZT[0][:, (HH * hf + n) * DH:(HH * hf + n + 1) * DH], TiT[hf][:, n, :],
                                       R[:, hf, n, :], start=True, stop=True)
                mm.then_inc(s_Up, 1)

            def outputs(t):
                wait_tile(pe, s_U, t)
                for hf in range(2):
                    rows = slice(DH * hf, DH * hf + DH)
                    for n in range(HH):
                        o = pZ[hf][:, n * DH:(n + 1) * DH]
                        pe.matmul(o, QT[t.par][rows, n, :], S[rows, n * DH:(n + 1) * DH], start=True, stop=False)
                        mm = pe.matmul(o, PT[hf][:, n, :], U[:, hf, n, :], start=False, stop=True)
                mm.then_inc(s_Op, 1)
                for hf in range(2):
                    rows = slice(DH * hf, DH * hf + DH)
                    for n in range(HH):
                        h = 2 * n + hf
                        mm = pe.matmul(pZT[1][rows, n * DH:(n + 1) * DH], kn[t.par][:, h * DH:(h + 1) * DH],
                                       U[:, hf, n, :], start=True, stop=True)
                mm.then_inc(s_Sp, 1)

            def oT_turn(t, nxt):
                wait_tile(pe, s_on, t)
                wait_before(pe, s_lg, t)
                if nxt:
                    wait_tile(pe, s_raw, nxt, 3, 3)
                for c in range(DC):
                    mm = pe.transpose(pF[1][:, c * P:(c + 1) * P], on[:, c * P:(c + 1) * P], ident[:, :])
                mm.then_inc(s_oTp, 1)

            def out_proj(t, nxt):
                wait_tile(pe, s_oT, t)
                if isinstance(t.v, int) and t.v == 0:
                    pe.wait_ge(s_wos, DC)
                wait_before(pe, s_x2nT, t, 2)
                if nxt:
                    wait_tile(pe, s_th, nxt)
                for k in range(DC):
                    mm = pe.matmul(pF[0][:, :], oT[:, k, :], wo[:, k, :], start=(k == 0), stop=(k == DC - 1))
                mm.then_inc(s_yp, 1)

            def x2T(t, nxt):
                wait_tile(pe, s_x2n, t)
                if nxt:
                    wait_tile(pe, s_sq, nxt, 2, 2)
                for c in range(DC):
                    mm = pe.transpose(pF[0][:, c * P:(c + 1) * P], x2n[:, c * P:(c + 1) * P], ident[:, :])
                mm.then_inc(s_x2Tp, 1)

            def gate(t, nxt):
                wait_tile(pe, s_x2nT, t, 2, 1)
                if nxt:
                    wait_tile(pe, s_vb, nxt)
                for k in range(DC):
                    mm = pe.matmul(pF[1][:, 0:E], x2g[:, k, :], gw[:, k, :], start=(k == 0), stop=(k == DC - 1))
                mm.then_inc(s_lgp, 1)

            pe.wait_ge(s_wload, 7 * 16)
            pe.wait_ge(s_const, 5)

            def step(t, nxt, prev):
                if t:
                    gram(t, 0)
                    gram(t, 1)
                for k in range(1, LEVELS + 1):
                    if t:
                        level_y(t, k, 0)
                        level_y(t, k, 1)
                        level_z(t, k, 0)
                    if k == 1 and nxt:
                        xT(nxt)
                    if k == 2 and nxt:
                        project(nxt, 1)
                    if k == 3 and nxt:
                        betas(nxt)
                    if k == 4:
                        if prev:
                            out_proj(prev, nxt)
                    if k == 5 and nxt:
                        to_tokens_k(nxt, prev)
                    if k == 6 and prev:
                        x2T(prev, nxt)
                    if t:
                        level_z(t, k, 1)
                    if k == 1 and nxt:
                        project(nxt, 0)
                    if k == 2 and nxt:
                        project(nxt, 2)
                    if k == 3 and prev:
                        oT_turn(prev, nxt)
                    if k == 4 and nxt:
                        to_tokens_q(nxt, prev)
                    if k == 5 and nxt:
                        to_tokens(nxt, 2)
                    if k == 6 and prev:
                        gate(prev, nxt)
                if t:
                    state_out(t)
                    solve(t)
                    outputs(t)
                if nxt:
                    for i in range(3):
                        if i == 0 and prev:
                            wait_tile(pe, s_x2nT, prev, 2)
                        if i == 1 and prev:
                            wait_tile(pe, s_lg, prev)
                        to_channels(nxt, i)

            def to_tokens_q(nxt, prev):
                if prev:
                    wait_tile(pe, s_oT, prev)
                to_tokens(nxt, 0)

            def to_tokens_k(nxt, prev):
                if prev:
                    wait_tile(pe, s_x2, prev, 2, 1)
                to_tokens(nxt, 1)

            run_tiles(pe, step)

        @block.vector
        def _(dve):
            fr, de, ba = Chain(dve, c_dF, 2 + 6 * 6 + 2), Chain(dve, c_dD, 4), Chain(dve, c_dB, 3)

            dve.memset(S[:, :], 0.0).then_inc(s_S0, 1)
            dve.memset(raw[:, :, P:P + HALO], 0.0).then_inc(s_S0, 1)
            dve.wait_ge(s_iota, 2)
            dve.tensor_tensor(xor_j[:, :], xor_i[:, :], xor_j[:, :], ALU.bitwise_xor).then_inc(s_masks, 1)
            dve.wait_ge(s_masks, 1)
            dve.tensor_copy(dist[:, :], xor_j[:, :]).then_inc(s_masks, 1)
            dve.wait_ge(s_const, 7)
            n = 0
            for src, dst in ((dist_lo, m_lo), (dist_up, m_up)):
                for k in range(LEVELS):
                    if n:
                        dve.wait_ge(c_init, n)
                    dve.tensor_scalar(ge_a[:, :], src[:, :], float(2 ** k), None, ALU.is_ge).then_inc(c_init, 1)
                    dve.tensor_scalar(ge_b[:, :], src[:, :], float(2 ** (k + 1)), None, ALU.is_ge).then_inc(c_init, 1)
                    n += 2
                    dve.wait_ge(c_init, n)
                    dve.tensor_tensor(dst[:, k, :], ge_a[:, :], ge_b[:, :], ALU.subtract).then_inc(c_init, 1)
                    n += 1
            dve.wait_ge(c_init, n)
            dve.wait_ge(s_wload, 7 * 16)
            dve.wait_ge(s_wo, 4 * 16)
            for c in range(DC):
                dve.tensor_scalar(wo[:, c, :], wo[:, c, :], nw[:, 0:1], None, ALU.mult).then_inc(s_wos, 1)

            def ln1_stats(t):
                fr.begin(t)
                if isinstance(t.v, int) and t.v < 2:
                    dve.wait_ge(s_xload, 16 if t.v == 0 else 4 * 16)
                fr.wait(0)
                wait_before(dve, s_xn, t)
                settle(dve)
                a = fr.done(dve.bn_stats(st1[:, :], xall[:, t.v, :]))
                fr.wait(a)
                settle(dve)
                b = fr.done(dve.bn_aggr(mv1[:, :], st1[:, :]))
                fr.wait(b)
                wait_before(dve, s_r1, t)
                dve.tensor_scalar(ve1[:, :], mv1[:, 1:2], LN_EPS, None, ALU.add).then_inc(s_stats, 1)

            def make_xn(t):
                wait_tile(dve, s_r1, t)
                wait_before(dve, s_xTp, t)
                dve.tensor_scalar(xn[:, :], xall[:, t.v, :], mv1[:, 0:1], r1[:, 0:1], ALU.subtract, ALU.mult)\
                   .then_inc(s_xn, 1)

            def conv(t, i, half):
                if half == 0:
                    wait_tile(dve, s_raw, t, 3, i + 1)
                    wait_before(dve, s_sil, t, 3)
                cs = [DC * i + 2 * half, DC * i + 2 * half + 1]
                last = {}
                for c in cs:
                    last[c] = fr.done(dve.tensor_scalar(acc[:, c, :], raw[:, c, HALO:HALO + P],
                                                        cw[:, c, TAPS - 1:TAPS], None, ALU.mult))
                for j in range(TAPS - 1):
                    for c in cs:
                        fr.wait(last[c])
                        ins = dve.scalar_tensor_tensor(out=acc[:, c, :], in0=raw[:, c, j:j + P],
                                                       scalar=cw[:, c, j:j + 1], in1=acc[:, c, :],
                                                       op0=ALU.mult, op1=ALU.add)
                        if j < TAPS - 2:
                            last[c] = fr.done(ins)
                        else:
                            ins.then_inc(s_conv, 1)

            def betas(t):
                wait_tile(dve, s_th, t)
                wait_before(dve, s_knorm, t, 3)
                wait_before(dve, s_vb, t)
                dve.tensor_scalar(nbeta[:, :], th[:, :], -0.5, -0.5, ALU.mult, ALU.add)\
                   .then_inc(s_nbeta, 1)
                dve.tensor_scalar(beta[:, :], th[:, :], 0.5, 0.5, ALU.mult, ALU.add).then_inc(s_beta, 1)

            def sums(t, i):
                wait_tile(dve, s_sq, t, 2, i + 1)
                wait_before(dve, s_rqk, t)
                a = fr.done(dve.tensor_reduce(ss[:, H * i:H * i + H], heads(sq[:, i, :]), AX.X, ALU.add))
                fr.wait(a)
                dve.tensor_scalar(ss[:, H * i:H * i + H], ss[:, H * i:H * i + H], L2_EPS, None, ALU.add)\
                   .then_inc(s_ss, 1)

            def make_vb(t):
                wait_tile(dve, s_tokp, t, 3, 3)
                wait_tile(dve, s_beta, t)
                wait_before(dve, s_R, t, 2, back=2)
                dve.tensor_tensor(heads(vb[t.par][:, :]), heads(pF[1][:, :]), over_heads(beta[:, :]), ALU.mult)\
                   .then_inc(s_vb, 1)

            def start_t(t, hf):
                if hf == 0:
                    de.begin(t)
                wait_before(dve, s_Up, t)
                wait_before(dve, s_Op, t)
                if hf == 0:
                    wait_before(dve, s_T, t, T_UPDATES)
                a = de.done(dve.tensor_copy(Ti[hf][:, :, :], over_mats(ident[:, :])))
                b = de.done(dve.tensor_copy(TiT[hf][:, :, :], over_mats(ident[:, :])))
                wait_tile(dve, s_D1, t, 2, hf + 1)
                dve.tensor_tensor(PT[hf][:, :, :], mats(pZT[hf][:, :]), over_mats(causal[:, :]), ALU.mult)\
                   .then_inc(s_PT, 1)
                de.wait(b)
                settle(dve)
                dve.copy_predicated(Ti[hf][:, :, :], over_mats(m_lo[:, 0, :]), mats(pY[hf][:, :])).then_inc(s_T0, 1)
                wait_tile(dve, s_AT, t, 2, hf + 1)
                settle(dve)
                dve.copy_predicated(TiT[hf][:, :, :], over_mats(m_up[:, 0, :]), AT[hf][:, :, :]).then_inc(s_T0, 1)

            def update_t(t, k, hf):
                wait_tile(dve, s_Z, t, 2 * LEVELS, 2 * k - 1 + hf)
                if k == 1:
                    wait_tile(dve, s_T0, t, T_STARTS, 2 * hf + 2)
                else:
                    wait_tile(dve, s_T, t, T_UPDATES, t_updates(k - 1, hf))
                if k < LEVELS:
                    settle(dve)
                    dve.copy_predicated(Ti[hf][:, :, :], over_mats(m_lo[:, k, :]), mats(pZ[hf][:, :]))\
                       .then_inc(s_T, 1)
                    dve.copy_predicated(TiT[hf][:, :, :], over_mats(m_up[:, k, :]), mats(pZT[hf][:, :]))\
                       .then_inc(s_T, 1)
                else:
                    dve.tensor_copy(TiT[hf][0:DH, :, DH:P], mats(pZT[hf][0:DH, :])[:, :, DH:P]).then_inc(s_T, 1)

            def make_r(t):
                wait_tile(dve, s_vb, t)
                wait_before(dve, s_Up, t)
                for hf in range(2):
                    wait_tile(dve, s_Rp, t, 2, hf + 1)
                    dve.tensor_tensor(R[:, hf], heads(pY[hf][:, 0:HH * DH]), by_half(vb[t.par], hf), ALU.add)\
                       .then_inc(s_R, 1)

            def update_s(t):
                wait_tile(dve, s_Sp, t)
                wait_before(dve, s_S, t)
                if isinstance(t.v, int) and t.v == 0:
                    dve.wait_ge(s_S0, 1)
                dve.tensor_tensor(S[:, :], S[:, :], pZT[1][:, 0:HH * DH], ALU.add).then_inc(s_S, 1)

            def o_sums(t):
                wait_tile(dve, s_O, t, 4)
                wait_before(dve, s_ro, t)
                ba.begin(t)
                a = ba.done(dve.tensor_reduce(so[:, :], heads(osq[:, :]), AX.X, ALU.add))
                ba.wait(a)
                dve.tensor_scalar(so[:, :], so[:, :], 1.0 / DH, RMS_EPS, ALU.mult, ALU.add).then_inc(s_so, 1)

            def make_on(t):
                wait_tile(dve, s_ro, t)
                wait_before(dve, s_oTp, t)
                dve.tensor_tensor(heads(on[:, :]), heads(osb[:, :]), over_heads(ro[:, :]), ALU.mult).then_inc(s_on, 1)

            def make_x2(t):
                wait_tile(dve, s_yp, t)
                dve.tensor_tensor(xall[:, t.v, :], xall[:, t.v, :], pF[0][:, :], ALU.add).then_inc(s_x2, 1)
                wait_tile(dve, s_x2, t, 2, 1)
                settle(dve)
                a = ba.done(dve.bn_stats(st2[:, :], xall[:, t.v, :]))
                ba.wait(a)
                wait_before(dve, s_x2n, t)
                settle(dve)
                b = ba.done(dve.bn_aggr(mv2[:, :], st2[:, :]))
                ba.wait(b)
                wait_before(dve, s_r2, t)
                dve.tensor_scalar(ve2[:, :], mv2[:, 1:2], LN_EPS, None, ALU.add).then_inc(s_x2, 1)

            def make_x2n(t):
                wait_tile(dve, s_r2, t)
                wait_before(dve, s_x2Tp, t)
                dve.tensor_scalar(x2n[:, :], xall[:, t.v, :], mv2[:, 0:1], r2[:, 0:1], ALU.subtract, ALU.mult)\
                   .then_inc(s_x2n, 1)

            def logits(t):
                wait_tile(dve, s_lgp, t)
                dve.tensor_copy(lg[:, t.v, :], pF[1][:, 0:E]).then_inc(s_lg, 1)

            def step(t, nxt, prev):
                if nxt:
                    ln1_stats(nxt)
                if prev:
                    o_sums(prev)
                if t:
                    start_t(t, 0)
                    start_t(t, 1)
                if nxt:
                    make_xn(nxt)
                if prev:
                    make_on(prev)
                for k in range(1, LEVELS + 1):
                    for hf in range(2):
                        if t:
                            update_t(t, k, hf)
                        if nxt and 2 <= k <= 4:
                            conv(nxt, k - 2, hf)
                        if k == 3 and hf == 1 and nxt:
                            betas(nxt)
                        if k == 4 and hf == 1 and prev:
                            make_x2(prev)
                        if k == 5 and hf == 0:
                            if nxt:
                                sums(nxt, 0)
                        if k == 5 and hf == 1:
                            if nxt:
                                sums(nxt, 1)
                                make_vb(nxt)
                            if prev:
                                make_x2n(prev)
                        if k == 6 and hf == 1 and prev:
                            logits(prev)
                if t:
                    make_r(t)
                    update_s(t)

            run_tiles(dve, step)


I = 352
IC = [P, P, I - 2 * P]
G, TOPG, K = 4, 2, 4
NE = E + 2


def routing(nc, es, lg, cw):
    V = NT * E

    def sb(name, shape):
        return es.enter_context(nc.sbuf_tensor(name, shape, F32))

    mx, sm = sb("mx", [P, NT]), sb("sm", [P, NT])
    z, sc = sb("z", [P, NT, E]), sb("sc", [P, NT, E])
    gs, grank, gsel = (sb(n, [P, NT, G]) for n in ("gs", "grank", "gsel"))
    rank, cmp_ = sb("rank", [P, NT, E]), sb("cmp", [P, NT, E])
    s_z, s_e, s_d = (es.enter_context(nc.semaphore(n)) for n in ("z_ready", "exp_done", "route_chain"))

    def over(ap, n):
        return ap.unsqueeze(2).to_broadcast([P, NT, n])

    with nc.Block() as block:
        @block.scalar
        def _(act):
            act.wait_ge(s_z, 1)
            act.activation(z[:, :, :], z[:, :, :], ACT.Exp).then_inc(s_e, 1)

        @block.vector
        def _(dve):
            n = [0]

            def link(ins):
                ins.then_inc(s_d, 1)
                n[0] += 1
                dve.wait_ge(s_d, n[0])

            def ranks(dst, v, count):
                link(dve.memset(dst, 0.0))
                for j in range(count):
                    one = v[:, :, j:j + 1]
                    tmp = cmp_[:, :, 0:count]
                    ins = dve.tensor_tensor(tmp[:, :, 0:j + 1], one.to_broadcast([P, NT, j + 1]),
                                            v[:, :, 0:j + 1], ALU.is_gt)
                    if j + 1 < count:
                        ins.then_inc(s_d, 1)
                        n[0] += 1
                        ins = dve.tensor_tensor(tmp[:, :, j + 1:], one.to_broadcast([P, NT, count - 1 - j]),
                                                v[:, :, j + 1:], ALU.is_ge)
                    link(ins)
                    link(dve.tensor_tensor(dst, dst, tmp, ALU.add))

            link(dve.tensor_reduce(mx[:, :], lg[:, :, :], AX.X, ALU.max))
            dve.tensor_tensor(z[:, :, :], lg[:, :, :], over(mx[:, :], E), ALU.subtract).then_inc(s_z, 1)
            dve.wait_ge(s_e, 1)
            link(dve.tensor_reduce(sm[:, :], z[:, :, :], AX.X, ALU.add))
            link(dve.reciprocal(sm[:, :], sm[:, :]))
            link(dve.tensor_tensor(sc[:, :, :], z[:, :, :], over(sm[:, :], E), ALU.mult))
            link(dve.tensor_reduce(gs[:, :, :], sc[:, :, :].rearrange("p t (g e) -> p t g e", g=G), AX.X, ALU.max))
            ranks(grank[:, :, :], gs, G)
            link(dve.tensor_scalar(gsel[:, :, :], grank[:, :, :], float(TOPG), None, ALU.is_lt))
            link(dve.tensor_tensor(sc[:, :, :].rearrange("p t (g e) -> p t g e", g=G),
                                   sc[:, :, :].rearrange("p t (g e) -> p t g e", g=G),
                                   gsel[:, :, :].unsqueeze(3).to_broadcast([P, NT, G, E // G]), ALU.mult))
            ranks(rank[:, :, :], sc, E)
            link(dve.tensor_scalar(rank[:, :, :], rank[:, :, :], float(K), None, ALU.is_lt))
            link(dve.tensor_tensor(sc[:, :, :], sc[:, :, :], rank[:, :, :], ALU.mult))
            link(dve.tensor_reduce(sm[:, :], sc[:, :, :], AX.X, ALU.add))
            link(dve.tensor_scalar(sm[:, :], sm[:, :], 1e-20, None, ALU.add))
            link(dve.reciprocal(sm[:, :], sm[:, :]))
            link(dve.tensor_tensor(cw[:, :, 0:E], sc[:, :, :], over(sm[:, :], E), ALU.mult))
            link(dve.memset(cw[:, :, E:NE], 1.0))


def experts(nc, es, wup_d, wdn_d, xall, x2nT, cw, out):
    N = 512
    NG = T // N
    TPG = N // P

    def sb(name, shape):
        return es.enter_context(nc.sbuf_tensor(name, shape, F32))

    wup = [sb(f"wup{i}", [P, DC, 2 * I]) for i in range(2)]
    wdn = [sb(f"wdn{i}", [P, len(IC), D]) for i in range(2)]
    sg = [sb(f"sg{i}", [P, N]) for i in range(2)]
    act_in = [sb(f"a{i}", [P, len(IC), N]) for i in range(2)]
    bank = lambda n: es.enter_context(nc.psum_tensor(n, [P, N], F32))
    pG, pU = [bank(f"pG{i}") for i in range(2)], [bank(f"pU{i}") for i in range(2)]
    pD = [bank(f"pD{i}") for i in range(TPG)]
    s_w = [es.enter_context(nc.semaphore(f"weights_loaded{i}")) for i in range(2)]
    s_up, s_sg, s_a, s_dn, s_acc, s_out = (es.enter_context(nc.semaphore(n)) for n in (
        "up_psum", "silu_done2", "a_ready", "down_psum", "acc_done", "out_stored"))
    UPS, DNS = NG * len(IC), NG * TPG

    def each(eng, body):
        body(0, 0)
        body(1, 1)
        with eng.Fori(1, NE // 2) as pair:
            body(2 * pair, 0)
            body(2 * pair + 1, 1)

    def wait_count(eng, sem, e, per_expert, n):
        if isinstance(e, int):
            if e * per_expert + n > 0:
                eng.wait_ge(sem, e * per_expert + n)
        else:
            eng.wait_ge(sem, e * per_expert + n)

    with nc.Block() as block:
        @block.sync
        def _(sp):
            def load(e, par):
                wait_count(sp, s_dn, e, DNS, -DNS)
                sp.dma_start(wup[par][:, :, :], wup_d[e].rearrange("(c p) n -> p c n", p=P)).then_inc(s_w[par], 16)
                sp.dma_start(wdn[par][:, 0:2, :], wdn_d[e, 0:2 * P, :].rearrange("(c p) n -> p c n", p=P))\
                    .then_inc(s_w[par], 16)
                sp.dma_start(wdn[par][0:IC[2], 2, :], wdn_d[e, 2 * P:I, :]).then_inc(s_w[par], 16)

            each(sp, load)
            ov = out.rearrange("b (t p) d -> p (b t) d", p=P)
            for g in range(NG):
                sp.wait_ge(s_acc, (NE - 1) * DNS + (g + 1) * TPG)
                sp.dma_start(ov[:, TPG * g:TPG * g + TPG, :], xall[:, TPG * g:TPG * g + TPG, :]).then_inc(s_out, 16)
            sp.wait_ge(s_out, 16 * NG)

        @block.scalar
        def _(act):
            def body(e, par):
                for u in range(UPS):
                    m = IC[u % 3]
                    wait_count(act, s_a, e, UPS, u - 1)
                    wait_count(act, s_up, e, UPS, u + 1)
                    act.activation(sg[u % 2][0:m, :], pG[u % 2][0:m, :], ACT.Silu).then_inc(s_sg, 1)

            each(act, body)

        @block.vector
        def _(dve):
            def body(e, par):
                def gated(g):
                    for c in range(3):
                        u, m = 3 * g + c, IC[c]
                        if c == 0:
                            wait_count(dve, s_dn, e, DNS, TPG * (g - 1))
                        wait_count(dve, s_sg, e, UPS, u + 1)
                        dve.tensor_tensor(act_in[g % 2][0:m, c, :], sg[u % 2][0:m, :], pU[u % 2][0:m, :], ALU.mult)\
                           .then_inc(s_a, 1)

                def accumulate(g):
                    for i in range(TPG):
                        j = TPG * g + i
                        wait_count(dve, s_acc, e, DNS, j + 1 - DNS)
                        wait_count(dve, s_dn, e, DNS, j + 1)
                        dve.scalar_tensor_tensor(out=xall[:, j, :], in0=pD[i][:, :], scalar=cw[:, j, bass.ds(e, 1)],
                                                 in1=xall[:, j, :], op0=ALU.mult, op1=ALU.add).then_inc(s_acc, 1)

                gated(0)
                for g in range(1, NG):
                    gated(g)
                    accumulate(g - 1)
                accumulate(NG - 1)

            each(dve, body)

        @block.tensor
        def _(pe):
            def body(e, par):
                def up(g):
                    for c in range(3):
                        u, m = 3 * g + c, IC[c]
                        wait_count(pe, s_a, e, UPS, u - 1)
                        for p, off in ((pG[u % 2], 0), (pU[u % 2], I)):
                            for k in range(DC):
                                mm = pe.matmul(p[0:m, :], wup[par][:, k, off + P * c:off + P * c + m],
                                               x2nT[:, k, N * g:N * g + N], start=(k == 0), stop=(k == DC - 1))
                        mm.then_inc(s_up, 1)

                def down(g):
                    wait_count(pe, s_a, e, UPS, 3 * (g + 1))
                    for i in range(TPG):
                        wait_count(pe, s_acc, e, DNS, TPG * (g - 1) + i + 1)
                        for c in range(3):
                            m = IC[c]
                            mm = pe.matmul(pD[i][:, :], act_in[g % 2][0:m, c, P * i:P * i + P],
                                           wdn[par][0:m, c, :], start=(c == 0), stop=(c == 2))
                        mm.then_inc(s_dn, 1)

                if isinstance(e, int):
                    pe.wait_ge(s_w[par], 48)
                else:
                    pe.wait_ge(s_w[par], (e - par) * 24 + 48)
                up(0)
                for g in range(1, NG):
                    up(g)
                    down(g - 1)
                down(NG - 1)

            each(pe, body)


def program(nc, x, wq, wk, wv, wb, cq, ck, cv, nw, wo, gw, wup, wdn, out):
    with ExitStack() as es:
        xall = es.enter_context(nc.sbuf_tensor("xall", [P, NT, D], F32))
        x2nT = es.enter_context(nc.sbuf_tensor("x2nT", [P, DC, T], F32))
        lg = es.enter_context(nc.sbuf_tensor("lg", [P, NT, E], F32))
        cw = es.enter_context(nc.sbuf_tensor("cw_all", [P, NT, NE], F32))
        with ExitStack() as inner:
            attention(nc, inner, x, wq, wk, wv, wb, cq, ck, cv, nw, wo, gw, xall, x2nT, lg)
        with ExitStack() as inner:
            routing(nc, inner, lg, cw)
        with ExitStack() as inner:
            experts(nc, inner, wup, wdn, xall, x2nT, cw, out)


_INS = ['L0_attn_hidden_states', 'L0_attn_Wq', 'L0_attn_Wk', 'L0_attn_Wv', 'L0_attn_Wb', 'L0_attn_conv_q',
        'L0_attn_conv_k', 'L0_attn_conv_v', 'L0_attn_norm_w', 'L0_attn_Wo']


def kernel(**inputs):
    import numpy as np
    import concourse.bacc as bacc
    from concourse.bass_utils import run_bass_kernel_spmd

    nc = bacc.Bacc("TRN2", target_bir_lowering=False, num_devices=1)
    laid = {n: np.asarray(inputs[n]) for n in _INS}
    laid['gate_T'] = np.asarray(inputs['L0_ffn_gate_w']).T
    up, down = np.asarray(inputs['L0_ffn_expert_up_w']), np.asarray(inputs['L0_ffn_expert_down_w'])
    sup, sdown = np.asarray(inputs['L0_ffn_shared_up_w']), np.asarray(inputs['L0_ffn_shared_down_w'])
    halves = sup.reshape(2, 2, I, D).transpose(1, 0, 2, 3).reshape(2, 2 * I, D)
    laid['up_T'] = np.concatenate([up, halves]).transpose(0, 2, 1)
    laid['down_T'] = np.concatenate([down.transpose(0, 2, 1), sdown.T.reshape(2, I, D)])
    arrays, args = {}, []
    for n, a in laid.items():
        a = np.ascontiguousarray(a)
        arrays[f"in_{n}"] = a
        args.append(nc.dram_tensor(f"in_{n}", a.shape, mybir.dt.from_np(a.dtype), kind="ExternalInput").ap())
    args.append(nc.dram_tensor("out_0", (1, T, D), F32, kind="ExternalOutput").ap())
    program(nc, *args)
    r = run_bass_kernel_spmd(nc, [arrays], core_ids=[0])
    return r.results[0]["out_0"]
```

```python
from contextlib import ExitStack

import concourse.bass as bass
from concourse import mybir

F32 = mybir.dt.float32
I32 = mybir.dt.int32
ALU = mybir.AluOpType
ACT = mybir.ActivationFunctionType
AX = mybir.AxisListType

P = 128
T, D = 2048, 512
H, DH = 8, 64
NT = T // P
DC = D // P
HH = H // 2
TAPS = 4
HALO = TAPS - 1
LEVELS = 6
E = 16
LN_EPS, L2_EPS, RMS_EPS = 1e-5, 1e-6, 1e-5


T_STARTS = 4
T_UPDATES = 4 * (LEVELS - 1) + 2


def t_updates(k, hf):
    return 4 * (k - 1) + (2 * hf + 2 if k < LEVELS else hf + 1)


class Tile:

    def __init__(self, v, par):
        self.v, self.par = v, par


def wait_tile(eng, sem, tile, per_tile=1, k=None):
    k = per_tile if k is None else k
    eng.wait_ge(sem, tile.v * per_tile + k)


def wait_before(eng, sem, tile, per_tile=1, back=1):
    if isinstance(tile.v, int) and tile.v < back:
        return
    eng.wait_ge(sem, (tile.v - (back - 1)) * per_tile)


class Chain:

    def __init__(self, eng, sem, per_tile):
        self.eng, self.sem, self.n, self.k = eng, sem, per_tile, 0

    def begin(self, tile):
        assert self.k in (0, self.n), (self.k, self.n)
        self.tile, self.k = tile, 0
        self.started = not (isinstance(tile.v, int) and tile.v == 0)

    def done(self, ins):
        ins.then_inc(self.sem, 1)
        self.k += 1
        return self.k

    def wait(self, k=None):
        k = self.k if k is None else k
        if k or self.started:
            self.eng.wait_ge(self.sem, self.tile.v * self.n + k)


def run_tiles(eng, step):
    a, b = (lambda v: Tile(v, 0)), (lambda v: Tile(v, 1))
    step(None, a(0), None)
    step(a(0), b(1), None)
    step(b(1), a(2), a(0))
    with eng.Fori(2, NT - 2, 2) as i:
        step(a(i), b(i + 1), b(i - 1))
        step(b(i + 1), a(i + 2), a(i))
    step(a(NT - 2), b(NT - 1), b(NT - 3))
    step(b(NT - 1), None, a(NT - 2))
    step(None, None, b(NT - 1))


def attention(nc, es, x_d, wq_d, wk_d, wv_d, wb_d, cq_d, ck_d, cv_d, nw_d, wo_d, gw_d, xall, x2nT, lg, stat2, xs_d):

    def sb(name, shape, dt=F32):
        return es.enter_context(nc.sbuf_tensor(name, shape, dt))

    def sem(name):
        return es.enter_context(nc.semaphore(name))

    ident = sb("ident", [P, P])
    causal = sb("causal", [P, P])
    xor_i, xor_j = sb("xor_i", [P, P], I32), sb("xor_j", [P, P], I32)
    dist = sb("dist", [P, P])
    dist_lo, dist_up = sb("dist_lo", [P, P]), sb("dist_up", [P, P])
    ge_a, ge_b = sb("ge_a", [P, P]), sb("ge_b", [P, P])
    m_lo = sb("m_lo", [P, LEVELS, P], I32)
    m_up = sb("m_up", [P, LEVELS, P], I32)
    nhalf = sb("nhalf", [P, 16])
    w3 = sb("w3", [P, 3, DC, D])
    wb = sb("wb", [P, DC, H])
    cw = sb("cw", [P, 3 * DC, TAPS])
    nw = sb("nw", [P, 1])
    wo = sb("wo", [P, DC, D])
    gw = sb("gw", [P, DC, E])
    xn = sb("xn", [P, D])
    xnT = sb("xnT", [P, DC, P])
    st1, mv1, r1 = sb("st1", [P, 6]), sb("mv1", [P, 2]), sb("r1", [P, 1])
    ve1 = sb("ve1", [P, 1])
    raw = sb("raw", [P, 3 * DC, HALO + P])
    acc = sb("acc", [P, 3 * DC, P])
    sil = sb("sil", [P, 3 * DC, P])
    th, beta, nbeta = sb("th", [P, H]), sb("beta", [P, H]), sb("nbeta", [P, H])
    tok = sb("tok", [P, 2, D])
    sq = sb("sq", [P, 2, D])
    ss, rqk = sb("ss", [P, 2 * H]), sb("rqk", [P, 2 * H])
    qn = sb("qn", [P, D])
    kn = [sb(f"kn{i}", [P, D]) for i in range(2)]
    nkb = sb("nkb", [P, D])
    vb = [sb(f"vb{i}", [P, D]) for i in range(2)]
    QT, KT, KBT = ([sb(f"{n}{i}", [P, DC, P]) for i in range(2)] for n in ("QT", "KT", "KBT"))
    AT, Ti, TiT, Ys, PT = ([sb(f"{n}{i}", [P, HH, P]) for i in range(2)] for n in ("AT", "Ti", "TiT", "Ys", "PT"))
    S = sb("S", [P, HH * DH])
    R, U = sb("R", [P, 2, HH, DH]), sb("U", [P, 2, HH, DH])
    osb, osq, on = sb("osb", [P, D]), sb("osq", [P, D]), sb("on", [P, D])
    so, ro = sb("so", [P, H]), sb("ro", [P, H])
    oT = sb("oT", [P, DC, P])
    st2, mv2, r2, ve2 = sb("st2", [P, 6]), sb("mv2", [P, 2]), sb("r2", [P, 1]), sb("ve2", [P, 1])
    x2n = sb("x2n", [P, D])
    x2g = sb("x2g", [P, DC, P])
    zeros = sb("zeros", [P, D])

    def bank(name):
        return es.enter_context(nc.psum_tensor(name, [P, D], F32))

    pY, pZ, pZT = ([bank(f"{n}{i}") for i in range(2)] for n in ("pY", "pZ", "pZT"))
    pF = [bank(f"pF{i}") for i in range(2)]

    s_zero, s_zeroed, s_stat = sem("zeros_ready"), sem("slots_zeroed"), sem("stat2_kept")
    (s_xload, s_wload, s_wo, s_iota, s_const, s_masks, s_wos, s_S0,
     s_stats, s_r1, s_xn, s_xTp, s_xnT, s_proj, s_raw, s_conv, s_sil, s_bp, s_th, s_beta, s_nbeta,
     s_tokp, s_tok, s_sq, s_vb, s_ss, s_rqk, s_knorm, s_back, s_qkT,
     s_D1, s_AT, s_T0, s_PT, s_Y, s_Ys, s_Z, s_T, s_Rp, s_R, s_Up, s_U, s_Op, s_O, s_Sp, s_S,
     s_so, s_ro, s_on, s_oTp, s_oT, s_yp, s_x2, s_r2, s_x2n, s_x2Tp, s_x2nT, s_lgp, s_lg,
     c_dF, c_dD, c_dB, c_aF, c_init) = (sem(n) for n in (
        "x_loaded", "w_loaded", "wo_loaded", "iota_done", "const_done", "masks_done", "wo_scaled", "S_zeroed",
        "ln1_stats", "ln1_rstd", "xn_ready", "xnT_psum", "xnT_ready", "proj_psum", "raw_ready", "conv_done",
        "silu_done", "beta_psum", "tanh_done", "beta_ready", "nbeta_ready",
        "tok_psum", "tok_ready", "tok_squared", "vb_ready", "qk_sums", "qk_rnorm", "qk_normed", "back_psum", "qkT_ready",
        "gram_psum", "AT_ready", "T_started", "PT_ready", "Y_psum", "Y_ready", "Z_psum", "T_updated",
        "R_psum", "R_ready", "U_psum", "U_ready", "O_psum", "O_ready", "S_psum", "S_ready",
        "o_sums", "o_rnorm", "on_ready", "oT_psum", "oT_ready", "y_psum", "x2_ready", "ln2_rstd", "x2n_ready",
        "x2nT_psum", "x2nT_ready", "logit_psum", "logits_ready",
        "dve_front", "dve_delta", "dve_back", "act_front", "init_chain"))

    def heads(ap):
        return ap.rearrange("p (h d) -> p h d", d=DH)

    def mats(ap):
        return ap.rearrange("p (h n) -> p h n", n=P)

    def over_heads(ap):
        return ap.unsqueeze(2).to_broadcast([P, H, DH])

    def by_half(buf, hf):
        return buf[:, :].rearrange("p (n f d) -> p f n d", f=2, d=DH)[:, hf]

    def settle(eng):
        eng.nop(nofuse=True)
        eng.wait_ge(s_const, 5)

    def over_mats(ap):
        return ap.unsqueeze(1).to_broadcast([P, HH, P])

    with nc.Block() as block:

        @block.sync
        def _(sp):
            xv = x_d.rearrange("b (t p) d -> p (b t) d", p=P)
            for g in range(4):
                sp.dma_start(xall[:, 4 * g:4 * g + 4, :], xv[:, 4 * g:4 * g + 4, :]).then_inc(s_xload, 16)
                if g == 0:
                    for i, w in enumerate((wq_d, wk_d, wv_d)):
                        sp.dma_start(w3[:, i], w.rearrange("(c p) n -> p c n", p=P)).then_inc(s_wload, 16)
                    sp.dma_start(wb[:, :, :], wb_d.rearrange("(c p) n -> p c n", p=P)).then_inc(s_wload, 16)
                    for i, w in enumerate((cq_d, ck_d, cv_d)):
                        sp.dma_start(cw[:, DC * i:DC * i + DC, :], w.rearrange("(c p) n -> p c n", p=P))\
                          .then_inc(s_wload, 16)
            for i in range(2):
                sp.dma_start(nw[DH * i:DH * i + DH, :], nw_d.rearrange("(p o) -> p o", o=1)).then_inc(s_wo, 16)
            sp.dma_start(wo[:, :, :], wo_d.rearrange("(c p) n -> p c n", p=P)).then_inc(s_wo, 16)
            sp.dma_start(gw[:, :, :], gw_d.rearrange("(c p) n -> p c n", p=P)).then_inc(s_wo, 16)
            rows = xs_d.rearrange("(p r) d -> p r d", p=P)
            R4 = rows.shape[1] // 4
            sp.wait_ge(s_zero, 1)
            for i in range(4):
                sp.dma_start(rows[:, R4 * i:R4 * (i + 1), :], zeros[:, :].unsqueeze(1).to_broadcast([P, R4, D]))\
                  .then_inc(s_zeroed, 16)
            sp.wait_ge(s_zeroed, 16 * 4)

        @block.gpsimd
        def _(pool):
            pool.memset(ident[:, :], 0.0).then_inc(s_const, 1)
            pool.memset(causal[:, :], 1.0).then_inc(s_const, 1)
            pool.memset(nhalf[:, :], -0.5).then_inc(s_const, 1)
            pool.iota(xor_i[:, :], pattern=[[0, P]], base=0, channel_multiplier=1).then_inc(s_iota, 1)
            pool.iota(xor_j[:, :], pattern=[[1, P]], base=0, channel_multiplier=0).then_inc(s_iota, 1)
            pool.wait_ge(s_const, 3)
            pool.affine_select(out=ident[:, :], in_=ident[:, :], compare_op=ALU.not_equal, fill=1.0,
                               base=0, pattern=[[-1, P]], channel_multiplier=1).then_inc(s_const, 1)
            pool.affine_select(out=causal[:, :], in_=causal[:, :], compare_op=ALU.is_ge, fill=0.0,
                               base=0, pattern=[[1, P]], channel_multiplier=-1).then_inc(s_const, 1)
            pool.wait_ge(s_masks, 2)
            pool.affine_select(out=dist_lo[:, :], in_=dist[:, :], compare_op=ALU.is_gt, fill=0.0,
                               base=0, pattern=[[-1, P]], channel_multiplier=1).then_inc(s_const, 1)
            pool.affine_select(out=dist_up[:, :], in_=dist[:, :], compare_op=ALU.is_gt, fill=0.0,
                               base=0, pattern=[[1, P]], channel_multiplier=-1).then_inc(s_const, 1)

            def rstd1(t):
                wait_tile(pool, s_stats, t)
                wait_before(pool, s_xn, t)
                pool.tensor_tensor(r1[:, :], ve1[:, :], nhalf[:, 0:1], ALU.pow).then_inc(s_r1, 1)

            def qk_norms(t):
                wait_tile(pool, s_ss, t, 2)
                wait_before(pool, s_knorm, t, 3)
                pool.tensor_tensor(rqk[:, :], ss[:, :], nhalf[:, :], ALU.pow).then_inc(s_rqk, 1)
                wait_tile(pool, s_rqk, t)
                wait_tile(pool, s_beta, t)
                wait_before(pool, s_back, t, 3)
                wait_before(pool, s_Sp, t, back=2)
                pool.tensor_tensor(heads(qn[:, :]), heads(tok[:, 0, :]), over_heads(rqk[:, 0:H]), ALU.mult)\
                    .then_inc(s_knorm, 1)
                pool.tensor_tensor(heads(kn[t.par][:, :]), heads(tok[:, 1, :]), over_heads(rqk[:, H:2 * H]), ALU.mult)\
                    .then_inc(s_knorm, 1)
                wait_tile(pool, s_knorm, t, 3, 2)
                pool.tensor_tensor(heads(nkb[:, :]), heads(kn[t.par][:, :]), over_heads(nbeta[:, :]), ALU.mult)\
                    .then_inc(s_knorm, 1)

            def o_rnorm(t):
                wait_tile(pool, s_so, t)
                wait_before(pool, s_on, t)
                pool.tensor_tensor(ro[:, :], so[:, :], nhalf[:, 0:H], ALU.pow).then_inc(s_ro, 1)

            def rstd2(t):
                wait_tile(pool, s_x2, t, 2)
                wait_before(pool, s_stat, t, 2)
                pool.tensor_tensor(r2[:, :], ve2[:, :], nhalf[:, 0:1], ALU.pow).then_inc(s_r2, 1)

            def step(t, nxt, prev):
                if nxt:
                    rstd1(nxt)
                if prev:
                    o_rnorm(prev)
                    rstd2(prev)
                if nxt:
                    qk_norms(nxt)

            run_tiles(pool, step)

        @block.scalar
        def _(act):
            cf = Chain(act, c_aF, 3)

            def xT_copy(t):
                wait_tile(act, s_xTp, t)
                wait_before(act, s_bp, t)
                act.activation(xnT[:, :, :], mats(pF[0][:, :]), ACT.Copy).then_inc(s_xnT, 1)

            def raw_copy(t, i):
                if i == 0:
                    cf.begin(t)
                sec = slice(DC * i, DC * i + DC)
                if isinstance(t.v, int) and t.v == 0:
                    act.wait_ge(s_S0, 2)
                    cf.done(act.activation(raw[:, sec, 0:HALO], raw[:, sec, P:P + HALO], ACT.Copy))
                else:
                    wait_before(act, s_conv, t, 3 * 4)
                    cf.done(act.activation(raw[:, sec, 0:HALO], raw[:, sec, P:P + HALO], ACT.Copy))
                cf.wait()
                wait_tile(act, s_proj, t, 3, i + 1)
                act.activation(raw[:, sec, HALO:], mats(pF[(i + 1) % 2][:, :]), ACT.Copy).then_inc(s_raw, 1)

            def silu(t, i):
                sec = slice(DC * i, DC * i + DC)
                wait_tile(act, s_conv, t, 3 * 4, 4 * i + 4)
                wait_before(act, s_tokp, t, 3)
                act.activation(sil[:, sec, :], acc[:, sec, :], ACT.Silu).then_inc(s_sil, 1)

            def tanh(t):
                wait_tile(act, s_bp, t)
                wait_before(act, s_beta, t)
                act.activation(th[:, :], pF[0][:, 0:H], ACT.Tanh, scale=0.5).then_inc(s_th, 1)

            def tok_copy(t, i):
                wait_tile(act, s_tokp, t, 3, i + 1)
                wait_before(act, s_knorm, t, 3)
                act.activation(tok[:, i, :], pF[(1, 0)[i]][:, :], ACT.Copy).then_inc(s_tok, 1)
                wait_before(act, s_ss, t, 2)
                act.activation(sq[:, i, :], pF[(1, 0)[i]][:, :], ACT.Square).then_inc(s_sq, 1)

            def back_copy(t, i):
                dst = (QT, KT, KBT)[i][t.par]
                wait_tile(act, s_back, t, 3, i + 1)
                wait_before(act, s_Op, t, back=2)
                act.activation(dst[:, :, :], mats(pF[i % 2][:, :]), ACT.Copy,
                               scale=DH ** -0.5 if i == 0 else 1.0).then_inc(s_qkT, 1)

            def at_copy(t, hf):
                wait_tile(act, s_D1, t, 2, hf + 1)
                wait_before(act, s_Z, t, 12)
                wait_before(act, s_T0, t, T_STARTS)
                act.activation(AT[hf][:, :, :], mats(pZ[hf][:, :]), ACT.Copy).then_inc(s_AT, 1)

            def y_copy(t, k, hf):
                wait_tile(act, s_Y, t, 2 * LEVELS, 2 * k - 1 + hf)
                if k > 1:
                    wait_tile(act, s_Z, t, 2 * LEVELS, 2 * k - 3 + hf)
                else:
                    wait_before(act, s_Z, t, 2 * LEVELS)
                if k < LEVELS:
                    act.activation(Ys[hf][:, :, :], mats(pY[hf][:, :]), ACT.Copy).then_inc(s_Ys, 1)
                else:
                    act.activation(Ys[hf][DH:P, :, 0:DH], mats(pY[hf][DH:P, :])[:, :, 0:DH], ACT.Copy)\
                       .then_inc(s_Ys, 1)

            def u_copy(t):
                wait_tile(act, s_Up, t)
                wait_before(act, s_Sp, t)
                act.activation(U[:, :, :, :], pZT[0][:, :].rearrange("p (f n d) -> p f n d", f=2, d=DH), ACT.Copy)\
                   .then_inc(s_U, 1)

            def o_copy(t):
                wait_tile(act, s_Op, t)
                wait_before(act, s_on, t)
                for hf in range(2):
                    o = heads(pZ[hf][:, 0:HH * DH])
                    act.activation(by_half(osb, hf), o, ACT.Copy).then_inc(s_O, 1)
                    act.activation(by_half(osq, hf), o, ACT.Square).then_inc(s_O, 1)

            def oT_copy(t):
                wait_tile(act, s_oTp, t)
                wait_before(act, s_yp, t)
                act.activation(oT[:, :, :], mats(pF[1][:, :]), ACT.Copy).then_inc(s_oT, 1)

            def x2T_copy(t):
                wait_tile(act, s_x2Tp, t)
                wait_before(act, s_lgp, t)
                act.activation(x2g[:, :, :], mats(pF[0][:, :]), ACT.Copy).then_inc(s_x2nT, 1)
                act.activation(x2nT[:, :, bass.ts(t.v, P)], mats(pF[0][:, :]), ACT.Copy).then_inc(s_x2nT, 1)

            def step(t, nxt, prev):
                if t:
                    at_copy(t, 0)
                    at_copy(t, 1)
                for k in range(1, LEVELS + 1):
                    if t:
                        y_copy(t, k, 0)
                        y_copy(t, k, 1)
                    if nxt:
                        if k == 1:
                            xT_copy(nxt)
                            raw_copy(nxt, 0)
                        elif k == 2:
                            raw_copy(nxt, 1)
                            raw_copy(nxt, 2)
                        elif k == 3:
                            tanh(nxt)
                            silu(nxt, 0)
                        elif k == 4:
                            silu(nxt, 1)
                            tok_copy(nxt, 0)
                        elif k == 5:
                            silu(nxt, 2)
                            tok_copy(nxt, 1)
                    if prev:
                        if k == 3:
                            oT_copy(prev)
                        elif k == 6:
                            x2T_copy(prev)
                if t:
                    u_copy(t)
                    o_copy(t)
                if nxt:
                    for i in range(3):
                        back_copy(nxt, i)

            run_tiles(act, step)

        @block.tensor
        def _(pe):
            def xT(t):
                wait_tile(pe, s_xn, t)
                wait_before(pe, s_qkT, t, 3)
                for c in range(DC):
                    mm = pe.transpose(pF[0][:, c * P:(c + 1) * P], xn[:, c * P:(c + 1) * P], ident[:, :])
                mm.then_inc(s_xTp, 1)

            def project(t, i):
                if i == 0:
                    wait_tile(pe, s_xnT, t)
                if i == 2:
                    wait_tile(pe, s_raw, t, 3, 1)
                if i == 1:
                    wait_tile(pe, s_xnT, t)
                for c in range(DC):
                    for k in range(DC):
                        mm = pe.matmul(pF[(i + 1) % 2][:, c * P:(c + 1) * P], w3[:, i, k, c * P:(c + 1) * P],
                                       xnT[:, k, :], start=(k == 0), stop=(k == DC - 1))
                mm.then_inc(s_proj, 1)

            def betas(t):
                wait_tile(pe, s_raw, t, 3, 2)
                for k in range(DC):
                    mm = pe.matmul(pF[0][:, 0:H], xnT[:, k, :], wb[:, k, :], start=(k == 0), stop=(k == DC - 1))
                mm.then_inc(s_bp, 1)

            def to_tokens(t, i):
                wait_tile(pe, s_sil, t, 3, i + 1)
                if i == 0:
                    wait_tile(pe, s_raw, t, 3, 3)
                elif i == 1:
                    wait_tile(pe, s_th, t)
                else:
                    wait_tile(pe, s_sq, t, 2, 1)
                for c in range(DC):
                    mm = pe.transpose(pF[(1, 0, 1)[i]][:, c * P:(c + 1) * P], sil[:, DC * i + c, :], ident[:, :])
                mm.then_inc(s_tokp, 1)

            def to_channels(t, i):
                src = (qn, kn[t.par], nkb)[i]
                wait_tile(pe, s_knorm, t, 3, i + 1)
                if i == 0:
                    wait_tile(pe, s_sq, t, 2, 2)
                elif i == 1:
                    wait_tile(pe, s_vb, t)
                else:
                    wait_tile(pe, s_qkT, t, 3, 1)
                for c in range(DC):
                    mm = pe.transpose(pF[i % 2][:, c * P:(c + 1) * P], src[:, c * P:(c + 1) * P], ident[:, :])
                mm.then_inc(s_back, 1)

            def gram(t, hf):
                if hf == 0:
                    wait_tile(pe, s_qkT, t, 3)
                    wait_before(pe, s_O, t, 4)
                    wait_before(pe, s_S, t)
                q, k, kb = QT[t.par], KT[t.par], KBT[t.par]
                for n in range(HH):
                    rows, cols = slice(DH * hf, DH * hf + DH), slice(n * P, (n + 1) * P)
                    pe.matmul(pZ[hf][:, cols], k[rows, n, :], kb[rows, n, :], start=True, stop=True)
                    pe.matmul(pY[hf][:, cols], kb[rows, n, :], k[rows, n, :], start=True, stop=True)
                    mm = pe.matmul(pZT[hf][:, cols], k[rows, n, :], q[rows, n, :], start=True, stop=True)
                mm.then_inc(s_D1, 1)

            def level_y(t, k, hf):
                if k == 1:
                    wait_tile(pe, s_AT, t, 2, hf + 1)
                    wait_tile(pe, s_T0, t, T_STARTS, 2 * hf + 2)
                else:
                    wait_tile(pe, s_Ys, t, 2 * LEVELS, 2 * k - 3 + hf)
                    wait_tile(pe, s_T, t, T_UPDATES, t_updates(k - 1, hf))
                if k == LEVELS:
                    settle(pe)
                for n in range(HH):
                    if k < LEVELS:
                        mm = pe.matmul(pY[hf][:, n * P:(n + 1) * P], AT[hf][:, n, :], Ti[hf][:, n, :],
                                       start=True, stop=True)
                    else:
                        mm = pe.matmul(pY[hf][DH:P, n * P:n * P + DH], AT[hf][0:DH, n, DH:P], Ti[hf][0:DH, n, 0:DH],
                                       start=True, stop=True)
                mm.then_inc(s_Y, 1)

            def level_z(t, k, hf):
                wait_tile(pe, s_Ys, t, 2 * LEVELS, 2 * k - 1 + hf)
                if k == 1:
                    wait_tile(pe, s_PT, t, 2, hf + 1)
                if k == LEVELS:
                    settle(pe)
                for n in range(HH):
                    cols = slice(n * P, (n + 1) * P)
                    if k < LEVELS:
                        pe.matmul(pZ[hf][:, cols], TiT[hf][:, n, :], Ys[hf][:, n, :], start=True, stop=True)
                        mm = pe.matmul(pZT[hf][:, cols], Ys[hf][:, n, :], TiT[hf][:, n, :], start=True, stop=True)
                    else:
                        mm = pe.matmul(pZT[hf][0:DH, n * P + DH:(n + 1) * P], Ys[hf][DH:P, n, 0:DH],
                                       TiT[hf][DH:P, n, DH:P], start=True, stop=True)
                mm.then_inc(s_Z, 1)

            def state_out(t):
                wait_tile(pe, s_Ys, t, 2 * LEVELS)
                if isinstance(t.v, int) and t.v == 0:
                    pe.wait_ge(s_S0, 1)
                else:
                    wait_before(pe, s_S, t)
                for hf in range(2):
                    rows = slice(DH * hf, DH * hf + DH)
                    for n in range(HH):
                        mm = pe.matmul(pY[hf][:, n * DH:(n + 1) * DH], KBT[t.par][rows, n, :],
                                       S[rows, n * DH:(n + 1) * DH], start=True, stop=True)
                    mm.then_inc(s_Rp, 1)

            def solve(t):
                wait_tile(pe, s_T, t, T_UPDATES)
                for hf in range(2):
                    wait_tile(pe, s_R, t, 2, hf + 1)
                    for n in range(HH):
                        mm = pe.matmul(pZT[0][:, (HH * hf + n) * DH:(HH * hf + n + 1) * DH], TiT[hf][:, n, :],
                                       R[:, hf, n, :], start=True, stop=True)
                mm.then_inc(s_Up, 1)

            def outputs(t):
                wait_tile(pe, s_U, t)
                for hf in range(2):
                    rows = slice(DH * hf, DH * hf + DH)
                    for n in range(HH):
                        o = pZ[hf][:, n * DH:(n + 1) * DH]
                        pe.matmul(o, QT[t.par][rows, n, :], S[rows, n * DH:(n + 1) * DH], start=True, stop=False)
                        mm = pe.matmul(o, PT[hf][:, n, :], U[:, hf, n, :], start=False, stop=True)
                mm.then_inc(s_Op, 1)
                for hf in range(2):
                    rows = slice(DH * hf, DH * hf + DH)
                    for n in range(HH):
                        h = 2 * n + hf
                        mm = pe.matmul(pZT[1][rows, n * DH:(n + 1) * DH], kn[t.par][:, h * DH:(h + 1) * DH],
                                       U[:, hf, n, :], start=True, stop=True)
                mm.then_inc(s_Sp, 1)

            def oT_turn(t, nxt):
                wait_tile(pe, s_on, t)
                wait_before(pe, s_lg, t)
                if nxt:
                    wait_tile(pe, s_raw, nxt, 3, 3)
                for c in range(DC):
                    mm = pe.transpose(pF[1][:, c * P:(c + 1) * P], on[:, c * P:(c + 1) * P], ident[:, :])
                mm.then_inc(s_oTp, 1)

            def out_proj(t, nxt):
                wait_tile(pe, s_oT, t)
                if isinstance(t.v, int) and t.v == 0:
                    pe.wait_ge(s_wos, DC)
                wait_before(pe, s_x2nT, t, 2)
                if nxt:
                    wait_tile(pe, s_th, nxt)
                for k in range(DC):
                    mm = pe.matmul(pF[0][:, :], oT[:, k, :], wo[:, k, :], start=(k == 0), stop=(k == DC - 1))
                mm.then_inc(s_yp, 1)

            def x2T(t, nxt):
                wait_tile(pe, s_x2n, t)
                if nxt:
                    wait_tile(pe, s_sq, nxt, 2, 2)
                for c in range(DC):
                    mm = pe.transpose(pF[0][:, c * P:(c + 1) * P], x2n[:, c * P:(c + 1) * P], ident[:, :])
                mm.then_inc(s_x2Tp, 1)

            def gate(t, nxt):
                wait_tile(pe, s_x2nT, t, 2, 1)
                if nxt:
                    wait_tile(pe, s_vb, nxt)
                for k in range(DC):
                    mm = pe.matmul(pF[1][:, 0:E], x2g[:, k, :], gw[:, k, :], start=(k == 0), stop=(k == DC - 1))
                mm.then_inc(s_lgp, 1)

            pe.wait_ge(s_wload, 7 * 16)
            pe.wait_ge(s_const, 5)

            def step(t, nxt, prev):
                if t:
                    gram(t, 0)
                    gram(t, 1)
                for k in range(1, LEVELS + 1):
                    if t:
                        level_y(t, k, 0)
                        level_y(t, k, 1)
                        level_z(t, k, 0)
                    if k == 1 and nxt:
                        xT(nxt)
                    if k == 2 and nxt:
                        project(nxt, 1)
                    if k == 3 and nxt:
                        betas(nxt)
                    if k == 4:
                        if prev:
                            out_proj(prev, nxt)
                    if k == 5 and nxt:
                        to_tokens_k(nxt, prev)
                    if k == 6 and prev:
                        x2T(prev, nxt)
                    if t:
                        level_z(t, k, 1)
                    if k == 1 and nxt:
                        project(nxt, 0)
                    if k == 2 and nxt:
                        project(nxt, 2)
                    if k == 3 and prev:
                        oT_turn(prev, nxt)
                    if k == 4 and nxt:
                        to_tokens_q(nxt, prev)
                    if k == 5 and nxt:
                        to_tokens(nxt, 2)
                    if k == 6 and prev:
                        gate(prev, nxt)
                if t:
                    state_out(t)
                    solve(t)
                    outputs(t)
                if nxt:
                    for i in range(3):
                        if i == 0 and prev:
                            wait_tile(pe, s_x2nT, prev, 2)
                        if i == 1 and prev:
                            wait_tile(pe, s_lg, prev)
                        to_channels(nxt, i)

            def to_tokens_q(nxt, prev):
                if prev:
                    wait_tile(pe, s_oT, prev)
                to_tokens(nxt, 0)

            def to_tokens_k(nxt, prev):
                if prev:
                    wait_tile(pe, s_x2, prev, 2, 1)
                to_tokens(nxt, 1)

            run_tiles(pe, step)

        @block.vector
        def _(dve):
            fr, de, ba = Chain(dve, c_dF, 2 + 6 * 6 + 2), Chain(dve, c_dD, 4), Chain(dve, c_dB, 3)

            dve.memset(S[:, :], 0.0).then_inc(s_S0, 1)
            dve.memset(raw[:, :, P:P + HALO], 0.0).then_inc(s_S0, 1)
            dve.memset(zeros[:, :], 0.0).then_inc(s_zero, 1)
            dve.wait_ge(s_iota, 2)
            dve.tensor_tensor(xor_j[:, :], xor_i[:, :], xor_j[:, :], ALU.bitwise_xor).then_inc(s_masks, 1)
            dve.wait_ge(s_masks, 1)
            dve.tensor_copy(dist[:, :], xor_j[:, :]).then_inc(s_masks, 1)
            dve.wait_ge(s_const, 7)
            n = 0
            for src, dst in ((dist_lo, m_lo), (dist_up, m_up)):
                for k in range(LEVELS):
                    if n:
                        dve.wait_ge(c_init, n)
                    dve.tensor_scalar(ge_a[:, :], src[:, :], float(2 ** k), None, ALU.is_ge).then_inc(c_init, 1)
                    dve.tensor_scalar(ge_b[:, :], src[:, :], float(2 ** (k + 1)), None, ALU.is_ge).then_inc(c_init, 1)
                    n += 2
                    dve.wait_ge(c_init, n)
                    dve.tensor_tensor(dst[:, k, :], ge_a[:, :], ge_b[:, :], ALU.subtract).then_inc(c_init, 1)
                    n += 1
            dve.wait_ge(c_init, n)
            dve.wait_ge(s_wload, 7 * 16)
            dve.wait_ge(s_wo, 4 * 16)
            for c in range(DC):
                dve.tensor_scalar(wo[:, c, :], wo[:, c, :], nw[:, 0:1], None, ALU.mult).then_inc(s_wos, 1)

            def ln1_stats(t):
                fr.begin(t)
                if isinstance(t.v, int) and t.v < 2:
                    dve.wait_ge(s_xload, 16 if t.v == 0 else 4 * 16)
                fr.wait(0)
                wait_before(dve, s_xn, t)
                settle(dve)
                a = fr.done(dve.bn_stats(st1[:, :], xall[:, t.v, :]))
                fr.wait(a)
                settle(dve)
                b = fr.done(dve.bn_aggr(mv1[:, :], st1[:, :]))
                fr.wait(b)
                wait_before(dve, s_r1, t)
                dve.tensor_scalar(ve1[:, :], mv1[:, 1:2], LN_EPS, None, ALU.add).then_inc(s_stats, 1)

            def make_xn(t):
                wait_tile(dve, s_r1, t)
                wait_before(dve, s_xTp, t)
                dve.tensor_scalar(xn[:, :], xall[:, t.v, :], mv1[:, 0:1], r1[:, 0:1], ALU.subtract, ALU.mult)\
                   .then_inc(s_xn, 1)

            def conv(t, i, half):
                if half == 0:
                    wait_tile(dve, s_raw, t, 3, i + 1)
                    wait_before(dve, s_sil, t, 3)
                cs = [DC * i + 2 * half, DC * i + 2 * half + 1]
                last = {}
                for c in cs:
                    last[c] = fr.done(dve.tensor_scalar(acc[:, c, :], raw[:, c, HALO:HALO + P],
                                                        cw[:, c, TAPS - 1:TAPS], None, ALU.mult))
                for j in range(TAPS - 1):
                    for c in cs:
                        fr.wait(last[c])
                        ins = dve.scalar_tensor_tensor(out=acc[:, c, :], in0=raw[:, c, j:j + P],
                                                       scalar=cw[:, c, j:j + 1], in1=acc[:, c, :],
                                                       op0=ALU.mult, op1=ALU.add)
                        if j < TAPS - 2:
                            last[c] = fr.done(ins)
                        else:
                            ins.then_inc(s_conv, 1)

            def betas(t):
                wait_tile(dve, s_th, t)
                wait_before(dve, s_knorm, t, 3)
                wait_before(dve, s_vb, t)
                dve.tensor_scalar(nbeta[:, :], th[:, :], -0.5, -0.5, ALU.mult, ALU.add)\
                   .then_inc(s_nbeta, 1)
                dve.tensor_scalar(beta[:, :], th[:, :], 0.5, 0.5, ALU.mult, ALU.add).then_inc(s_beta, 1)

            def sums(t, i):
                wait_tile(dve, s_sq, t, 2, i + 1)
                wait_before(dve, s_rqk, t)
                a = fr.done(dve.tensor_reduce(ss[:, H * i:H * i + H], heads(sq[:, i, :]), AX.X, ALU.add))
                fr.wait(a)
                dve.tensor_scalar(ss[:, H * i:H * i + H], ss[:, H * i:H * i + H], L2_EPS, None, ALU.add)\
                   .then_inc(s_ss, 1)

            def make_vb(t):
                wait_tile(dve, s_tokp, t, 3, 3)
                wait_tile(dve, s_beta, t)
                wait_before(dve, s_R, t, 2, back=2)
                dve.tensor_tensor(heads(vb[t.par][:, :]), heads(pF[1][:, :]), over_heads(beta[:, :]), ALU.mult)\
                   .then_inc(s_vb, 1)

            def start_t(t, hf):
                if hf == 0:
                    de.begin(t)
                wait_before(dve, s_Up, t)
                wait_before(dve, s_Op, t)
                if hf == 0:
                    wait_before(dve, s_T, t, T_UPDATES)
                a = de.done(dve.tensor_copy(Ti[hf][:, :, :], over_mats(ident[:, :])))
                b = de.done(dve.tensor_copy(TiT[hf][:, :, :], over_mats(ident[:, :])))
                wait_tile(dve, s_D1, t, 2, hf + 1)
                dve.tensor_tensor(PT[hf][:, :, :], mats(pZT[hf][:, :]), over_mats(causal[:, :]), ALU.mult)\
                   .then_inc(s_PT, 1)
                de.wait(b)
                settle(dve)
                dve.copy_predicated(Ti[hf][:, :, :], over_mats(m_lo[:, 0, :]), mats(pY[hf][:, :])).then_inc(s_T0, 1)
                wait_tile(dve, s_AT, t, 2, hf + 1)
                settle(dve)
                dve.copy_predicated(TiT[hf][:, :, :], over_mats(m_up[:, 0, :]), AT[hf][:, :, :]).then_inc(s_T0, 1)

            def update_t(t, k, hf):
                wait_tile(dve, s_Z, t, 2 * LEVELS, 2 * k - 1 + hf)
                if k == 1:
                    wait_tile(dve, s_T0, t, T_STARTS, 2 * hf + 2)
                else:
                    wait_tile(dve, s_T, t, T_UPDATES, t_updates(k - 1, hf))
                if k < LEVELS:
                    settle(dve)
                    dve.copy_predicated(Ti[hf][:, :, :], over_mats(m_lo[:, k, :]), mats(pZ[hf][:, :]))\
                       .then_inc(s_T, 1)
                    dve.copy_predicated(TiT[hf][:, :, :], over_mats(m_up[:, k, :]), mats(pZT[hf][:, :]))\
                       .then_inc(s_T, 1)
                else:
                    dve.tensor_copy(TiT[hf][0:DH, :, DH:P], mats(pZT[hf][0:DH, :])[:, :, DH:P]).then_inc(s_T, 1)

            def make_r(t):
                wait_tile(dve, s_vb, t)
                wait_before(dve, s_Up, t)
                for hf in range(2):
                    wait_tile(dve, s_Rp, t, 2, hf + 1)
                    dve.tensor_tensor(R[:, hf], heads(pY[hf][:, 0:HH * DH]), by_half(vb[t.par], hf), ALU.add)\
                       .then_inc(s_R, 1)

            def update_s(t):
                wait_tile(dve, s_Sp, t)
                wait_before(dve, s_S, t)
                if isinstance(t.v, int) and t.v == 0:
                    dve.wait_ge(s_S0, 1)
                dve.tensor_tensor(S[:, :], S[:, :], pZT[1][:, 0:HH * DH], ALU.add).then_inc(s_S, 1)

            def o_sums(t):
                wait_tile(dve, s_O, t, 4)
                wait_before(dve, s_ro, t)
                ba.begin(t)
                a = ba.done(dve.tensor_reduce(so[:, :], heads(osq[:, :]), AX.X, ALU.add))
                ba.wait(a)
                dve.tensor_scalar(so[:, :], so[:, :], 1.0 / DH, RMS_EPS, ALU.mult, ALU.add).then_inc(s_so, 1)

            def make_on(t):
                wait_tile(dve, s_ro, t)
                wait_before(dve, s_oTp, t)
                dve.tensor_tensor(heads(on[:, :]), heads(osb[:, :]), over_heads(ro[:, :]), ALU.mult).then_inc(s_on, 1)

            def make_x2(t):
                wait_tile(dve, s_yp, t)
                dve.tensor_tensor(xall[:, t.v, :], xall[:, t.v, :], pF[0][:, :], ALU.add).then_inc(s_x2, 1)
                wait_tile(dve, s_x2, t, 2, 1)
                settle(dve)
                a = ba.done(dve.bn_stats(st2[:, :], xall[:, t.v, :]))
                ba.wait(a)
                wait_before(dve, s_stat, t, 2)
                settle(dve)
                b = ba.done(dve.bn_aggr(mv2[:, :], st2[:, :]))
                ba.wait(b)
                wait_before(dve, s_r2, t)
                dve.tensor_scalar(ve2[:, :], mv2[:, 1:2], LN_EPS, None, ALU.add).then_inc(s_x2, 1)

            def make_x2n(t):
                wait_tile(dve, s_r2, t)
                wait_before(dve, s_x2Tp, t)
                dve.tensor_scalar(x2n[:, :], xall[:, t.v, :], mv2[:, 0:1], r2[:, 0:1], ALU.subtract, ALU.mult)\
                   .then_inc(s_x2n, 1)
                dve.tensor_copy(stat2[:, t.v, 0:1], mv2[:, 0:1]).then_inc(s_stat, 1)
                dve.tensor_copy(stat2[:, t.v, 1:2], r2[:, 0:1]).then_inc(s_stat, 1)

            def logits(t):
                wait_tile(dve, s_lgp, t)
                dve.tensor_copy(lg[:, t.v, :], pF[1][:, 0:E]).then_inc(s_lg, 1)

            def step(t, nxt, prev):
                if nxt:
                    ln1_stats(nxt)
                if prev:
                    o_sums(prev)
                if t:
                    start_t(t, 0)
                    start_t(t, 1)
                if nxt:
                    make_xn(nxt)
                if prev:
                    make_on(prev)
                for k in range(1, LEVELS + 1):
                    for hf in range(2):
                        if t:
                            update_t(t, k, hf)
                        if nxt and 2 <= k <= 4:
                            conv(nxt, k - 2, hf)
                        if k == 3 and hf == 1 and nxt:
                            betas(nxt)
                        if k == 4 and hf == 1 and prev:
                            make_x2(prev)
                        if k == 5 and hf == 0:
                            if nxt:
                                sums(nxt, 0)
                        if k == 5 and hf == 1:
                            if nxt:
                                sums(nxt, 1)
                                make_vb(nxt)
                            if prev:
                                make_x2n(prev)
                        if k == 6 and hf == 1 and prev:
                            logits(prev)
                if t:
                    make_r(t)
                    update_s(t)

            run_tiles(dve, step)


I = 352
IC = [P, P, I - 2 * P]
G, TOPG, K = 4, 2, 4
NE = E + 2
NQ = 80
assert NQ == K * T // P + E
NS = 3
UPW = DC * 2 * I
DNW = len(IC) * D


def routing(nc, es, lg, wsel, pos, qslot, qexp, tiles_to):

    def sb(name, shape, dt=F32):
        return es.enter_context(nc.sbuf_tensor(name, shape, dt))

    mx, sm = sb("mx", [P, NT]), sb("sm", [P, NT])
    z, sc = sb("z", [P, NT, E]), sb("sc", [P, NT, E])
    gs, grank, gsel = (sb(n, [P, NT, G]) for n in ("gs", "grank", "gsel"))
    rank, cmp_, sel = sb("rank", [P, NT, E]), sb("cmp", [P, NT, E]), sb("sel", [P, NT, E])
    before, ones = sb("before", [P, P]), sb("ones", [P, P])
    cnt, seg, inc = sb("cnt", [P, E, NT]), sb("seg", [P, E, NT]), sb("inc", [P, E, NT])
    nti = sb("nti", [P, E], I32)
    nt, one_e, tinc, posf = sb("nt", [P, E]), sb("one_e", [P, E]), sb("tinc", [P, E]), sb("posf", [P, NT, E])
    pj = sb("pj", [P, NT, K])
    qi, qc = sb("qi", [1, NQ]), sb("qc", [1, NQ, E])
    qf, q3 = sb("qf", [1, NQ]), sb("q3", [1, NQ])
    pre = es.enter_context(nc.psum_tensor("pre", [P, NT * E], F32))
    tot = es.enter_context(nc.psum_tensor("tot", [P, NT * E], F32))
    s_z, s_e, s_d, s_k, s_sel, s_cnt = (es.enter_context(nc.semaphore(n)) for n in (
        "z_ready", "exp_done", "route_chain", "route_consts", "sel_ready", "counts_psum"))

    def over(ap, n):
        return ap.unsqueeze(2).to_broadcast([P, NT, n])

    with nc.Block() as block:
        @block.scalar
        def _(act):
            act.wait_ge(s_z, 1)
            act.activation(z[:, :, :], z[:, :, :], ACT.Exp).then_inc(s_e, 1)

        @block.gpsimd
        def _(pool):
            pool.memset(before[:, :], 1.0).then_inc(s_k, 1)
            pool.memset(ones[:, :], 1.0).then_inc(s_k, 1)
            pool.iota(qi[:, :], pattern=[[1, NQ]], base=0, channel_multiplier=0,
                      allow_small_or_imprecise_dtypes=True).then_inc(s_k, 1)
            pool.wait_ge(s_k, 3)
            pool.affine_select(out=before[:, :], in_=before[:, :], compare_op=ALU.is_gt, fill=0.0,
                               base=0, pattern=[[1, P]], channel_multiplier=-1).then_inc(s_k, 1)

        @block.tensor
        def _(pe):
            pe.wait_ge(s_k, 4)
            pe.wait_ge(s_sel, 1)
            flat = sel[:, :, :].rearrange("p t e -> p (t e)")
            pe.matmul(pre[:, :], before[:, :], flat, start=True, stop=True).then_inc(s_cnt, 1)
            pe.matmul(tot[:, :], ones[:, :], flat, start=True, stop=True).then_inc(s_cnt, 1)

        @block.vector
        def _(dve):
            n = [0]

            def link(ins):
                ins.then_inc(s_d, 1)
                n[0] += 1
                dve.wait_ge(s_d, n[0])

            def ranks(dst, v, count):
                link(dve.memset(dst, 0.0))
                for j in range(count):
                    one = v[:, :, j:j + 1]
                    tmp = cmp_[:, :, 0:count]
                    ins = dve.tensor_tensor(tmp[:, :, 0:j + 1], one.to_broadcast([P, NT, j + 1]),
                                            v[:, :, 0:j + 1], ALU.is_gt)
                    if j + 1 < count:
                        ins.then_inc(s_d, 1)
                        n[0] += 1
                        ins = dve.tensor_tensor(tmp[:, :, j + 1:], one.to_broadcast([P, NT, count - 1 - j]),
                                                v[:, :, j + 1:], ALU.is_ge)
                    link(ins)
                    link(dve.tensor_tensor(dst, dst, tmp, ALU.add))

            link(dve.tensor_reduce(mx[:, :], lg[:, :, :], AX.X, ALU.max))
            dve.tensor_tensor(z[:, :, :], lg[:, :, :], over(mx[:, :], E), ALU.subtract).then_inc(s_z, 1)
            link(dve.memset(seg[:, :, :], 1.0))
            link(dve.memset(seg[:, :, 0:1], 0.0))
            link(dve.memset(one_e[:, :], 1.0))
            dve.wait_ge(s_e, 1)
            link(dve.tensor_reduce(sm[:, :], z[:, :, :], AX.X, ALU.add))
            link(dve.reciprocal(sm[:, :], sm[:, :]))
            link(dve.tensor_tensor(sc[:, :, :], z[:, :, :], over(sm[:, :], E), ALU.mult))
            link(dve.tensor_reduce(gs[:, :, :], sc[:, :, :].rearrange("p t (g e) -> p t g e", g=G), AX.X, ALU.max))
            ranks(grank[:, :, :], gs, G)
            link(dve.tensor_scalar(gsel[:, :, :], grank[:, :, :], float(TOPG), None, ALU.is_lt))
            link(dve.tensor_tensor(sc[:, :, :].rearrange("p t (g e) -> p t g e", g=G),
                                   sc[:, :, :].rearrange("p t (g e) -> p t g e", g=G),
                                   gsel[:, :, :].unsqueeze(3).to_broadcast([P, NT, G, E // G]), ALU.mult))
            ranks(rank[:, :, :], sc, E)
            dve.tensor_scalar(sel[:, :, :], rank[:, :, :], float(K), None, ALU.is_lt).then_inc(s_sel, 1)
            dve.wait_ge(s_sel, 1)
            link(dve.tensor_tensor(sc[:, :, :], sc[:, :, :], sel[:, :, :], ALU.mult))
            link(dve.tensor_reduce(sm[:, :], sc[:, :, :], AX.X, ALU.add))
            link(dve.tensor_scalar(sm[:, :], sm[:, :], 1e-20, None, ALU.add))
            link(dve.reciprocal(sm[:, :], sm[:, :]))
            link(dve.tensor_tensor(sc[:, :, :], sc[:, :, :], over(sm[:, :], E), ALU.mult))
            dve.wait_ge(s_cnt, 2)
            link(dve.tensor_copy(cnt[:, :, :], tot[:, :].rearrange("p (t e) -> p e t", e=E)))
            link(dve.tensor_tensor_scan(inc[:, :, :].rearrange("p e t -> p (e t)"),
                                        seg[:, :, :].rearrange("p e t -> p (e t)"),
                                        cnt[:, :, :].rearrange("p e t -> p (e t)"), 0.0, ALU.mult, ALU.add))
            link(dve.tensor_tensor(cnt[:, :, :], inc[:, :, :], cnt[:, :, :], ALU.subtract))
            link(dve.tensor_scalar(nti[:, :], inc[:, :, NT - 1], float(P - 1), None, ALU.add))
            link(dve.tensor_scalar(nti[:, :], nti[:, :], 7, None, ALU.logical_shift_right))
            link(dve.tensor_scalar(nt[:, :], nti[:, :], 1.0, None, ALU.max))
            link(dve.tensor_tensor_scan(tinc[:, :], one_e[:, :], nt[:, :], 0.0, ALU.mult, ALU.add))
            link(dve.tensor_copy(tiles_to[:, :], tinc[0:1, :]))
            link(dve.tensor_tensor(nt[:, :], tinc[:, :], nt[:, :], ALU.subtract))
            link(dve.scalar_tensor_tensor(out=cnt[:, :, :], in0=nt[:, :].unsqueeze(2).to_broadcast([P, E, NT]),
                                          scalar=float(P), in1=cnt[:, :, :], op0=ALU.mult, op1=ALU.add))
            link(dve.tensor_tensor(posf[:, :, :], pre[:, :].rearrange("p (t e) -> p t e", e=E),
                                   cnt[:, :, :].rearrange("p e t -> p t e"), ALU.add))
            for j in range(K):
                link(dve.tensor_scalar(sel[:, :, :], rank[:, :, :], float(j), None, ALU.is_equal))
                link(dve.tensor_tensor(cmp_[:, :, :], sel[:, :, :], posf[:, :, :], ALU.mult))
                link(dve.tensor_reduce(pj[:, :, j], cmp_[:, :, :], AX.X, ALU.add))
                link(dve.tensor_tensor(cmp_[:, :, :], sel[:, :, :], sc[:, :, :], ALU.mult))
                link(dve.tensor_reduce(wsel[:, :, j], cmp_[:, :, :], AX.X, ALU.add))
            link(dve.tensor_copy(pos[:, :, :], pj[:, :, :]))
            dve.wait_ge(s_k, 4)
            link(dve.tensor_tensor(qc[:, :, :], qi[:, :].unsqueeze(2).to_broadcast([1, NQ, E]),
                                   tinc[0:1, :].unsqueeze(1).to_broadcast([1, NQ, E]), ALU.is_ge))
            link(dve.tensor_reduce(qf[:, :], qc[:, :, :], AX.X, ALU.add))
            link(dve.tensor_scalar(qf[:, :], qf[:, :], float(E - 1), None, ALU.min))
            link(dve.tensor_copy(qexp[:, :], qf[:, :]))
            link(dve.tensor_scalar(qf[:, :], qf[:, :], 1.0, None, ALU.add))
            link(dve.tensor_copy(q3[:, :], qf[:, :]))
            for m in range(NS, NE, NS):
                link(dve.tensor_scalar(qc[:, :, 0], qf[:, :], float(m), -float(NS), ALU.is_ge, ALU.mult))
                link(dve.tensor_tensor(q3[:, :], q3[:, :], qc[:, :, 0], ALU.add))
            link(dve.tensor_copy(qslot[:, :], q3[:, :]))


def experts(nc, es, wup_d, wdn_d, xs_d, ys_d, xall, x2nT, stat2, wsel, pos, qslot, qexp, tiles_to, out):
    N = 512
    NG = T // N
    TPG = N // P

    def sb(name, shape, dt=F32):
        return es.enter_context(nc.sbuf_tensor(name, shape, dt))

    def sem(name):
        return es.enter_context(nc.semaphore(name))

    w = sb("w", [P, NS, UPW + DNW])
    ident = sb("ident2", [P, P])
    x2n = sb("x2n_all", [P, NT, D])
    gath = [x2n[:, K * i:K * i + K, :] for i in range(2)]
    ssg = [sb(f"ssg{i}", [P, N]) for i in range(2)]
    sa = [sb(f"sa{i}", [P, len(IC), N]) for i in range(2)]
    xs = [sb(f"xs{i}", [P, D]) for i in range(2)]
    xsT = [sb(f"xsT{i}", [P, DC, P]) for i in range(2)]
    g, a = sb("g", [P, I]), sb("a", [P, I])
    aT = sb("aT", [P, len(IC), P])
    y = [sb(f"y{i}", [P, D]) for i in range(2)]

    def bank(n):
        return es.enter_context(nc.psum_tensor(n, [P, N], F32))

    pG, pU = [bank(f"pG{i}") for i in range(2)], [bank(f"pU{i}") for i in range(2)]
    pD = [bank(f"pD{i}") for i in range(TPG)]
    pX, pA, pYq = pD[0], pD[1], pD[2]

    s_w, s_x2n, s_id = sem("weights_loaded"), sem("x2n_rows"), sem("ident_ready")
    s_scat = sem("rows_scattered")
    s_xl, s_ys = [sem(f"slots_loaded{i}") for i in range(2)], [sem(f"slots_stored{i}") for i in range(2)]
    s_xTp, s_xT, s_gp, s_g, s_up, s_a, s_aTp, s_aT, s_yp, s_y = (sem(n) for n in (
        "slotsT_psum", "slotsT_ready", "gate_psum", "gate_silu", "up_psum", "gated_ready", "gatedT_psum",
        "gatedT_ready", "y_psum2", "y_ready"))
    s_sup, s_ssg, s_sa, s_sdn, s_sacc = (sem(n) for n in (
        "shared_up_psum", "shared_silu", "shared_gated", "shared_down_psum", "shared_added"))
    s_gath = [sem(f"rows_gathered{i}") for i in range(2)]
    s_comb, s_cch, s_out = sem("combined"), sem("combine_chain"), sem("out_stored")
    UPS, DNS = NG * len(IC), NG * TPG

    def wup(slot, k):
        return w[:, slot, 2 * I * k:2 * I * (k + 1)]

    def wdn(slot, c):
        return w[:, slot, UPW + D * c:UPW + D * (c + 1)]

    def run_slots(eng, body):
        body(0, 0)
        body(1, 1)
        with eng.Fori(1, NQ // 2 - 1) as pair:
            body(2 * pair, 0)
            body(2 * pair + 1, 1)
        body(NQ - 2, 0)
        body(NQ - 1, 1)
        body(NQ, 0)

    def first(q):
        return isinstance(q, int) and q == 0

    def last(q):
        return isinstance(q, int) and q >= NQ - 1

    def end(q):
        return isinstance(q, int) and q == NQ

    def wait_pos(eng, s, value):
        if not (isinstance(value, int) and value <= 0):
            eng.wait_ge(s, value)

    with nc.Block() as block:
        @block.sync
        def _(sp):
            xv = xs_d.rearrange("(q p) d -> q p d", p=P)
            yv = ys_d.rearrange("(q p) d -> q p d", p=P)
            sp.wait_ge(s_scat, 16 * NT * K)
            for q in range(2):
                sp.dma_start(xs[q][:, :], xv[q]).then_inc(s_xl[q], 16)

            def body(q, par):
                if not (isinstance(q, int) and q >= NQ - 2):
                    sp.wait_ge(s_xTp, q + 1)
                    sp.dma_start(xs[par][:, :], xv[q + 2]).then_inc(s_xl[par], 16)
                if not first(q):
                    sp.wait_ge(s_y, q)
                    sp.dma_start(yv[q - 1], y[1 - par][:, :]).then_inc(s_ys[1 - par], 16)

            run_slots(sp, body)
            ov = out.rearrange("b (t p) d -> p (b t) d", p=P)
            for i in range(NG):
                sp.wait_ge(s_comb, (i + 1) * TPG)
                sp.dma_start(ov[:, TPG * i:TPG * i + TPG, :], xall[:, TPG * i:TPG * i + TPG, :]).then_inc(s_out, 16)
            sp.wait_ge(s_out, 16 * NG)

        @block.gpsimd
        def _(pool):
            def load(s, expert):
                b = s % NS
                pool.dma_start(w[:, b, 0:UPW].rearrange("p (c n) -> p c n", c=DC),
                               wup_d[expert].rearrange("(c p) n -> p c n", p=P)).then_inc(s_w, 16)
                pool.dma_start(w[:, b, UPW:UPW + 2 * D].rearrange("p (c n) -> p c n", c=2),
                               wdn_d[expert, 0:2 * P, :].rearrange("(c p) n -> p c n", p=P)).then_inc(s_w, 16)
                pool.dma_start(w[0:IC[2], b, UPW + 2 * D:UPW + DNW], wdn_d[expert, 2 * P:I, :]).then_inc(s_w, 16)

            load(0, E)
            pool.memset(ident[:, :], 0.0).then_inc(s_id, 1)
            pool.wait_ge(s_id, 1)
            pool.affine_select(out=ident[:, :], in_=ident[:, :], compare_op=ALU.not_equal, fill=1.0,
                               base=0, pattern=[[-1, P]], channel_multiplier=1).then_inc(s_id, 1)
            for i in range(NT):
                pool.wait_ge(s_x2n, i + 1)
                for j in range(K):
                    pool.indirect_dma_start(out=xs_d[:, :], out_offset=bass.IndirectOffsetOnAxis(
                        ap=pos[:, i, j:j + 1], axis=0), in_=x2n[:, i, :], in_offset=None).then_inc(s_scat, 16)
                if i in (1, 3):
                    s = (i + 1) // 2
                    pool.wait_ge(s_w, 48 * s)
                    load(s, s - 1)
            for s in range(NS, NE):
                pool.wait_ge(s_w, 48 * s)
                if s == NS:
                    pool.wait_ge(s_sdn, DNS)
                else:
                    done = pool.value_load(tiles_to[0:1, s - NS - 1:s - NS], min_val=1, max_val=NQ)
                    pool.wait_ge(s_yp, done)
                    pool.nop(nofuse=True)
                    pool.wait_ge(s_id, 2)
                load(s, s - 1 if s <= E else E + 1)
            for par in range(2):
                pool.wait_ge(s_ys[par], 16 * NQ // 2)
            for i in range(NT):
                if i >= 2:
                    pool.wait_ge(s_comb, i - 1)
                for j in range(K):
                    pool.indirect_dma_start(out=gath[i % 2][:, j, :], out_offset=None, in_=ys_d[:, :],
                                            in_offset=bass.IndirectOffsetOnAxis(ap=pos[:, i, j:j + 1], axis=0))\
                        .then_inc(s_gath[i % 2], 16)

        @block.scalar
        def _(act):
            def shared(half):
                for u in range(UPS):
                    m = IC[u % 3]
                    n = UPS * half + u
                    wait_pos(act, s_sa, n - 1)
                    act.wait_ge(s_sup, n + 1)
                    act.activation(ssg[u % 2][0:m, :], pG[u % 2][0:m, :], ACT.Silu).then_inc(s_ssg, 1)

            def turned_rows(q, par):
                act.wait_ge(s_xTp, q + 1)
                wait_pos(act, s_up, q - 1)
                act.activation(xsT[par][:, :, :], pX[:, :].rearrange("p (c n) -> p c n", c=DC), ACT.Copy)\
                   .then_inc(s_xT, 1)

            def body(q, par):
                if first(q):
                    turned_rows(0, 0)
                if not first(q):
                    act.wait_ge(s_aTp, q)
                    wait_pos(act, s_yp, q - 1)
                    act.activation(aT[:, 0:2, :], pA[:, 0:2 * P].rearrange("p (c n) -> p c n", c=2), ACT.Copy)\
                       .then_inc(s_aT, 1)
                    act.activation(aT[0:IC[2], 2, :], pA[0:IC[2], 2 * P:3 * P], ACT.Copy).then_inc(s_aT, 1)
                if not last(q):
                    turned_rows(q + 1, 1 - par)
                if not end(q):
                    act.wait_ge(s_gp, q + 1)
                    wait_pos(act, s_a, q)
                    act.activation(g[:, :], pG[0][:, 0:I], ACT.Silu).then_inc(s_g, 1)
                if not first(q):
                    act.wait_ge(s_yp, q)
                    if not (isinstance(q, int) and q < 3):
                        act.wait_ge(s_ys[1 - par], (q - 1 - (1 - par)) * 8)
                    act.activation(y[1 - par][:, :], pYq[:, :], ACT.Copy).then_inc(s_y, 1)

            shared(0)
            run_slots(act, body)
            shared(1)

        @block.vector
        def _(dve):
            for i in range(NT):
                dve.tensor_scalar(x2n[:, i, :], xall[:, i, :], stat2[:, i, 0:1], stat2[:, i, 1:2],
                                  ALU.subtract, ALU.mult).then_inc(s_x2n, 1)
            comb = [0]

            def gated(half, gr):
                for c in range(3):
                    u, m = 3 * gr + c, IC[c]
                    if c == 0:
                        wait_pos(dve, s_sdn, half * DNS + TPG * (gr - 1))
                    dve.wait_ge(s_ssg, half * UPS + u + 1)
                    dve.tensor_tensor(sa[gr % 2][0:m, c, :], ssg[u % 2][0:m, :], pU[u % 2][0:m, :], ALU.mult)\
                       .then_inc(s_sa, 1)

            def accumulate(half, gr):
                for i in range(TPG):
                    j = TPG * gr + i
                    dve.wait_ge(s_sdn, half * DNS + j + 1)
                    if half:
                        dve.wait_ge(s_sacc, j + 1)
                    else:
                        dve.wait_ge(s_x2n, NT)
                    dve.tensor_tensor(xall[:, j, :], xall[:, j, :], pD[i][:, :], ALU.add).then_inc(s_sacc, 1)

            def combine(i):
                dve.wait_ge(s_gath[i % 2], 16 * K * (i // 2 + 1))
                dve.wait_ge(s_sacc, DNS + i + 1)
                for j in range(K):
                    ins = dve.scalar_tensor_tensor(out=xall[:, i, :], in0=gath[i % 2][:, j, :],
                                                   scalar=wsel[:, i, j:j + 1], in1=xall[:, i, :],
                                                   op0=ALU.mult, op1=ALU.add)
                    if j < K - 1:
                        comb[0] += 1
                        ins.then_inc(s_cch, 1)
                        dve.wait_ge(s_cch, comb[0])
                    else:
                        ins.then_inc(s_comb, 1)

            def shared(half):
                for gr in range(NG + 1):
                    if gr < NG:
                        gated(half, gr)
                    if gr:
                        accumulate(half, gr - 1)
                        if half:
                            for i in range(TPG * (gr - 1), TPG * gr):
                                combine(i)

            def body(q, par):
                if not end(q):
                    dve.wait_ge(s_g, q + 1)
                    dve.wait_ge(s_up, q + 1)
                    wait_pos(dve, s_aTp, q)
                    dve.tensor_tensor(a[:, :], g[:, :], pU[0][:, 0:I], ALU.mult).then_inc(s_a, 1)

            shared(0)
            run_slots(dve, body)
            shared(1)

        @block.tensor
        def _(pe):
            def shared(half, slot):
                def up(gr):
                    for c in range(3):
                        u, m = 3 * gr + c, IC[c]
                        wait_pos(pe, s_sa, half * UPS + u - 1)
                        for p, off in ((pG[u % 2], 0), (pU[u % 2], I)):
                            for k in range(DC):
                                mm = pe.matmul(p[0:m, :], wup(slot, k)[:, off + P * c:off + P * c + m],
                                               x2nT[:, k, N * gr:N * gr + N], start=(k == 0), stop=(k == DC - 1))
                        mm.then_inc(s_sup, 1)

                def down(gr):
                    pe.wait_ge(s_sa, half * UPS + 3 * (gr + 1))
                    for i in range(TPG):
                        wait_pos(pe, s_sacc, half * DNS + TPG * (gr - 1) + i + 1)
                        for c in range(3):
                            m = IC[c]
                            mm = pe.matmul(pD[i][:, :], sa[gr % 2][0:m, c, P * i:P * i + P],
                                           wdn(slot, c)[0:m, :], start=(c == 0), stop=(c == 2))
                        mm.then_inc(s_sdn, 1)

                up(0)
                for gr in range(1, NG):
                    up(gr)
                    down(gr - 1)
                down(NG - 1)

            def turn_rows(q, par):
                pe.wait_ge(s_xl[par], (q - par) * 8 + 16)
                wait_pos(pe, s_xT, q)
                for c in range(DC):
                    mm = pe.transpose(pX[:, c * P:(c + 1) * P], xs[par][:, c * P:(c + 1) * P], ident[:, :])
                mm.then_inc(s_xTp, 1)

            def body(q, par):
                if first(q):
                    turn_rows(0, 0)
                if not end(q):
                    slot = pe.value_load(qslot[0:1, bass.ds(q, 1)], min_val=0, max_val=NS - 1)
                    expert = pe.value_load(qexp[0:1, bass.ds(q, 1)], min_val=0, max_val=E - 1)
                if not first(q):
                    before = pe.value_load(qslot[0:1, bass.ds(q - 1, 1)], min_val=0, max_val=NS - 1)
                    down = w[:, bass.ds(before, 1), :]
                    pe.wait_ge(s_a, q)
                    wait_pos(pe, s_aT, 2 * (q - 1))
                    for c in range(3):
                        mm = pe.transpose(pA[0:IC[c], c * P:(c + 1) * P], a[:, P * c:P * c + IC[c]], ident[:, :])
                    mm.then_inc(s_aTp, 1)
                if not last(q):
                    turn_rows(q + 1, 1 - par)
                if not end(q):
                    pe.wait_ge(s_xT, q + 1)
                    pe.wait_ge(s_w, expert * 48 + 96)
                    wait_pos(pe, s_g, q)
                    for k in range(DC):
                        mm = pe.matmul(pG[0][:, 0:I], xsT[par][:, k, :], w[:, bass.ds(slot, 1), 2 * I * k:2 * I * k + I],
                                       start=(k == 0), stop=(k == DC - 1))
                    mm.then_inc(s_gp, 1)
                if not first(q):
                    pe.wait_ge(s_aT, 2 * q)
                    wait_pos(pe, s_y, q - 1)
                    for c in range(3):
                        m = IC[c]
                        mm = pe.matmul(pYq[:, :], aT[0:m, c, :], down[0:m, :, UPW + D * c:UPW + D * (c + 1)],
                                       start=(c == 0), stop=(c == 2))
                    mm.then_inc(s_yp, 1)
                if not end(q):
                    wait_pos(pe, s_a, q)
                    for k in range(DC):
                        mm = pe.matmul(pU[0][:, 0:I], xsT[par][:, k, :],
                                       w[:, bass.ds(slot, 1), 2 * I * k + I:2 * I * (k + 1)],
                                       start=(k == 0), stop=(k == DC - 1))
                    mm.then_inc(s_up, 1)

            pe.wait_ge(s_w, 48)
            shared(0, 0)
            pe.wait_ge(s_sacc, DNS)
            pe.wait_ge(s_id, 2)
            run_slots(pe, body)
            pe.wait_ge(s_w, 48 * NE)
            pe.wait_ge(s_y, NQ)
            shared(1, (NE - 1) % NS)


def program(nc, x, wq, wk, wv, wb, cq, ck, cv, nw, wo, gw, wup, wdn, out):
    with ExitStack() as es:
        xall = es.enter_context(nc.sbuf_tensor("xall", [P, NT, D], F32))
        x2nT = es.enter_context(nc.sbuf_tensor("x2nT", [P, DC, T], F32))
        lg = es.enter_context(nc.sbuf_tensor("lg", [P, NT, E], F32))
        stat2 = es.enter_context(nc.sbuf_tensor("stat2", [P, NT, 2], F32))
        wsel = es.enter_context(nc.sbuf_tensor("wsel", [P, NT, K], F32))
        pos = es.enter_context(nc.sbuf_tensor("pos", [P, NT, K], I32))
        qslot = es.enter_context(nc.sbuf_tensor("qslot", [1, NQ], I32))
        qexp = es.enter_context(nc.sbuf_tensor("qexp", [1, NQ], I32))
        tiles_to = es.enter_context(nc.sbuf_tensor("tiles_to", [1, E], I32))
        xs_d = nc.dram_tensor("slot_rows", (NQ * P, D), F32, kind="Internal").ap()
        ys_d = nc.dram_tensor("slot_results", (NQ * P, D), F32, kind="Internal").ap()
        with ExitStack() as inner:
            attention(nc, inner, x, wq, wk, wv, wb, cq, ck, cv, nw, wo, gw, xall, x2nT, lg, stat2, xs_d)
        with ExitStack() as inner:
            routing(nc, inner, lg, wsel, pos, qslot, qexp, tiles_to)
        with ExitStack() as inner:
            experts(nc, inner, wup, wdn, xs_d, ys_d, xall, x2nT, stat2, wsel, pos, qslot, qexp, tiles_to, out)


_INS = ['L0_attn_hidden_states', 'L0_attn_Wq', 'L0_attn_Wk', 'L0_attn_Wv', 'L0_attn_Wb', 'L0_attn_conv_q',
        'L0_attn_conv_k', 'L0_attn_conv_v', 'L0_attn_norm_w', 'L0_attn_Wo']


def kernel(**inputs):
    import numpy as np
    import concourse.bacc as bacc
    from concourse.bass_utils import run_bass_kernel_spmd

    nc = bacc.Bacc("TRN2", target_bir_lowering=False, num_devices=1)
    laid = {n: np.asarray(inputs[n]) for n in _INS}
    laid['gate_T'] = np.asarray(inputs['L0_ffn_gate_w']).T
    up, down = np.asarray(inputs['L0_ffn_expert_up_w']), np.asarray(inputs['L0_ffn_expert_down_w'])
    sup, sdown = np.asarray(inputs['L0_ffn_shared_up_w']), np.asarray(inputs['L0_ffn_shared_down_w'])
    halves = sup.reshape(2, 2, I, D).transpose(1, 0, 2, 3).reshape(2, 2 * I, D)
    laid['up_T'] = np.concatenate([up, halves]).transpose(0, 2, 1)
    laid['down_T'] = np.concatenate([down.transpose(0, 2, 1), sdown.T.reshape(2, I, D)])
    arrays, args = {}, []
    for n, a in laid.items():
        a = np.ascontiguousarray(a)
        arrays[f"in_{n}"] = a
        args.append(nc.dram_tensor(f"in_{n}", a.shape, mybir.dt.from_np(a.dtype), kind="ExternalInput").ap())
    args.append(nc.dram_tensor("out_0", (1, T, D), F32, kind="ExternalOutput").ap())
    program(nc, *args)
    r = run_bass_kernel_spmd(nc, [arrays], core_ids=[0])
    return r.results[0]["out_0"]
```

```python
from contextlib import ExitStack

import concourse.bass as bass
from concourse import mybir

F32 = mybir.dt.float32
I32 = mybir.dt.int32
ALU = mybir.AluOpType
ACT = mybir.ActivationFunctionType
AX = mybir.AxisListType

P = 128
T, D = 2048, 512
H, DH = 8, 64
NT = T // P
DC = D // P
HH = H // 2
TAPS = 4
HALO = TAPS - 1
LEVELS = 6
E = 16
LN_EPS, L2_EPS, RMS_EPS = 1e-5, 1e-6, 1e-5


I = 352
IC = [P, P, I - 2 * P]
UPW = DC * 2 * I
DNW = len(IC) * D
B = 32
BLOCKS = P // B
T_STARTS = 4
T_SIGNALS = {1: 2, 2: 2, 3: 2, 4: 2, 5: 3, 6: 1}
T_UPDATES = 2 * sum(T_SIGNALS.values())
Y_SIGNALS = {1: 1, 2: 1, 3: 1, 4: 1, 5: 2, 6: 1}
Y_COPIES = 2 * sum(Y_SIGNALS.values())


def through(signals, k, hf, n=None):
    n = signals[k] if n is None else n
    return 2 * sum(signals[i] for i in range(1, k)) + signals[k] * hf + n


class Tile:

    def __init__(self, v, par):
        self.v, self.par = v, par


def wait_tile(eng, sem, tile, per_tile=1, k=None):
    k = per_tile if k is None else k
    eng.wait_ge(sem, tile.v * per_tile + k)


def wait_before(eng, sem, tile, per_tile=1, back=1):
    if isinstance(tile.v, int) and tile.v < back:
        return
    eng.wait_ge(sem, (tile.v - (back - 1)) * per_tile)


class Chain:

    def __init__(self, eng, sem, per_tile):
        self.eng, self.sem, self.n, self.k = eng, sem, per_tile, 0

    def begin(self, tile):
        assert self.k in (0, self.n), (self.k, self.n)
        self.tile, self.k = tile, 0
        self.started = not (isinstance(tile.v, int) and tile.v == 0)

    def done(self, ins):
        ins.then_inc(self.sem, 1)
        self.k += 1
        return self.k

    def wait(self, k=None):
        k = self.k if k is None else k
        if k or self.started:
            self.eng.wait_ge(self.sem, self.tile.v * self.n + k)


def load_expert(eng, buf, up, down, loaded):
    eng.dma_start(buf[:, 0:UPW].rearrange("p (c n) -> p c n", c=DC),
                  up.rearrange("(c p) n -> p c n", p=P)).then_inc(loaded, 16)
    eng.dma_start(buf[:, UPW:UPW + 2 * D].rearrange("p (c n) -> p c n", c=2),
                  down[0:2 * P, :].rearrange("(c p) n -> p c n", p=P)).then_inc(loaded, 16)
    eng.dma_start(buf[0:IC[2], UPW + 2 * D:UPW + DNW], down[2 * P:I, :]).then_inc(loaded, 16)


def run_tiles(eng, step):
    a, b = (lambda v: Tile(v, 0)), (lambda v: Tile(v, 1))
    step(None, a(0), None, None)
    step(a(0), b(1), None, None)
    step(b(1), a(2), a(0), None)
    step(a(2), b(3), b(1), a(0))
    step(b(3), a(4), a(2), b(1))
    with eng.Fori(4, NT - 2, 2) as i:
        step(a(i), b(i + 1), b(i - 1), a(i - 2))
        step(b(i + 1), a(i + 2), a(i), b(i - 1))
    step(a(NT - 2), b(NT - 1), b(NT - 3), a(NT - 4))
    step(b(NT - 1), None, a(NT - 2), b(NT - 3))
    step(None, None, b(NT - 1), a(NT - 2))
    step(None, None, None, b(NT - 1))


def attention(nc, es, x_d, wq_d, wk_d, wv_d, wb_d, cq_d, ck_d, cv_d, nw_d, wo_d, gw_d, wup_d, wdn_d, xall, lg, acc_d, xs_d,
              wsh1, s_wsh1):

    def sb(name, shape, dt=F32):
        return es.enter_context(nc.sbuf_tensor(name, shape, dt))

    def sem(name):
        return es.enter_context(nc.semaphore(name))

    ident = sb("ident", [P, P])
    causal = sb("causal", [P, P])
    xor_i, xor_j = sb("xor_i", [P, P], I32), sb("xor_j", [P, P], I32)
    scratch = sb("scratch", [P, 5, P])
    dist, dist_lo, dist_up, ge_a, ge_b = (scratch[:, i] for i in range(5))
    zeros = scratch[:, 0:D // P].rearrange("p c n -> p (c n)")
    dist_st = sb("dist_st", [P, B])
    m_lo = sb("m_lo", [P, LEVELS - 1, B], I32)
    m_up = sb("m_up", [P, LEVELS - 1, P], I32)
    ident_st = sb("ident_st", [P, B])
    nhalf = sb("nhalf", [P, 16])
    w3 = sb("w3", [P, 3, DC, D])
    wb = sb("wb", [P, DC, H])
    cw = sb("cw", [P, 3 * DC, TAPS])
    nw = sb("nw", [P, 1])
    wo = sb("wo", [P, DC, D])
    gw = sb("gw", [P, DC, E])
    xn = sb("xn", [P, D])
    xnT = sb("xnT", [P, DC, P])
    st1, mv1, r1 = sb("st1", [P, 6]), sb("mv1", [P, 2]), sb("r1", [P, 1])
    ve1 = sb("ve1", [P, 1])
    raw = sb("raw", [P, 3 * DC, HALO + P])
    acc = sb("acc", [P, 3 * DC, P])
    sil = acc
    th, beta, nbeta = sb("th", [P, H]), sb("beta", [P, H]), sb("nbeta", [P, H])
    tok = sb("tok", [P, 2, D])
    sq = sb("sq", [P, 2, D])
    ss, rqk = sb("ss", [P, 2 * H]), sb("rqk", [P, 2 * H])
    qn = sb("qn", [P, D])
    kn = [sb(f"kn{i}", [P, D]) for i in range(2)]
    nkb = sb("nkb", [P, D])
    vb = [sb(f"vb{i}", [P, D]) for i in range(2)]
    QT, KT, KBT = ([sb(f"{n}{i}", [P, DC, P]) for i in range(2)] for n in ("QT", "KT", "KBT"))
    TiT, PT = ([sb(f"{n}{i}", [P, HH, P]) for i in range(2)] for n in ("TiT", "PT"))
    AB, A5 = ([sb(f"{n}{i}", [P, HH, P]) for i in range(2)] for n in ("AB", "A5"))
    A6 = [sb(f"A6_{i}", [DH, HH, DH]) for i in range(2)]
    Tst, Yst, ZTs = ([sb(f"{n}{i}", [P, HH, B]) for i in range(2)] for n in ("Tst", "Yst", "ZTs"))
    Y5 = [sb(f"Y5_{i}", [P, HH, P]) for i in range(2)]
    Y6 = [sb(f"Y6_{i}", [P, HH, DH]) for i in range(2)]
    T64 = [buf[0:DH] for buf in Y6]
    S = sb("S", [P, HH * DH])
    R, U = sb("R", [P, 2, HH, DH]), sb("U", [P, 2, HH, DH])
    osb, osq = sb("osb", [P, D]), sb("osq", [P, D])
    on = osb
    so, ro = sb("so", [P, H]), sb("ro", [P, H])
    oT = sb("oT", [P, DC, P])
    st2, mv2, r2, ve2 = sb("st2", [P, 6]), sb("mv2", [P, 2]), sb("r2", [P, 1]), sb("ve2", [P, 1])
    x2n = sb("x2n", [P, D])
    x2g = sb("x2g", [P, DC, P])
    x2r = [sb(f"x2r{i}", [P, D]) for i in range(2)]
    wsh = sb("wsh", [P, UPW + DNW])
    ssg, sa = sb("ssg_t", [P, len(IC), P]), sb("sa_t", [P, len(IC), P])

    def bank(name):
        return es.enter_context(nc.psum_tensor(name, [P, D], F32))

    pY, pZ, pZT = ([bank(f"{n}{i}") for i in range(2)] for n in ("pY", "pZ", "pZT"))
    pF = [bank(f"pF{i}") for i in range(2)]

    s_proj_w = [sem(f"proj_w_loaded{i}") for i in range(3)]
    s_AB, s_st, s_T64, s_clear = sem("AB_ready"), sem("A_stack_psum"), sem("T64_ready"), sem("cleared")
    s_zero, s_zeroed, s_xkeep = sem("zeros_ready"), sem("slots_zeroed"), sem("x2n_kept")
    s_wsh, s_hg, s_hs, s_hu, s_ha, s_hd, s_hacc = (sem(n) for n in (
        "shared_w_loaded", "sh_gate_psum", "sh_silu", "sh_up_psum", "sh_gated", "sh_down_psum", "sh_added"))
    s_st2 = [sem(f"acc_stored{i}") for i in range(2)]
    (s_xload, s_wload, s_wo, s_iota, s_const, s_masks, s_wos, s_S0,
     s_stats, s_r1, s_xn, s_xTp, s_xnT, s_proj, s_raw, s_conv, s_sil, s_bp, s_th, s_beta, s_nbeta,
     s_tokp, s_tok, s_sq, s_vb, s_ss, s_rqk, s_knorm, s_back, s_qkT,
     s_D1, s_AT, s_T0, s_PT, s_Y, s_Ys, s_Z, s_T, s_Rp, s_R, s_Up, s_U, s_Op, s_O, s_Sp, s_S,
     s_so, s_ro, s_on, s_oTp, s_oT, s_yp, s_x2, s_r2, s_x2n, s_x2Tp, s_x2nT, s_lgp, s_lg,
     c_dF, c_dD, c_dB, c_aF, c_init) = (sem(n) for n in (
        "x_loaded", "w_loaded", "wo_loaded", "iota_done", "const_done", "masks_done", "wo_scaled", "S_zeroed",
        "ln1_stats", "ln1_rstd", "xn_ready", "xnT_psum", "xnT_ready", "proj_psum", "raw_ready", "conv_done",
        "silu_done", "beta_psum", "tanh_done", "beta_ready", "nbeta_ready",
        "tok_psum", "tok_ready", "tok_squared", "vb_ready", "qk_sums", "qk_rnorm", "qk_normed", "back_psum", "qkT_ready",
        "gram_psum", "AT_ready", "T_started", "PT_ready", "Y_psum", "Y_ready", "Z_psum", "T_updated",
        "R_psum", "R_ready", "U_psum", "U_ready", "O_psum", "O_ready", "S_psum", "S_ready",
        "o_sums", "o_rnorm", "on_ready", "oT_psum", "oT_ready", "y_psum", "x2_ready", "ln2_rstd", "x2n_ready",
        "x2nT_psum", "x2nT_ready", "logit_psum", "logits_ready",
        "dve_front", "dve_delta", "dve_back", "act_front", "init_chain"))

    def heads(ap):
        return ap.rearrange("p (h d) -> p h d", d=DH)

    def mats(ap):
        return ap.rearrange("p (h n) -> p h n", n=P)

    def stack(ap):
        return ap.rearrange("p (h n) -> p h n", n=P)[:, :, 0:B]

    def repeated(ap, times=BLOCKS):
        return ap.unsqueeze(1).to_broadcast([ap.shape[0], times, ap.shape[1]])

    def in_turn(ap, n=B):
        return ap.rearrange("p (r n) -> p r n", n=n)

    def over_blocks(ap):
        return ap.unsqueeze(2).to_broadcast([P, HH, BLOCKS, B])

    def blocks(ap):
        return ap.rearrange("p h (b n) -> p h b n", n=B)

    def over_heads(ap):
        return ap.unsqueeze(2).to_broadcast([P, H, DH])

    def by_half(buf, hf):
        return buf[:, :].rearrange("p (n f d) -> p f n d", f=2, d=DH)[:, hf]

    def settle(eng):
        eng.nop(nofuse=True)
        eng.wait_ge(s_const, 5)

    def over_mats(ap):
        return ap.unsqueeze(1).to_broadcast([P, HH, P])

    def over_stack(ap):
        return ap.unsqueeze(1).to_broadcast([P, HH, B])

    with nc.Block() as block:

        @block.sync
        def _(sp):
            xv = x_d.rearrange("b (t p) d -> p (b t) d", p=P)
            sp.dma_start(xall[:, 0:1, :], xv[:, 0:1, :]).then_inc(s_xload, 16)
            for i, w in enumerate((wq_d, wk_d, wv_d)):
                sp.dma_start(w3[:, i], w.rearrange("(c p) n -> p c n", p=P)).then_inc(s_proj_w[i], 16)
            sp.dma_start(wb[:, :, :], wb_d.rearrange("(c p) n -> p c n", p=P)).then_inc(s_wload, 16)
            for i, w in enumerate((cq_d, ck_d, cv_d)):
                sp.dma_start(cw[:, DC * i:DC * i + DC, :], w.rearrange("(c p) n -> p c n", p=P)).then_inc(s_wload, 16)
            for lo, hi in ((1, 4), (4, 8), (8, NT)):
                sp.dma_start(xall[:, lo:hi, :], xv[:, lo:hi, :]).then_inc(s_xload, 16)
            for i in range(2):
                sp.dma_start(nw[DH * i:DH * i + DH, :], nw_d.rearrange("(p o) -> p o", o=1)).then_inc(s_wo, 16)
            sp.dma_start(wo[:, :, :], wo_d.rearrange("(c p) n -> p c n", p=P)).then_inc(s_wo, 16)
            sp.dma_start(gw[:, :, :], gw_d.rearrange("(c p) n -> p c n", p=P)).then_inc(s_wo, 16)
            load_expert(sp, wsh, wup_d[E], wdn_d[E], s_wsh)
            load_expert(sp, wsh1, wup_d[E + 1], wdn_d[E + 1], s_wsh1)
            rows = xs_d.rearrange("(p r) d -> p r d", p=P)
            R4 = -(-rows.shape[1] // 4)
            sp.wait_ge(s_zero, 1)
            for i in range(4):
                part = rows[:, R4 * i:min(R4 * (i + 1), rows.shape[1]), :]
                sp.dma_start(part, zeros.unsqueeze(1).to_broadcast([P, part.shape[1], D])).then_inc(s_zeroed, 16)
            sp.wait_ge(s_zeroed, 16 * 4)
            av = acc_d.rearrange("(t p) d -> t p d", p=P)

            def step(t, nxt, prev, old):
                if old:
                    wait_tile(sp, s_hacc, old)
                    sp.dma_start(av[old.v], x2r[old.par][:, :]).then_inc(s_st2[old.par], 16)

            run_tiles(sp, step)
            for par in range(2):
                sp.wait_ge(s_st2[par], 16 * NT // 2)

        @block.gpsimd
        def _(pool):
            pool.memset(ident[:, :], 0.0).then_inc(s_const, 1)
            pool.memset(causal[:, :], 1.0).then_inc(s_const, 1)
            pool.memset(nhalf[:, :], -0.5).then_inc(s_const, 1)
            pool.iota(xor_i[:, :], pattern=[[0, P]], base=0, channel_multiplier=1).then_inc(s_iota, 1)
            pool.iota(xor_j[:, :], pattern=[[1, P]], base=0, channel_multiplier=0).then_inc(s_iota, 1)
            pool.wait_ge(s_const, 3)
            pool.affine_select(out=ident[:, :], in_=ident[:, :], compare_op=ALU.not_equal, fill=1.0,
                               base=0, pattern=[[-1, P]], channel_multiplier=1).then_inc(s_const, 1)
            pool.affine_select(out=causal[:, :], in_=causal[:, :], compare_op=ALU.is_ge, fill=0.0,
                               base=0, pattern=[[1, P]], channel_multiplier=-1).then_inc(s_const, 1)
            pool.wait_ge(s_masks, 2)
            pool.affine_select(out=dist_lo[:, :], in_=dist[:, :], compare_op=ALU.is_gt, fill=0.0,
                               base=0, pattern=[[-1, P]], channel_multiplier=1).then_inc(s_const, 1)
            pool.affine_select(out=dist_up[:, :], in_=dist[:, :], compare_op=ALU.is_gt, fill=0.0,
                               base=0, pattern=[[1, P]], channel_multiplier=-1).then_inc(s_const, 1)

            def rstd1(t):
                wait_tile(pool, s_stats, t)
                wait_before(pool, s_xn, t)
                pool.tensor_tensor(r1[:, :], ve1[:, :], nhalf[:, 0:1], ALU.pow).then_inc(s_r1, 1)

            def qk_norms(t):
                wait_tile(pool, s_ss, t, 2)
                wait_before(pool, s_knorm, t, 3)
                pool.tensor_tensor(rqk[:, :], ss[:, :], nhalf[:, :], ALU.pow).then_inc(s_rqk, 1)
                wait_tile(pool, s_rqk, t)
                wait_tile(pool, s_beta, t)
                wait_before(pool, s_back, t, 3)
                wait_before(pool, s_Sp, t, back=2)
                pool.tensor_tensor(heads(qn[:, :]), heads(tok[:, 0, :]), over_heads(rqk[:, 0:H]), ALU.mult)\
                    .then_inc(s_knorm, 1)
                pool.tensor_tensor(heads(kn[t.par][:, :]), heads(tok[:, 1, :]), over_heads(rqk[:, H:2 * H]), ALU.mult)\
                    .then_inc(s_knorm, 1)
                wait_tile(pool, s_knorm, t, 3, 2)
                pool.tensor_tensor(heads(nkb[:, :]), heads(kn[t.par][:, :]), over_heads(nbeta[:, :]), ALU.mult)\
                    .then_inc(s_knorm, 1)

            def o_rnorm(t):
                wait_tile(pool, s_so, t)
                wait_before(pool, s_on, t)
                pool.tensor_tensor(ro[:, :], so[:, :], nhalf[:, 0:H], ALU.pow).then_inc(s_ro, 1)

            def rstd2(t):
                wait_tile(pool, s_x2, t, 2)
                wait_before(pool, s_x2n, t)
                pool.tensor_tensor(r2[:, :], ve2[:, :], nhalf[:, 0:1], ALU.pow).then_inc(s_r2, 1)

            def t64_blocks(t, hf):
                wait_tile(pool, s_T, t, T_UPDATES, through(T_SIGNALS, 4, hf))
                wait_before(pool, s_Z, t, 2 * LEVELS)
                settle(pool)
                for b in range(2):
                    rows = slice(B * b, B * b + B)
                    pool.tensor_copy(T64[hf][rows, :, B * b:B * b + B], Tst[hf][rows, :, :]).then_inc(s_T64, 1)

            pool.wait_ge(s_clear, 2 * 4)

            def step(t, nxt, prev, old):
                if nxt:
                    rstd1(nxt)
                if prev:
                    o_rnorm(prev)
                if t:
                    t64_blocks(t, 0)
                    t64_blocks(t, 1)
                    wait_tile(pool, s_T64, t, 2 * 2)
                if prev:
                    rstd2(prev)
                if nxt:
                    qk_norms(nxt)

            run_tiles(pool, step)

        @block.scalar
        def _(act):
            cf = Chain(act, c_aF, 3)

            def xT_copy(t):
                wait_tile(act, s_xTp, t)
                wait_before(act, s_bp, t)
                act.activation(xnT[:, :, :], mats(pF[0][:, :]), ACT.Copy).then_inc(s_xnT, 1)

            def raw_copy(t, i):
                if i == 0:
                    cf.begin(t)
                sec = slice(DC * i, DC * i + DC)
                if isinstance(t.v, int) and t.v == 0:
                    act.wait_ge(s_S0, 2)
                    cf.done(act.activation(raw[:, sec, 0:HALO], raw[:, sec, P:P + HALO], ACT.Copy))
                else:
                    wait_before(act, s_conv, t, 3 * 4)
                    cf.done(act.activation(raw[:, sec, 0:HALO], raw[:, sec, P:P + HALO], ACT.Copy))
                cf.wait()
                wait_tile(act, s_proj, t, 3, i + 1)
                act.activation(raw[:, sec, HALO:], mats(pF[(i + 1) % 2][:, :]), ACT.Copy).then_inc(s_raw, 1)

            def silu(t, i):
                sec = slice(DC * i, DC * i + DC)
                wait_tile(act, s_conv, t, 3 * 4, 4 * i + 4)
                act.activation(sil[:, sec, :], acc[:, sec, :], ACT.Silu).then_inc(s_sil, 1)

            def tanh(t):
                wait_tile(act, s_bp, t)
                wait_before(act, s_beta, t)
                act.activation(th[:, :], pF[0][:, 0:H], ACT.Tanh, scale=0.5).then_inc(s_th, 1)

            def tok_copy(t, i):
                wait_tile(act, s_tokp, t, 3, i + 1)
                wait_before(act, s_knorm, t, 3)
                act.activation(tok[:, i, :], pF[(1, 0)[i]][:, :], ACT.Copy).then_inc(s_tok, 1)
                wait_before(act, s_ss, t, 2)
                act.activation(sq[:, i, :], pF[(1, 0)[i]][:, :], ACT.Square).then_inc(s_sq, 1)

            def back_copy(t, i):
                dst = (QT, KT, KBT)[i][t.par]
                wait_tile(act, s_back, t, 3, i + 1)
                wait_before(act, s_Op, t, back=2)
                act.activation(dst[:, :, :], mats(pF[i % 2][:, :]), ACT.Copy,
                               scale=DH ** -0.5 if i == 0 else 1.0).then_inc(s_qkT, 1)

            def ab_copy(t, hf):
                wait_tile(act, s_D1, t, 2, hf + 1)
                wait_before(act, s_Z, t, 2 * LEVELS)
                wait_before(act, s_T0, t, T_STARTS)
                for b in range(BLOCKS):
                    rows = slice(B * b, B * b + B)
                    act.activation(AB[hf][rows, :, rows], mats(pZ[hf][rows, :])[:, :, rows], ACT.Copy).then_inc(s_AB, 1)

            def a56_copy(t, hf):
                wait_before(act, s_Z, t, 2 * LEVELS)
                for b in (0, 2):
                    rows, cols = slice(B * b, B * b + B), slice(B * b + B, B * b + 2 * B)
                    act.activation(A5[hf][rows, :, cols], mats(pZ[hf][rows, :])[:, :, cols], ACT.Copy).then_inc(s_AT, 1)
                act.activation(A6[hf][:, :, :], mats(pZ[hf][0:DH, :])[:, :, DH:P], ACT.Copy).then_inc(s_AT, 1)

            def y_copy(t, k, hf):
                wait_tile(act, s_Y, t, 2 * LEVELS, 2 * k - 1 + hf)
                if k > 1:
                    wait_tile(act, s_Z, t, 2 * LEVELS, 2 * k - 3 + hf)
                else:
                    wait_before(act, s_Z, t, 2 * LEVELS)
                if k < 5:
                    act.activation(Yst[hf][:, :, :], stack(pY[hf][:, :]), ACT.Copy).then_inc(s_Ys, 1)
                elif k == 5:
                    for b in (1, 3):
                        rows, cols = slice(B * b, B * b + B), slice(B * (b - 1), B * b)
                        act.activation(Y5[hf][rows, :, cols], stack(pY[hf][rows, :]), ACT.Copy).then_inc(s_Ys, 1)
                else:
                    act.activation(Y6[hf][DH:P, :, :], mats(pY[hf][DH:P, :])[:, :, 0:DH], ACT.Copy)\
                       .then_inc(s_Ys, 1)

            def u_copy(t):
                wait_tile(act, s_Up, t)
                wait_before(act, s_Sp, t)
                act.activation(U[:, :, :, :], pZT[0][:, :].rearrange("p (f n d) -> p f n d", f=2, d=DH), ACT.Copy)\
                   .then_inc(s_U, 1)

            def o_copy(t):
                wait_tile(act, s_Op, t)
                wait_before(act, s_oTp, t)
                for hf in range(2):
                    o = heads(pZ[hf][:, 0:HH * DH])
                    act.activation(by_half(osb, hf), o, ACT.Copy).then_inc(s_O, 1)
                    act.activation(by_half(osq, hf), o, ACT.Square).then_inc(s_O, 1)

            def oT_copy(t):
                wait_tile(act, s_oTp, t)
                wait_before(act, s_yp, t)
                act.activation(oT[:, :, :], mats(pF[1][:, :]), ACT.Copy).then_inc(s_oT, 1)

            def x2T_copy(t):
                wait_tile(act, s_x2Tp, t)
                wait_before(act, s_lgp, t)
                wait_before(act, s_hu, t)
                act.activation(x2g[:, :, :], mats(pF[0][:, :]), ACT.Copy).then_inc(s_x2nT, 1)

            def keep_x2n(t):
                wait_tile(act, s_x2n, t)
                act.activation(xall[:, t.v, :], x2n[:, :], ACT.Copy).then_inc(s_xkeep, 1)

            def shared_silu(t):
                wait_tile(act, s_hg, t)
                wait_before(act, s_ha, t)
                act.activation(ssg[:, :, :], mats(pZ[0][:, 0:len(IC) * P]), ACT.Silu).then_inc(s_hs, 1)

            def step(t, nxt, prev, old):
                if t:
                    ab_copy(t, 0)
                    ab_copy(t, 1)
                for k in range(1, LEVELS + 1):
                    if t:
                        y_copy(t, k, 0)
                        y_copy(t, k, 1)
                        if k == 1:
                            a56_copy(t, 0)
                            a56_copy(t, 1)
                    if nxt:
                        if k == 1:
                            xT_copy(nxt)
                            raw_copy(nxt, 0)
                        elif k == 2:
                            raw_copy(nxt, 1)
                            raw_copy(nxt, 2)
                        elif k == 3:
                            tanh(nxt)
                            silu(nxt, 0)
                        elif k == 4:
                            silu(nxt, 1)
                            tok_copy(nxt, 0)
                        elif k == 5:
                            silu(nxt, 2)
                            tok_copy(nxt, 1)
                    if prev:
                        if k == 3:
                            oT_copy(prev)
                        elif k == 6:
                            keep_x2n(prev)
                            x2T_copy(prev)
                    if old and k == 4:
                        shared_silu(old)
                if t:
                    u_copy(t)
                    o_copy(t)
                if nxt:
                    for i in range(3):
                        back_copy(nxt, i)

            act.wait_ge(s_clear, 2 * 4)
            run_tiles(act, step)

        @block.tensor
        def _(pe):
            def xT(t):
                wait_tile(pe, s_xn, t)
                wait_before(pe, s_qkT, t, 3)
                for c in range(DC):
                    mm = pe.transpose(pF[0][:, c * P:(c + 1) * P], xn[:, c * P:(c + 1) * P], ident[:, :])
                mm.then_inc(s_xTp, 1)

            def project(t, i):
                if i == 0:
                    wait_tile(pe, s_xnT, t)
                if isinstance(t.v, int) and t.v == 0:
                    pe.wait_ge(s_proj_w[i], 16)
                if i == 2:
                    wait_tile(pe, s_raw, t, 3, 1)
                if i == 1:
                    wait_tile(pe, s_xnT, t)
                for c in range(DC):
                    for k in range(DC):
                        mm = pe.matmul(pF[(i + 1) % 2][:, c * P:(c + 1) * P], w3[:, i, k, c * P:(c + 1) * P],
                                       xnT[:, k, :], start=(k == 0), stop=(k == DC - 1))
                mm.then_inc(s_proj, 1)

            def betas(t):
                wait_tile(pe, s_raw, t, 3, 2)
                if isinstance(t.v, int) and t.v == 0:
                    pe.wait_ge(s_wload, 4 * 16)
                for k in range(DC):
                    mm = pe.matmul(in_turn(pF[0][:, 0:P], H), xnT[:, k, :], repeated(wb[:, k, :], P // H),
                                   start=(k == 0), stop=(k == DC - 1))
                mm.then_inc(s_bp, 1)

            def to_tokens(t, i):
                wait_tile(pe, s_sil, t, 3, i + 1)
                if i == 0:
                    wait_tile(pe, s_raw, t, 3, 3)
                elif i == 1:
                    wait_tile(pe, s_th, t)
                else:
                    wait_tile(pe, s_sq, t, 2, 1)
                for c in range(DC):
                    mm = pe.transpose(pF[(1, 0, 1)[i]][:, c * P:(c + 1) * P], sil[:, DC * i + c, :], ident[:, :])
                mm.then_inc(s_tokp, 1)

            def to_channels(t, i):
                src = (qn, kn[t.par], nkb)[i]
                wait_tile(pe, s_knorm, t, 3, i + 1)
                if i == 0:
                    wait_tile(pe, s_sq, t, 2, 2)
                elif i == 1:
                    wait_tile(pe, s_vb, t)
                else:
                    wait_tile(pe, s_qkT, t, 3, 1)
                for c in range(DC):
                    mm = pe.transpose(pF[i % 2][:, c * P:(c + 1) * P], src[:, c * P:(c + 1) * P], ident[:, :])
                mm.then_inc(s_back, 1)

            def gram(t, hf):
                if hf == 0:
                    wait_tile(pe, s_qkT, t, 3)
                    wait_before(pe, s_O, t, 4)
                    wait_before(pe, s_S, t)
                q, k, kb = QT[t.par], KT[t.par], KBT[t.par]
                for n in range(HH):
                    rows, cols = slice(DH * hf, DH * hf + DH), slice(n * P, (n + 1) * P)
                    pe.matmul(pZ[hf][:, cols], k[rows, n, :], kb[rows, n, :], start=True, stop=True)
                    mm = pe.matmul(pZT[hf][:, cols], k[rows, n, :], q[rows, n, :], start=True, stop=True)
                mm.then_inc(s_D1, 1)

            def stack_a(t, hf):
                wait_tile(pe, s_AB, t, 2 * BLOCKS, BLOCKS * (hf + 1))
                for n in range(HH):
                    mm = pe.matmul(in_turn(pY[hf][:, n * P:(n + 1) * P]), AB[hf][:, n, :], repeated(ident_st[:, :]),
                                   start=True, stop=True)
                mm.then_inc(s_st, 1)

            def level_y(t, k, hf):
                if k == 1:
                    wait_tile(pe, s_T0, t, T_STARTS, 2 * hf + 2)
                else:
                    wait_tile(pe, s_Ys, t, Y_COPIES, through(Y_SIGNALS, k - 1, hf))
                    wait_tile(pe, s_T, t, T_UPDATES, through(T_SIGNALS, k - 1, hf, 1))
                if k == 5:
                    wait_tile(pe, s_AT, t, 2 * 3, 3 * (hf + 1))
                if k == LEVELS:
                    wait_tile(pe, s_T64, t, 2 * 2, 2 * (hf + 1))
                    settle(pe)
                for n in range(HH):
                    if k < LEVELS:
                        mm = pe.matmul(in_turn(pY[hf][:, n * P:(n + 1) * P]), (AB if k < 5 else A5)[hf][:, n, :],
                                       repeated(Tst[hf][:, n, :]), start=True, stop=True)
                    else:
                        mm = pe.matmul(pY[hf][DH:P, n * P:n * P + DH], A6[hf][:, n, :], T64[hf][:, n, :],
                                       start=True, stop=True)
                mm.then_inc(s_Y, 1)

            def level_z(t, k, hf):
                wait_tile(pe, s_Ys, t, Y_COPIES, through(Y_SIGNALS, k, hf))
                if k == 1:
                    wait_tile(pe, s_PT, t, 2, hf + 1)
                else:
                    wait_tile(pe, s_T, t, T_UPDATES, through(T_SIGNALS, k - 1, hf))
                if k == LEVELS:
                    settle(pe)
                for n in range(HH):
                    if k < 5:
                        mm = pe.matmul(in_turn(pZT[hf][:, n * P:(n + 1) * P]), TiT[hf][:, n, :], repeated(Yst[hf][:, n, :]),
                                       start=True, stop=True)
                    elif k == 5:
                        pe.matmul(in_turn(pZT[hf][:, n * P:n * P + 2 * B]), TiT[hf][:, n, :],
                                  repeated(Y5[hf][:, n, 0:B], 2), start=True, stop=True)
                        mm = pe.matmul(in_turn(pZT[hf][:, n * P + 2 * B:(n + 1) * P]),
                                       Y5[hf][:, n, :],
                                       TiT[hf][:, n, :].rearrange("p (g o m) -> p g o m", g=2, o=2)[:, :, 1],
                                       start=True, stop=True)
                    else:
                        mm = pe.matmul(pZT[hf][0:DH, n * P + DH:(n + 1) * P], Y6[hf][DH:P, n, :],
                                       TiT[hf][DH:P, n, DH:P], start=True, stop=True)
                mm.then_inc(s_Z, 1)

            def state_out(t):
                wait_tile(pe, s_Ys, t, Y_COPIES)
                if isinstance(t.v, int) and t.v == 0:
                    pe.wait_ge(s_S0, 1)
                else:
                    wait_before(pe, s_S, t)
                for hf in range(2):
                    rows = slice(DH * hf, DH * hf + DH)
                    for n in range(HH):
                        mm = pe.matmul(in_turn(pY[hf][:, n * P:(n + 1) * P], DH), KBT[t.par][rows, n, :],
                                       repeated(S[rows, n * DH:(n + 1) * DH], 2), start=True, stop=True)
                    mm.then_inc(s_Rp, 1)

            def solve(t):
                wait_tile(pe, s_T, t, T_UPDATES)
                for hf in range(2):
                    wait_tile(pe, s_R, t, 2, hf + 1)
                    for n in range(HH):
                        mm = pe.matmul(pZT[0][:, (HH * hf + n) * DH:(HH * hf + n + 1) * DH], TiT[hf][:, n, :],
                                       R[:, hf, n, :], start=True, stop=True)
                mm.then_inc(s_Up, 1)

            def outputs(t, old):
                wait_tile(pe, s_U, t)
                if old:
                    wait_tile(pe, s_ha, old)
                for hf in range(2):
                    rows = slice(DH * hf, DH * hf + DH)
                    for n in range(HH):
                        o = pZ[hf][:, n * DH:(n + 1) * DH]
                        pe.matmul(o, QT[t.par][rows, n, :], S[rows, n * DH:(n + 1) * DH], start=True, stop=False)
                        mm = pe.matmul(o, PT[hf][:, n, :], U[:, hf, n, :], start=False, stop=True)
                mm.then_inc(s_Op, 1)
                for hf in range(2):
                    rows = slice(DH * hf, DH * hf + DH)
                    for n in range(HH):
                        h = 2 * n + hf
                        mm = pe.matmul(pZT[1][rows, n * DH:(n + 1) * DH], kn[t.par][:, h * DH:(h + 1) * DH],
                                       U[:, hf, n, :], start=True, stop=True)
                mm.then_inc(s_Sp, 1)

            def oT_turn(t, nxt):
                wait_tile(pe, s_on, t)
                wait_before(pe, s_lg, t)
                if nxt:
                    wait_tile(pe, s_raw, nxt, 3, 3)
                for c in range(DC):
                    mm = pe.transpose(pF[1][:, c * P:(c + 1) * P], on[:, c * P:(c + 1) * P], ident[:, :])
                mm.then_inc(s_oTp, 1)

            def out_proj(t, nxt):
                wait_tile(pe, s_oT, t)
                if isinstance(t.v, int) and t.v == 0:
                    pe.wait_ge(s_wos, DC)
                wait_before(pe, s_x2nT, t)
                wait_before(pe, s_hacc, t, back=2)
                if nxt:
                    wait_tile(pe, s_th, nxt)
                for k in range(DC):
                    mm = pe.matmul(pF[0][:, :], oT[:, k, :], wo[:, k, :], start=(k == 0), stop=(k == DC - 1))
                mm.then_inc(s_yp, 1)

            def x2T(t, nxt):
                wait_tile(pe, s_x2n, t)
                if nxt:
                    wait_tile(pe, s_sq, nxt, 2, 2)
                for c in range(DC):
                    mm = pe.transpose(pF[0][:, c * P:(c + 1) * P], x2n[:, c * P:(c + 1) * P], ident[:, :])
                mm.then_inc(s_x2Tp, 1)

            def gate(t, nxt):
                wait_tile(pe, s_x2nT, t)
                if nxt:
                    wait_tile(pe, s_vb, nxt)
                for k in range(DC):
                    mm = pe.matmul(in_turn(pF[1][:, 0:P], E), x2g[:, k, :], repeated(gw[:, k, :], P // E),
                                   start=(k == 0), stop=(k == DC - 1))
                mm.then_inc(s_lgp, 1)

            def shared_up(t, part):
                if isinstance(t.v, int) and t.v == 0:
                    pe.wait_ge(s_wsh, 3 * 16)
                for c in range(len(IC)):
                    for k in range(DC):
                        lo = 2 * I * k + I * part + P * c
                        mm = pe.matmul(pZ[part][:, c * P:(c + 1) * P], wsh[:, lo:lo + P], x2g[:, k, :],
                                       start=(k == 0), stop=(k == DC - 1))
                mm.then_inc((s_hg, s_hu)[part], 1)

            def shared_gate(t, cur, prev):
                wait_tile(pe, s_x2nT, t)
                if cur:
                    wait_tile(pe, s_AT, cur, 2 * 3, 3)
                elif prev:
                    wait_tile(pe, s_O, prev, 4)
                shared_up(t, 0)

            def shared_ups(t, cur):
                if cur:
                    wait_tile(pe, s_AT, cur, 2 * 3)
                wait_before(pe, s_ha, t)
                shared_up(t, 1)

            def shared_down(t, newer):
                wait_tile(pe, s_ha, t)
                if newer:
                    wait_tile(pe, s_x2nT, newer)
                for c in range(len(IC)):
                    mm = pe.matmul(pF[0][:, :], sa[0:IC[c], c, :], wsh[0:IC[c], UPW + D * c:UPW + D * (c + 1)],
                                   start=(c == 0), stop=(c == len(IC) - 1))
                mm.then_inc(s_hd, 1)

            pe.wait_ge(s_const, 5)
            pe.wait_ge(s_clear, 2 * 4)

            def step(t, nxt, prev, old):
                if t:
                    gram(t, 0)
                    gram(t, 1)
                    stack_a(t, 0)
                    stack_a(t, 1)
                for k in range(1, LEVELS + 1):
                    if t:
                        level_y(t, k, 0)
                        level_y(t, k, 1)
                        level_z(t, k, 0)
                    if k == 1 and nxt:
                        xT(nxt)
                    if k == 2 and nxt:
                        project(nxt, 1)
                    if k == 3 and nxt:
                        betas(nxt)
                    if k == 3 and old:
                        shared_gate(old, t, prev)
                    if k == 4:
                        if prev:
                            out_proj(prev, nxt)
                    if k == 5 and nxt:
                        to_tokens_k(nxt, prev)
                    if k == 5 and old:
                        shared_ups(old, t)
                    if k == 6 and prev:
                        x2T(prev, nxt)
                    if t:
                        level_z(t, k, 1)
                    if k == 1 and nxt:
                        project(nxt, 0)
                    if k == 2 and nxt:
                        project(nxt, 2)
                    if k == 3 and prev:
                        oT_turn(prev, nxt)
                    if k == 4 and nxt:
                        to_tokens_q(nxt, prev)
                    if k == 5 and nxt:
                        to_tokens(nxt, 2)
                    if k == 6 and prev:
                        gate(prev, nxt)
                if t:
                    state_out(t)
                    solve(t)
                if old:
                    shared_down(old, prev)
                if t:
                    outputs(t, old)
                if nxt:
                    for i in range(3):
                        if i == 0 and prev:
                            wait_tile(pe, s_x2nT, prev)
                        if i == 0 and old:
                            wait_tile(pe, s_hacc, old)
                        if i == 1 and prev:
                            wait_tile(pe, s_lg, prev)
                        to_channels(nxt, i)

            def to_tokens_q(nxt, prev):
                if prev:
                    wait_tile(pe, s_oT, prev)
                to_tokens(nxt, 0)

            def to_tokens_k(nxt, prev):
                if prev:
                    wait_tile(pe, s_x2, prev, 2, 1)
                to_tokens(nxt, 1)

            run_tiles(pe, step)

        @block.vector
        def _(dve):
            fr, de, ba = Chain(dve, c_dF, 2 + 6 * 6 + 2), Chain(dve, c_dD, 2 * 2 + 2 * 4), Chain(dve, c_dB, 3)

            dve.memset(S[:, :], 0.0).then_inc(s_S0, 1)
            dve.memset(raw[:, :, P:P + HALO], 0.0).then_inc(s_S0, 1)
            dve.wait_ge(s_iota, 2)
            dve.tensor_tensor(xor_j[:, :], xor_i[:, :], xor_j[:, :], ALU.bitwise_xor).then_inc(s_masks, 1)
            dve.wait_ge(s_masks, 1)
            dve.tensor_copy(dist[:, :], xor_j[:, :]).then_inc(s_masks, 1)
            dve.wait_ge(s_const, 7)
            n = 0
            for b in range(BLOCKS):
                rows = slice(B * b, B * b + B)
                dve.tensor_copy(dist_st[rows, :], dist_lo[rows, rows]).then_inc(c_init, 1)
                dve.tensor_copy(ident_st[rows, :], ident[rows, rows]).then_inc(c_init, 1)
                n += 2
            for src, dst, width in ((dist_st, m_lo, B), (dist_up, m_up, P)):
                for k in range(LEVELS - 1):
                    dve.wait_ge(c_init, n)
                    dve.tensor_scalar(ge_a[:, 0:width], src[:, :], float(2 ** k), None, ALU.is_ge).then_inc(c_init, 1)
                    dve.tensor_scalar(ge_b[:, 0:width], src[:, :], float(2 ** (k + 1)), None, ALU.is_ge)\
                       .then_inc(c_init, 1)
                    n += 2
                    dve.wait_ge(c_init, n)
                    dve.tensor_tensor(dst[:, k, :], ge_a[:, 0:width], ge_b[:, 0:width], ALU.subtract)\
                       .then_inc(c_init, 1)
                    n += 1
            dve.wait_ge(c_init, n)
            dve.memset(zeros, 0.0).then_inc(s_zero, 1)
            for buf in (AB, A5, Y5, T64):
                for hf in range(2):
                    dve.memset(buf[hf][:, :, :], 0.0).then_inc(s_clear, 1)
            dve.wait_ge(s_wload, 4 * 16)

            def ln1_stats(t):
                fr.begin(t)
                if isinstance(t.v, int) and t.v < 2:
                    dve.wait_ge(s_xload, 16 if t.v == 0 else 4 * 16)
                fr.wait(0)
                wait_before(dve, s_xn, t)
                settle(dve)
                a = fr.done(dve.bn_stats(st1[:, :], xall[:, t.v, :]))
                fr.wait(a)
                settle(dve)
                b = fr.done(dve.bn_aggr(mv1[:, :], st1[:, :]))
                fr.wait(b)
                wait_before(dve, s_r1, t)
                dve.tensor_scalar(ve1[:, :], mv1[:, 1:2], LN_EPS, None, ALU.add).then_inc(s_stats, 1)

            def make_xn(t):
                wait_tile(dve, s_r1, t)
                wait_before(dve, s_xTp, t)
                dve.tensor_scalar(xn[:, :], xall[:, t.v, :], mv1[:, 0:1], r1[:, 0:1], ALU.subtract, ALU.mult)\
                   .then_inc(s_xn, 1)

            def conv(t, i, half):
                if half == 0:
                    wait_tile(dve, s_raw, t, 3, i + 1)
                    wait_before(dve, s_tokp, t, 3)
                cs = [DC * i + 2 * half, DC * i + 2 * half + 1]
                last = {}
                for c in cs:
                    last[c] = fr.done(dve.tensor_scalar(acc[:, c, :], raw[:, c, HALO:HALO + P],
                                                        cw[:, c, TAPS - 1:TAPS], None, ALU.mult))
                for j in range(TAPS - 1):
                    for c in cs:
                        fr.wait(last[c])
                        ins = dve.scalar_tensor_tensor(out=acc[:, c, :], in0=raw[:, c, j:j + P],
                                                       scalar=cw[:, c, j:j + 1], in1=acc[:, c, :],
                                                       op0=ALU.mult, op1=ALU.add)
                        if j < TAPS - 2:
                            last[c] = fr.done(ins)
                        else:
                            ins.then_inc(s_conv, 1)

            def betas(t):
                wait_tile(dve, s_th, t)
                wait_before(dve, s_knorm, t, 3)
                wait_before(dve, s_vb, t)
                dve.tensor_scalar(nbeta[:, :], th[:, :], -0.5, -0.5, ALU.mult, ALU.add)\
                   .then_inc(s_nbeta, 1)
                dve.tensor_scalar(beta[:, :], th[:, :], 0.5, 0.5, ALU.mult, ALU.add).then_inc(s_beta, 1)

            def sums(t, i):
                wait_tile(dve, s_sq, t, 2, i + 1)
                wait_before(dve, s_rqk, t)
                a = fr.done(dve.tensor_reduce(ss[:, H * i:H * i + H], heads(sq[:, i, :]), AX.X, ALU.add))
                fr.wait(a)
                dve.tensor_scalar(ss[:, H * i:H * i + H], ss[:, H * i:H * i + H], L2_EPS, None, ALU.add)\
                   .then_inc(s_ss, 1)

            def make_vb(t):
                wait_tile(dve, s_tokp, t, 3, 3)
                wait_tile(dve, s_beta, t)
                wait_before(dve, s_R, t, 2, back=2)
                dve.tensor_tensor(heads(vb[t.par][:, :]), heads(pF[1][:, :]), over_heads(beta[:, :]), ALU.mult)\
                   .then_inc(s_vb, 1)

            def start_t(t, hf):
                if hf == 0:
                    de.begin(t)
                wait_before(dve, s_Up, t)
                wait_before(dve, s_Op, t)
                wait_before(dve, s_T64, t, 2 * 2)
                if hf == 0:
                    wait_before(dve, s_T, t, T_UPDATES)
                a = de.done(dve.tensor_copy(TiT[hf][:, :, :], over_mats(ident[:, :])))
                b = de.done(dve.tensor_copy(Tst[hf][:, :, :], ident_st[:, :].unsqueeze(1).to_broadcast([P, HH, B])))
                wait_tile(dve, s_D1, t, 2, hf + 1)
                dve.tensor_tensor(PT[hf][:, :, :], mats(pZT[hf][:, :]), over_mats(causal[:, :]), ALU.mult)\
                   .then_inc(s_PT, 1)
                de.wait(b)
                wait_tile(dve, s_AB, t, 2 * BLOCKS, BLOCKS * (hf + 1))
                settle(dve)
                dve.copy_predicated(TiT[hf][:, :, :], over_mats(m_up[:, 0, :]), AB[hf][:, :, :]).then_inc(s_T0, 1)
                wait_tile(dve, s_st, t, 2, hf + 1)
                settle(dve)
                dve.copy_predicated(Tst[hf][:, :, :], over_stack(m_lo[:, 0, :]), stack(pY[hf][:, :])).then_inc(s_T0, 1)

            def update_t(t, k, hf):
                wait_tile(dve, s_Z, t, 2 * LEVELS, 2 * k - 1 + hf)
                if k == 1:
                    wait_tile(dve, s_T0, t, T_STARTS, 2 * hf + 2)
                else:
                    wait_tile(dve, s_T, t, T_UPDATES, through(T_SIGNALS, k - 1, hf))
                if k < 5:
                    settle(dve)
                    dve.copy_predicated(Tst[hf][:, :, :], over_stack(m_lo[:, k, :]), stack(pZT[hf][:, :]))\
                       .then_inc(s_T, 1)
                    a = de.done(dve.transpose(ZTs[hf][:, :, :], stack(pZT[hf][:, :])))
                    de.wait(a)
                    settle(dve)
                    dve.copy_predicated(blocks(TiT[hf][:, :, :]),
                                        blocks(m_up[:, k:k + 1, :]).to_broadcast([P, HH, BLOCKS, B]),
                                        over_blocks(ZTs[hf][:, :, :])).then_inc(s_T, 1)
                elif k == 5:
                    wait_tile(dve, s_T64, t, 2 * 2, 2 * (hf + 1))
                    dve.tensor_copy(T64[hf][B:2 * B, :, 0:B], stack(pZT[hf][B:2 * B, :])).then_inc(s_T, 1)
                    for g in range(2):
                        rows = slice(DH * g, DH * g + B)
                        dve.tensor_copy(TiT[hf][rows, :, DH * g + B:DH * g + 2 * B],
                                        mats(pZT[hf][rows, :])[:, :, (2 + g) * B:(3 + g) * B])\
                           .then_inc(s_T, 1)
                else:
                    dve.tensor_copy(TiT[hf][0:DH, :, DH:P], mats(pZT[hf][0:DH, :])[:, :, DH:P]).then_inc(s_T, 1)

            def make_r(t):
                wait_tile(dve, s_vb, t)
                wait_before(dve, s_Up, t)
                for hf in range(2):
                    wait_tile(dve, s_Rp, t, 2, hf + 1)
                    dve.tensor_tensor(R[:, hf], mats(pY[hf][:, :])[:, :, 0:DH], by_half(vb[t.par], hf), ALU.add)\
                       .then_inc(s_R, 1)

            def update_s(t):
                wait_tile(dve, s_Sp, t)
                wait_before(dve, s_S, t)
                if isinstance(t.v, int) and t.v == 0:
                    dve.wait_ge(s_S0, 1)
                dve.tensor_tensor(S[:, :], S[:, :], pZT[1][:, 0:HH * DH], ALU.add).then_inc(s_S, 1)

            def o_sums(t):
                wait_tile(dve, s_O, t, 4)
                wait_before(dve, s_ro, t)
                ba.begin(t)
                a = ba.done(dve.tensor_reduce(so[:, :], heads(osq[:, :]), AX.X, ALU.add))
                ba.wait(a)
                dve.tensor_scalar(so[:, :], so[:, :], 1.0 / DH, RMS_EPS, ALU.mult, ALU.add).then_inc(s_so, 1)

            def make_on(t):
                wait_tile(dve, s_ro, t)
                wait_before(dve, s_oTp, t)
                dve.tensor_tensor(heads(on[:, :]), heads(osb[:, :]), over_heads(ro[:, :]), ALU.mult).then_inc(s_on, 1)

            def make_x2(t):
                wait_tile(dve, s_yp, t)
                if not (isinstance(t.v, int) and t.v < 2):
                    dve.wait_ge(s_st2[t.par], (t.v - t.par) * 8)
                dve.tensor_tensor(x2r[t.par][:, :], xall[:, t.v, :], pF[0][:, :], ALU.add).then_inc(s_x2, 1)
                wait_tile(dve, s_x2, t, 2, 1)
                settle(dve)
                a = ba.done(dve.bn_stats(st2[:, :], x2r[t.par][:, :]))
                ba.wait(a)
                wait_before(dve, s_x2n, t)
                settle(dve)
                b = ba.done(dve.bn_aggr(mv2[:, :], st2[:, :]))
                ba.wait(b)
                wait_before(dve, s_r2, t)
                dve.tensor_scalar(ve2[:, :], mv2[:, 1:2], LN_EPS, None, ALU.add).then_inc(s_x2, 1)

            def make_x2n(t):
                wait_tile(dve, s_r2, t)
                wait_before(dve, s_x2Tp, t)
                wait_before(dve, s_xkeep, t)
                dve.tensor_scalar(x2n[:, :], x2r[t.par][:, :], mv2[:, 0:1], r2[:, 0:1], ALU.subtract, ALU.mult)\
                   .then_inc(s_x2n, 1)

            def shared_gated(t):
                wait_tile(dve, s_hs, t)
                wait_tile(dve, s_hu, t)
                wait_before(dve, s_hd, t)
                dve.tensor_tensor(sa[:, :, :], ssg[:, :, :], mats(pZ[1][:, 0:len(IC) * P]), ALU.mult).then_inc(s_ha, 1)

            def shared_add(t):
                wait_tile(dve, s_hd, t)
                dve.tensor_tensor(x2r[t.par][:, :], x2r[t.par][:, :], pF[0][:, :], ALU.add).then_inc(s_hacc, 1)

            def logits(t):
                wait_tile(dve, s_lgp, t)
                dve.tensor_copy(lg[:, t.v, :], pF[1][:, 0:E]).then_inc(s_lg, 1)

            def step(t, nxt, prev, old):
                if nxt:
                    ln1_stats(nxt)
                if prev:
                    o_sums(prev)
                if t and isinstance(t.v, int) and t.v == 0:
                    dve.wait_ge(s_wo, 4 * 16)
                    for c in range(DC):
                        dve.tensor_scalar(wo[:, c, :], wo[:, c, :], nw[:, 0:1], None, ALU.mult).then_inc(s_wos, 1)
                if t:
                    start_t(t, 0)
                    start_t(t, 1)
                if nxt:
                    make_xn(nxt)
                if prev:
                    make_on(prev)
                for k in range(1, LEVELS + 1):
                    for hf in range(2):
                        if t:
                            update_t(t, k, hf)
                        if nxt and 2 <= k <= 4:
                            conv(nxt, k - 2, hf)
                        if k == 3 and hf == 1 and nxt:
                            betas(nxt)
                        if k == 4 and hf == 1 and prev:
                            make_x2(prev)
                        if k == 5 and hf == 0:
                            if nxt:
                                sums(nxt, 0)
                        if k == 5 and hf == 1:
                            if nxt:
                                sums(nxt, 1)
                                make_vb(nxt)
                            if prev:
                                make_x2n(prev)
                        if k == 6 and hf == 0 and old:
                            shared_gated(old)
                        if k == 6 and hf == 1 and prev:
                            logits(prev)
                if t:
                    make_r(t)
                if old:
                    shared_add(old)
                if t:
                    update_s(t)

            run_tiles(dve, step)


G, TOPG, K = 4, 2, 4
NE = E + 2
NQ = K * T // P + E - 1
assert NQ % 2 == 1
NS = 3

def routing(nc, es, counts, scratch, lg, wsel, pos, qslot, qexp, tiles_to, s_pos, s_routed):

    def sb(name, shape, dt=F32):
        return es.enter_context(nc.sbuf_tensor(name, shape, dt))

    used = [0]

    def part(*shape):
        size = 1
        for n in shape:
            size *= n
        ap = scratch[:, used[0]:used[0] + size]
        used[0] += size
        return ap.rearrange("p (a b) -> p a b", b=shape[1]) if len(shape) == 2 else ap

    mx, sm = part(NT), part(NT)
    z, sc = part(NT, E), part(NT, E)
    gs, grank, gsel = part(NT, G), part(NT, G), part(NT, G)
    rank, cmp_, sel = part(NT, E), part(NT, E), part(NT, E)
    before, ones = part(P), part(P)
    cnt, seg, inc = part(E, NT), part(E, NT), part(E, NT)
    nti = sb("nti", [P, E], I32)
    nt, one_e, tinc, posf = part(E), part(E), part(E), part(NT, E)
    pj = part(NT, K)
    qi, qc = sb("qi", [1, NQ]), sb("qc", [1, NQ, E])
    qf, q3 = sb("qf", [1, NQ]), sb("q3", [1, NQ])
    pre, tot = counts[:, 0:NT * E], counts[:, NT * E:2 * NT * E]
    s_z, s_e, s_d, s_k, s_sel, s_cnt = (es.enter_context(nc.semaphore(n)) for n in (
        "z_ready", "exp_done", "route_chain", "route_consts", "sel_ready", "counts_psum"))

    def over(ap, n):
        return ap.unsqueeze(2).to_broadcast([P, NT, n])

    def route_act(act):
        act.wait_ge(s_z, 1)
        act.activation(z[:, :, :], z[:, :, :], ACT.Exp).then_inc(s_e, 1)

    def route_pool(pool):
        pool.memset(before[:, :], 1.0).then_inc(s_k, 1)
        pool.memset(ones[:, :], 1.0).then_inc(s_k, 1)
        pool.iota(qi[:, :], pattern=[[1, NQ]], base=0, channel_multiplier=0,
                  allow_small_or_imprecise_dtypes=True).then_inc(s_k, 1)
        pool.wait_ge(s_k, 3)
        pool.affine_select(out=before[:, :], in_=before[:, :], compare_op=ALU.is_gt, fill=0.0,
                           base=0, pattern=[[1, P]], channel_multiplier=-1).then_inc(s_k, 1)

    def route_pe(pe):
        pe.wait_ge(s_k, 4)
        pe.wait_ge(s_sel, 1)
        flat = sel[:, :, :].rearrange("p t e -> p (t e)")
        pe.matmul(pre[:, :], before[:, :], flat, start=True, stop=True).then_inc(s_cnt, 1)
        pe.matmul(tot[:, :], ones[:, :], flat, start=True, stop=True).then_inc(s_cnt, 1)

    def route_dve(dve, between):
        n, links = [0], [0]

        def link(ins):
            ins.then_inc(s_d, 1)
            n[0] += 1
            dve.wait_ge(s_d, n[0])
            links[0] += 1
            between(links[0])

        def ranks(dst, v, count):
            link(dve.memset(dst, 0.0))
            for j in range(count):
                one = v[:, :, j:j + 1]
                tmp = cmp_[:, :, 0:count]
                ins = dve.tensor_tensor(tmp[:, :, 0:j + 1], one.to_broadcast([P, NT, j + 1]),
                                        v[:, :, 0:j + 1], ALU.is_gt)
                if j + 1 < count:
                    ins.then_inc(s_d, 1)
                    n[0] += 1
                    ins = dve.tensor_tensor(tmp[:, :, j + 1:], one.to_broadcast([P, NT, count - 1 - j]),
                                            v[:, :, j + 1:], ALU.is_ge)
                link(ins)
                link(dve.tensor_tensor(dst, dst, tmp, ALU.add))

        link(dve.tensor_reduce(mx[:, :], lg[:, :, :], AX.X, ALU.max))
        dve.tensor_tensor(z[:, :, :], lg[:, :, :], over(mx[:, :], E), ALU.subtract).then_inc(s_z, 1)
        link(dve.memset(seg[:, :, :], 1.0))
        link(dve.memset(seg[:, :, 0:1], 0.0))
        link(dve.memset(one_e[:, :], 1.0))
        dve.wait_ge(s_e, 1)
        link(dve.tensor_reduce(sm[:, :], z[:, :, :], AX.X, ALU.add))
        link(dve.reciprocal(sm[:, :], sm[:, :]))
        link(dve.tensor_tensor(sc[:, :, :], z[:, :, :], over(sm[:, :], E), ALU.mult))
        link(dve.tensor_reduce(gs[:, :, :], sc[:, :, :].rearrange("p t (g e) -> p t g e", g=G), AX.X, ALU.max))
        ranks(grank[:, :, :], gs, G)
        link(dve.tensor_scalar(gsel[:, :, :], grank[:, :, :], float(TOPG), None, ALU.is_lt))
        link(dve.tensor_tensor(sc[:, :, :].rearrange("p t (g e) -> p t g e", g=G),
                               sc[:, :, :].rearrange("p t (g e) -> p t g e", g=G),
                               gsel[:, :, :].unsqueeze(3).to_broadcast([P, NT, G, E // G]), ALU.mult))
        ranks(rank[:, :, :], sc, E)
        dve.tensor_scalar(sel[:, :, :], rank[:, :, :], float(K), None, ALU.is_lt).then_inc(s_sel, 1)
        dve.wait_ge(s_sel, 1)
        link(dve.tensor_tensor(sc[:, :, :], sc[:, :, :], sel[:, :, :], ALU.mult))
        link(dve.tensor_reduce(sm[:, :], sc[:, :, :], AX.X, ALU.add))
        link(dve.tensor_scalar(sm[:, :], sm[:, :], 1e-20, None, ALU.add))
        link(dve.reciprocal(sm[:, :], sm[:, :]))
        link(dve.tensor_tensor(sc[:, :, :], sc[:, :, :], over(sm[:, :], E), ALU.mult))
        dve.wait_ge(s_cnt, 2)
        link(dve.tensor_copy(cnt[:, :, :], tot[:, :].rearrange("p (t e) -> p e t", e=E)))
        link(dve.tensor_tensor_scan(inc[:, :, :].rearrange("p e t -> p (e t)"),
                                    seg[:, :, :].rearrange("p e t -> p (e t)"),
                                    cnt[:, :, :].rearrange("p e t -> p (e t)"), 0.0, ALU.mult, ALU.add))
        link(dve.tensor_tensor(cnt[:, :, :], inc[:, :, :], cnt[:, :, :], ALU.subtract))
        link(dve.tensor_scalar(nti[:, :], inc[:, :, NT - 1], float(P - 1), None, ALU.add))
        link(dve.tensor_scalar(nti[:, :], nti[:, :], 7, None, ALU.logical_shift_right))
        link(dve.tensor_scalar(nt[:, :], nti[:, :], 1.0, None, ALU.max))
        link(dve.tensor_tensor_scan(tinc[:, :], one_e[:, :], nt[:, :], 0.0, ALU.mult, ALU.add))
        link(dve.tensor_copy(tiles_to[:, :], tinc[0:1, :]))
        link(dve.tensor_tensor(nt[:, :], tinc[:, :], nt[:, :], ALU.subtract))
        link(dve.scalar_tensor_tensor(out=cnt[:, :, :], in0=nt[:, :].unsqueeze(2).to_broadcast([P, E, NT]),
                                      scalar=float(P), in1=cnt[:, :, :], op0=ALU.mult, op1=ALU.add))
        link(dve.tensor_tensor(posf[:, :, :], pre[:, :].rearrange("p (t e) -> p t e", e=E),
                               cnt[:, :, :].rearrange("p e t -> p t e"), ALU.add))
        for j in range(K):
            link(dve.tensor_scalar(sel[:, :, :], rank[:, :, :], float(j), None, ALU.is_equal))
            link(dve.tensor_tensor(cmp_[:, :, :], sel[:, :, :], posf[:, :, :], ALU.mult))
            link(dve.tensor_reduce(pj[:, :, j], cmp_[:, :, :], AX.X, ALU.add))
            link(dve.tensor_tensor(cmp_[:, :, :], sel[:, :, :], sc[:, :, :], ALU.mult))
            link(dve.tensor_reduce(wsel[:, :, j], cmp_[:, :, :], AX.X, ALU.add))
        dve.tensor_copy(pos[:, :, :], pj[:, :, :]).then_inc(s_pos, 1)
        dve.wait_ge(s_k, 4)
        link(dve.tensor_tensor(qc[:, :, :], qi[:, :].unsqueeze(2).to_broadcast([1, NQ, E]),
                               tinc[0:1, :].unsqueeze(1).to_broadcast([1, NQ, E]), ALU.is_ge))
        link(dve.tensor_reduce(qf[:, :], qc[:, :, :], AX.X, ALU.add))
        link(dve.tensor_scalar(qf[:, :], qf[:, :], float(E - 1), None, ALU.min))
        link(dve.tensor_copy(qexp[:, :], qf[:, :]))
        link(dve.tensor_copy(q3[:, :], qf[:, :]))
        for m in range(NS, E, NS):
            link(dve.tensor_scalar(qc[:, :, 0], qf[:, :], float(m), -float(NS), ALU.is_ge, ALU.mult))
            link(dve.tensor_tensor(q3[:, :], q3[:, :], qc[:, :, 0], ALU.add))
        dve.tensor_copy(qslot[:, :], q3[:, :]).then_inc(s_routed, 1)

    return route_act, route_pool, route_pe, route_dve


def experts(nc, es, wup_d, wdn_d, xs_d, ys_d, acc_d, xall, lg, wsel, pos, qslot, qexp, tiles_to, wsh1, s_wsh1, out):
    N = 512
    NG = T // N
    TPG = N // P

    def sb(name, shape, dt=F32):
        return es.enter_context(nc.sbuf_tensor(name, shape, dt))

    def sem(name):
        return es.enter_context(nc.semaphore(name))

    w = sb("w", [P, NS, UPW + DNW])
    ident = sb("ident2", [P, P])
    acc = sb("acc_all", [P, NT, D])
    both = sb("gath", [P, 2 * K * D])
    gath = [both[:, K * D * i:K * D * (i + 1)].rearrange("p (k d) -> p k d", d=D) for i in range(2)]\
        + [xall[:, K * i:K * (i + 1), :] for i in range(2)]
    NB = len(gath)
    xg = [sb(f"xg{i}", [P, DC, N]) for i in range(2)]
    ssg = [sb(f"ssg{i}", [P, N]) for i in range(2)]
    sa = [sb(f"sa{i}", [P, len(IC), N]) for i in range(2)]
    xs = [sb(f"xs{i}", [P, D]) for i in range(2)]
    xsT = [sb(f"xsT{i}", [P, DC, P]) for i in range(2)]
    g, a = sb("g", [P, I]), sb("a", [P, I])
    aT = sb("aT", [P, len(IC), P])
    y = [sb(f"y{i}", [P, D]) for i in range(2)]

    def bank(n):
        return es.enter_context(nc.psum_tensor(n, [P, N], F32))

    pG, pU = [bank(f"pG{i}") for i in range(2)], [bank(f"pU{i}") for i in range(2)]
    pD = [bank(f"pD{i}") for i in range(TPG)]
    pX, pA, pYq = pD[0], pD[1], pD[2]

    s_w, s_accl, s_id = sem("weights_loaded"), sem("acc_loaded"), sem("ident_ready")
    s_xgp, s_xg = sem("group_turned_psum"), sem("group_turned")
    s_scat = sem("rows_scattered")
    s_xl, s_ys = [sem(f"slots_loaded{i}") for i in range(2)], [sem(f"slots_stored{i}") for i in range(2)]
    s_xTp, s_xT, s_gp, s_g, s_up, s_a, s_aTp, s_aT, s_yp, s_y = (sem(n) for n in (
        "slotsT_psum", "slotsT_ready", "gate_psum", "gate_silu", "up_psum", "gated_ready", "gatedT_psum",
        "gatedT_ready", "y_psum2", "y_ready"))
    s_sup, s_ssg, s_sa, s_sdn, s_sacc = (sem(n) for n in (
        "shared_up_psum", "shared_silu", "shared_gated", "shared_down_psum", "shared_added"))
    s_gath = [sem(f"rows_gathered{i}") for i in range(NB)]
    s_comb, s_cch, s_out = sem("combined"), sem("combine_chain"), sem("out_stored")
    COMBINE_AT = {"up": 2, "down": 1}
    FRONT_AT = (32, 48, 62, 76)
    front, tail = range(0, NG - 1), range(NG - 1, NG)
    FRONT = (("turn", 0), ("turn", 1), ("up", 0), ("counts", 0), ("up", 1), ("down", 0), ("turn", 2), ("up", 2),
             ("down", 1), ("down", 2))
    TAIL = (("turn", 3), ("up", 3), ("down", 3))
    assert NG == 4
    DNF = TPG * len(front)

    def wup(k):
        return wsh1[:, 2 * I * k:2 * I * (k + 1)]

    def wdn(c):
        return wsh1[:, UPW + D * c:UPW + D * (c + 1)]

    def run_slots(eng, body):
        body(0, 0)
        body(1, 1)
        with eng.Fori(1, (NQ - 3) // 2) as pair:
            body(2 * pair, 0)
            body(2 * pair + 1, 1)
        body(NQ - 3, 0)
        body(NQ - 2, 1)
        body(NQ - 1, 0)
        body(NQ, 1)

    def first(q):
        return isinstance(q, int) and q == 0

    def last(q):
        return isinstance(q, int) and q >= NQ - 1

    def end(q):
        return isinstance(q, int) and q == NQ

    def wait_pos(eng, s, value):
        if not (isinstance(value, int) and value <= 0):
            eng.wait_ge(s, value)

    s_pos, s_routed = sem("pos_ready"), sem("routed")
    route_act, route_pool, route_pe, route_dve = routing(nc, es, pD[0], both, lg, wsel, pos, qslot, qexp, tiles_to,
                                                         s_pos, s_routed)

    with nc.Block() as block:
        @block.sync
        def _(sp):
            xv = xs_d.rearrange("(q p) d -> q p d", p=P)
            yv = ys_d.rearrange("(q p) d -> q p d", p=P)
            for i in range(NG):
                sp.dma_start(acc[:, TPG * i:TPG * i + TPG, :], acc_d.rearrange("(t p) d -> p t d", p=P)
                             [:, TPG * i:TPG * i + TPG, :]).then_inc(s_accl, 16)
                sp.wait_ge(s_accl, 16 * (i + 1))
            sp.wait_ge(s_scat, 16 * NT * K)
            for q in range(2):
                sp.dma_start(xs[q][:, :], xv[q]).then_inc(s_xl[q], 16)

            def body(q, par):
                if not (isinstance(q, int) and q >= NQ - 2):
                    sp.wait_ge(s_xTp, q + 1)
                    sp.dma_start(xs[par][:, :], xv[q + 2]).then_inc(s_xl[par], 16)
                if not first(q):
                    sp.wait_ge(s_y, q)
                    sp.dma_start(yv[q - 1], y[1 - par][:, :]).then_inc(s_ys[1 - par], 16)

            run_slots(sp, body)
            ov = out.rearrange("b (t p) d -> p (b t) d", p=P)
            for i in range(0, NT, 2):
                sp.wait_ge(s_comb, i + 2)
                sp.dma_start(ov[:, i:i + 2, :], acc[:, i:i + 2, :]).then_inc(s_out, 16)
            sp.wait_ge(s_out, 16 * NT // 2)

        @block.gpsimd
        def _(pool):
            route_pool(pool)
            pool.memset(ident[:, :], 0.0).then_inc(s_id, 1)
            pool.wait_ge(s_id, 1)
            pool.affine_select(out=ident[:, :], in_=ident[:, :], compare_op=ALU.not_equal, fill=1.0,
                               base=0, pattern=[[-1, P]], channel_multiplier=1).then_inc(s_id, 1)
            load_expert(pool, w[:, 0], wup_d[0], wdn_d[0], s_w)
            pool.wait_ge(s_pos, 1)
            for i in range(NT):
                for j in range(K):
                    pool.indirect_dma_start(out=xs_d[:, :], out_offset=bass.IndirectOffsetOnAxis(
                        ap=pos[:, i, j:j + 1], axis=0), in_=xall[:, i, :], in_offset=None).then_inc(s_scat, 16)
            for s in range(1, E):
                pool.wait_ge(s_w, 48 * s)
                if s < NS:
                    load_expert(pool, w[:, s], wup_d[s], wdn_d[s], s_w)
                    continue
                if s == NS:
                    pool.wait_ge(s_routed, 1)
                done = pool.value_load(tiles_to[0:1, s - NS:s - NS + 1], min_val=1, max_val=NQ)
                pool.wait_ge(s_yp, done)
                pool.nop(nofuse=True)
                pool.wait_ge(s_id, 2)
                load_expert(pool, w[:, s % NS], wup_d[s], wdn_d[s], s_w)
            for par in range(2):
                pool.wait_ge(s_ys[par], 16 * ((NQ + 1 - par) // 2))
            for i in range(NT):
                if i >= NB:
                    pool.wait_ge(s_comb, i - NB + 1)
                for j in range(K):
                    pool.indirect_dma_start(out=gath[i % NB][:, j, :], out_offset=None, in_=ys_d[:, :],
                                            in_offset=bass.IndirectOffsetOnAxis(ap=pos[:, i, j:j + 1], axis=0))\
                        .then_inc(s_gath[i % NB], 16)

        @block.scalar
        def _(act):
            def turned(gr):
                for i in range(TPG):
                    act.wait_ge(s_xgp, TPG * gr + i + 1)
                    if gr >= 2:
                        act.wait_ge(s_sup, len(IC) * (gr - 1))
                    act.activation(xg[gr % 2][:, :, P * i:P * i + P],
                                   pD[i][:, :].rearrange("p (c n) -> p c n", c=DC), ACT.Copy).then_inc(s_xg, 1)

            def silu(gr):
                for c in range(len(IC)):
                    u, m = len(IC) * gr + c, IC[c]
                    wait_pos(act, s_sa, u - 1)
                    act.wait_ge(s_sup, u + 1)
                    act.activation(ssg[u % 2][0:m, :], pG[u % 2][0:m, :], ACT.Silu).then_inc(s_ssg, 1)

            def shared(stages):
                for stage, gr in stages:
                    if stage == "turn":
                        turned(gr)
                    elif stage == "up":
                        silu(gr)

            def turned_rows(q, par):
                act.wait_ge(s_xTp, q + 1)
                wait_pos(act, s_up, q - 1)
                act.activation(xsT[par][:, :, :], pX[:, :].rearrange("p (c n) -> p c n", c=DC), ACT.Copy)\
                   .then_inc(s_xT, 1)

            def body(q, par):
                if first(q):
                    turned_rows(0, 0)
                if not end(q):
                    act.wait_ge(s_gp, q + 1)
                    wait_pos(act, s_a, q)
                    act.activation(g[:, :], pG[0][:, 0:I], ACT.Silu).then_inc(s_g, 1)
                if not first(q):
                    act.wait_ge(s_aTp, q)
                    wait_pos(act, s_yp, q - 1)
                    act.activation(aT[:, 0:2, :], pA[:, 0:2 * P].rearrange("p (c n) -> p c n", c=2), ACT.Copy)\
                       .then_inc(s_aT, 1)
                    act.activation(aT[0:IC[2], 2, :], pA[0:IC[2], 2 * P:3 * P], ACT.Copy).then_inc(s_aT, 1)
                if not last(q):
                    turned_rows(q + 1, 1 - par)
                if not first(q):
                    act.wait_ge(s_yp, q)
                    if not (isinstance(q, int) and q < 3):
                        act.wait_ge(s_ys[1 - par], (q - 1 - (1 - par)) * 8)
                    act.activation(y[1 - par][:, :], pYq[:, :], ACT.Copy).then_inc(s_y, 1)

            route_act(act)
            shared(FRONT)
            run_slots(act, body)
            shared(TAIL)

        @block.vector
        def _(dve):
            comb = [0]

            def gated(gr, c):
                u, m = len(IC) * gr + c, IC[c]
                if c == 0:
                    wait_pos(dve, s_sdn, TPG * (gr - 1))
                dve.wait_ge(s_ssg, u + 1)
                dve.tensor_tensor(sa[gr % 2][0:m, c, :], ssg[u % 2][0:m, :], pU[u % 2][0:m, :], ALU.mult)\
                   .then_inc(s_sa, 1)

            def accumulate(gr, i):
                j = TPG * gr + i
                dve.wait_ge(s_sdn, j + 1)
                dve.wait_ge(s_accl, 16 * (gr + 1))
                dve.tensor_tensor(acc[:, j, :], acc[:, j, :], pD[i][:, :], ALU.add).then_inc(s_sacc, 1)

            def combine(i):
                dve.wait_ge(s_gath[i % NB], 16 * K * (i // NB + 1))
                dve.wait_ge(s_sacc, i + 1)
                for j in range(K):
                    ins = dve.scalar_tensor_tensor(out=acc[:, i, :], in0=gath[i % NB][:, j, :],
                                                   scalar=wsel[:, i, j:j + 1], in1=acc[:, i, :],
                                                   op0=ALU.mult, op1=ALU.add)
                    if j < K - 1:
                        comb[0] += 1
                        ins.then_inc(s_cch, 1)
                        dve.wait_ge(s_cch, comb[0])
                    else:
                        ins.then_inc(s_comb, 1)

            def front_between(links):
                if links in FRONT_AT:
                    gated(*divmod(FRONT_AT.index(links), len(IC)))

            def shared(stages):
                combined = 0
                for stage, gr in stages:
                    for n in range({"up": len(IC), "down": TPG}.get(stage, 0)):
                        if stage == "down":
                            accumulate(gr, n)
                        elif len(IC) * gr + n >= len(FRONT_AT):
                            gated(gr, n)
                        if stages is TAIL:
                            for _ in range(COMBINE_AT[stage]):
                                combine(combined)
                                combined += 1
                if stages is TAIL:
                    for i in range(combined, NT):
                        combine(i)

            def body(q, par):
                if not end(q):
                    dve.wait_ge(s_g, q + 1)
                    dve.wait_ge(s_up, q + 1)
                    wait_pos(dve, s_aTp, q)
                    dve.tensor_tensor(a[:, :], g[:, :], pU[0][:, 0:I], ALU.mult).then_inc(s_a, 1)

            route_dve(dve, front_between)
            shared(FRONT)
            run_slots(dve, body)
            shared(TAIL)

        @block.tensor
        def _(pe):
            def shared(stages):
                groups = front if stages is FRONT else tail

                def turn(gr):
                    for i in range(TPG):
                        wait_pos(pe, s_xg, TPG * (gr - 1) + i + 1)
                        wait_pos(pe, s_sacc, TPG * (gr - 2) + i + 1 if gr < tail[0] else DNF)
                        for c in range(DC):
                            mm = pe.transpose(pD[i][:, c * P:(c + 1) * P], xall[:, TPG * gr + i, c * P:(c + 1) * P],
                                              ident[:, :])
                        mm.then_inc(s_xgp, 1)

                def up(gr):
                    pe.wait_ge(s_xg, TPG * (gr + 1))
                    for c in range(3):
                        u, m = 3 * gr + c, IC[c]
                        wait_pos(pe, s_sa, u - 1)
                        for p, off in ((pG[u % 2], 0), (pU[u % 2], I)):
                            for k in range(DC):
                                mm = pe.matmul(p[0:m, :], wup(k)[:, off + P * c:off + P * c + m],
                                               xg[gr % 2][:, k, :], start=(k == 0), stop=(k == DC - 1))
                        mm.then_inc(s_sup, 1)

                def down(gr):
                    pe.wait_ge(s_sa, 3 * (gr + 1))
                    for i in range(TPG):
                        pe.wait_ge(s_xg, TPG * (gr if gr == groups[-1] else gr + 1) + i + 1)
                        wait_pos(pe, s_sacc, TPG * (gr - 1) + i + 1)
                        for c in range(3):
                            m = IC[c]
                            mm = pe.matmul(pD[i][:, :], sa[gr % 2][0:m, c, P * i:P * i + P],
                                           wdn(c)[0:m, :], start=(c == 0), stop=(c == 2))
                        mm.then_inc(s_sdn, 1)

                for stage, gr in stages:
                    if stage == "turn":
                        turn(gr)
                    elif stage == "up":
                        up(gr)
                    elif stage == "down":
                        if gr == 0:
                            pe.wait_ge(s_pos, 1)
                        down(gr)
                    else:
                        pe.wait_ge(s_xg, TPG * 2)
                        route_pe(pe)

            def turn_rows(q, par):
                pe.wait_ge(s_xl[par], (q - par) * 8 + 16)
                wait_pos(pe, s_xT, q)
                for c in range(DC):
                    mm = pe.transpose(pX[:, c * P:(c + 1) * P], xs[par][:, c * P:(c + 1) * P], ident[:, :])
                mm.then_inc(s_xTp, 1)

            def body(q, par):
                if first(q):
                    turn_rows(0, 0)
                if not end(q):
                    slot = pe.value_load(qslot[0:1, bass.ds(q, 1)], min_val=0, max_val=NS - 1)
                    expert = pe.value_load(qexp[0:1, bass.ds(q, 1)], min_val=0, max_val=E - 1)
                    pe.wait_ge(s_xT, q + 1)
                    pe.wait_ge(s_w, expert * 48 + 48)
                    wait_pos(pe, s_g, q)
                    for k in range(DC):
                        mm = pe.matmul(pG[0][:, 0:I], xsT[par][:, k, :], w[:, bass.ds(slot, 1), 2 * I * k:2 * I * k + I],
                                       start=(k == 0), stop=(k == DC - 1))
                    mm.then_inc(s_gp, 1)
                if not first(q):
                    before = pe.value_load(qslot[0:1, bass.ds(q - 1, 1)], min_val=0, max_val=NS - 1)
                    down = w[:, bass.ds(before, 1), :]
                    pe.wait_ge(s_a, q)
                    wait_pos(pe, s_aT, 2 * (q - 1))
                    for c in range(3):
                        mm = pe.transpose(pA[0:IC[c], c * P:(c + 1) * P], a[:, P * c:P * c + IC[c]], ident[:, :])
                    mm.then_inc(s_aTp, 1)
                if not last(q):
                    turn_rows(q + 1, 1 - par)
                if not end(q):
                    wait_pos(pe, s_a, q)
                    for k in range(DC):
                        mm = pe.matmul(pU[0][:, 0:I], xsT[par][:, k, :],
                                       w[:, bass.ds(slot, 1), 2 * I * k + I:2 * I * (k + 1)],
                                       start=(k == 0), stop=(k == DC - 1))
                    mm.then_inc(s_up, 1)
                if not first(q):
                    pe.wait_ge(s_aT, 2 * q)
                    wait_pos(pe, s_y, q - 1)
                    for c in range(3):
                        m = IC[c]
                        mm = pe.matmul(pYq[:, :], aT[0:m, c, :], down[0:m, :, UPW + D * c:UPW + D * (c + 1)],
                                       start=(c == 0), stop=(c == 2))
                    mm.then_inc(s_yp, 1)

            pe.wait_ge(s_wsh1, 48)
            pe.wait_ge(s_id, 2)
            shared(FRONT)
            pe.wait_ge(s_sacc, DNF)
            pe.wait_ge(s_routed, 1)
            run_slots(pe, body)
            pe.wait_ge(s_y, NQ)
            shared(TAIL)


def program(nc, x, wq, wk, wv, wb, cq, ck, cv, nw, wo, gw, wup, wdn, out):
    with ExitStack() as es:
        xall = es.enter_context(nc.sbuf_tensor("xall", [P, NT, D], F32))
        lg = es.enter_context(nc.sbuf_tensor("lg", [P, NT, E], F32))
        wsel = es.enter_context(nc.sbuf_tensor("wsel", [P, NT, K], F32))
        pos = es.enter_context(nc.sbuf_tensor("pos", [P, NT, K], I32))
        qslot = es.enter_context(nc.sbuf_tensor("qslot", [1, NQ], I32))
        qexp = es.enter_context(nc.sbuf_tensor("qexp", [1, NQ], I32))
        tiles_to = es.enter_context(nc.sbuf_tensor("tiles_to", [1, E], I32))
        xs_d = nc.dram_tensor("slot_rows", (NQ * P, D), F32, kind="Internal").ap()
        wsh1 = es.enter_context(nc.sbuf_tensor("wsh1", [P, UPW + DNW], F32))
        s_wsh1 = es.enter_context(nc.semaphore("shared_w1_loaded"))
        acc_d = nc.dram_tensor("partial_sums", (T, D), F32, kind="Internal").ap()
        ys_d = nc.dram_tensor("slot_results", (NQ * P, D), F32, kind="Internal").ap()
        with ExitStack() as inner:
            attention(nc, inner, x, wq, wk, wv, wb, cq, ck, cv, nw, wo, gw, wup, wdn, xall, lg, acc_d, xs_d, wsh1, s_wsh1)
        with ExitStack() as inner:
            experts(nc, inner, wup, wdn, xs_d, ys_d, acc_d, xall, lg, wsel, pos, qslot, qexp, tiles_to, wsh1, s_wsh1, out)


_INS = ['L0_attn_hidden_states', 'L0_attn_Wq', 'L0_attn_Wk', 'L0_attn_Wv', 'L0_attn_Wb', 'L0_attn_conv_q',
        'L0_attn_conv_k', 'L0_attn_conv_v', 'L0_attn_norm_w', 'L0_attn_Wo']


def kernel(**inputs):
    import numpy as np
    import concourse.bacc as bacc
    from concourse.bass_utils import run_bass_kernel_spmd

    nc = bacc.Bacc("TRN2", target_bir_lowering=False, num_devices=1)
    laid = {n: np.asarray(inputs[n]) for n in _INS}
    laid['gate_T'] = np.asarray(inputs['L0_ffn_gate_w']).T
    up, down = np.asarray(inputs['L0_ffn_expert_up_w']), np.asarray(inputs['L0_ffn_expert_down_w'])
    sup, sdown = np.asarray(inputs['L0_ffn_shared_up_w']), np.asarray(inputs['L0_ffn_shared_down_w'])
    halves = sup.reshape(2, 2, I, D).transpose(1, 0, 2, 3).reshape(2, 2 * I, D)
    laid['up_T'] = np.concatenate([up, halves]).transpose(0, 2, 1)
    laid['down_T'] = np.concatenate([down.transpose(0, 2, 1), sdown.T.reshape(2, I, D)])
    arrays, args = {}, []
    for n, a in laid.items():
        a = np.ascontiguousarray(a)
        arrays[f"in_{n}"] = a
        args.append(nc.dram_tensor(f"in_{n}", a.shape, mybir.dt.from_np(a.dtype), kind="ExternalInput").ap())
    args.append(nc.dram_tensor("out_0", (1, T, D), F32, kind="ExternalOutput").ap())
    program(nc, *args)
    r = run_bass_kernel_spmd(nc, [arrays], core_ids=[0])
    return r.results[0]["out_0"]
```
